# Optimizing a Trainium2 kernel written in Bass

```python
import numpy as np
import jax
import jax.numpy as jnp

def _softmax(x, axis=-1):
    return jax.nn.softmax(x, axis=axis)

def _gelu(x):
    return jax.nn.gelu(x, approximate=True)

def _silu(x):
    return jax.nn.silu(x)

def _sigmoid(x):
    return jax.nn.sigmoid(x)

def _layernorm(x, axis=-1, eps=1e-05):
    m = jnp.mean(x, axis=axis, keepdims=True)
    v = jnp.var(x, axis=axis, keepdims=True)
    return (x - m) / jnp.sqrt(v + eps)

def _scatter_add(tgt, idx, src, axis=0):
    return tgt.at[idx].add(src)

def _segment_sum(src, seg, n):
    return jax.ops.segment_sum(src, seg, n)
kernel_name = 'mk_seq_postln_d2_jaxref_r8_fa46b1'

def setup_inputs(seed: int=0):
    np.random.seed(seed)
    _w = jnp.asarray

    def _L0_attn_setup():
        import jax, jax.numpy as jnp
        import numpy as np
        D_MODEL = 256
        D_STATE = 64
        EXPAND = 2
        N_HEADS = 64
        NGROUPS = 1
        MIMO_RANK = 1
        D_INNER = EXPAND * D_MODEL
        HEAD_DIM = D_INNER // N_HEADS
        HEADS_PER_GROUP = N_HEADS // NGROUPS
        SSD_SCALE = (D_STATE * MIMO_RANK) ** (-0.5)
        EPS = 1e-06
        BATCH, SEQ = (2, 256)

        def _rms(v):
            return v * jax.lax.rsqrt(jnp.mean(v * v, axis=-1, keepdims=True) + EPS)

        def _rope(v, phi):
            v1, v2 = (v[..., 0::2], v[..., 1::2])
            c, s = (jnp.cos(phi), jnp.sin(phi))
            r1 = v1 * c - v2 * s
            r2 = v1 * s + v2 * c
            return jnp.stack([r1, r2], axis=-1).reshape(v.shape)
        key = jax.random.key(seed)
        ks = jax.random.split(key, 10)
        d_in_proj = 2 * D_INNER + 2 * NGROUPS * MIMO_RANK * D_STATE + N_HEADS
        return {'x': jax.random.normal(ks[0], (BATCH, SEQ, D_MODEL), jnp.float32), 'W_in': jax.random.normal(ks[1], (D_MODEL, d_in_proj), jnp.float32) * 0.02, 'W_out': jax.random.normal(ks[2], (D_INNER, D_MODEL), jnp.float32) * 0.02, 'dt_bias': jax.random.normal(ks[3], (N_HEADS,), jnp.float32) * 0.1, 'A_log': jnp.log(jax.random.uniform(ks[4], (N_HEADS,), jnp.float32, 1.0, 16.0)), 'D_param': jnp.ones((N_HEADS,), jnp.float32), 'B_bias': jax.random.normal(ks[5], (N_HEADS, D_STATE), jnp.float32) * 0.02, 'C_bias': jax.random.normal(ks[6], (N_HEADS, D_STATE), jnp.float32) * 0.02, 'rope_freqs': jax.random.uniform(ks[7], (N_HEADS, D_STATE // 2), jnp.float32, 0.0, 1.0), 'norm_w': jnp.ones((D_INNER,), jnp.float32)}
    _L0_attn_in = _L0_attn_setup()

    def _L0_ffn_setup():
        import jax, jax.numpy as jnp
        import numpy as np
        BS, SLEN, DIM, HID, E, TOPK = (4, 256, 256, 224, 8, 2)
        key = jax.random.key(seed)
        ks = jax.random.split(key, 9)
        s = 0.02
        return {'x': jax.random.normal(ks[0], (BS, SLEN, DIM), jnp.float32), 'gate_w': jax.random.normal(ks[1], (DIM, E), jnp.float32) * s, 'w1': jax.random.normal(ks[2], (E, DIM, HID), jnp.float32) * s, 'w2': jax.random.normal(ks[3], (E, HID, DIM), jnp.float32) * s, 'w3': jax.random.normal(ks[4], (E, DIM, HID), jnp.float32) * s, 'sw1': jax.random.normal(ks[5], (DIM, HID), jnp.float32) * s, 'sw2': jax.random.normal(ks[6], (HID, DIM), jnp.float32) * s, 'sw3': jax.random.normal(ks[7], (DIM, HID), jnp.float32) * s, 'expert_bias': jnp.zeros((E,), jnp.float32)}
    _L0_ffn_in = _L0_ffn_setup()

    def _L1_attn_setup():
        import jax, jax.numpy as jnp
        import numpy as np
        B, S, D = (4, 512, 256)
        THETA = 10000.0
        LN_EPS = 1e-05

        def _layernorm(x, w, b):
            mu = jnp.mean(x, axis=-1, keepdims=True)
            var = jnp.mean(jnp.square(x - mu), axis=-1, keepdims=True)
            return (x - mu) * jax.lax.rsqrt(var + LN_EPS) * w + b

        def _rope_half(x):
            rot_dim = x.shape[-1] // 2
            seq = x.shape[-2]
            inv_freq = 1.0 / THETA ** (jnp.arange(0, rot_dim, 2, dtype=jnp.float32) / rot_dim)
            freqs = jnp.arange(seq, dtype=jnp.float32)[:, None] * inv_freq[None, :]
            freqs = jnp.repeat(freqs, 2, axis=-1)
            cos, sin = (jnp.cos(freqs), jnp.sin(freqs))
            xl, xr = (x[..., :rot_dim], x[..., rot_dim:])
            x1, x2 = (xl[..., 0::2], xl[..., 1::2])
            rh = jnp.stack((-x2, x1), axis=-1).reshape(xl.shape)
            return jnp.concatenate([xl * cos + rh * sin, xr], axis=-1)

        def _cos_sim(x):
            return x / jnp.linalg.norm(x, axis=-1, keepdims=True)
        key = jax.random.key(seed)
        k0, k1, k2 = jax.random.split(key, 3)
        X = jax.random.normal(k0, (B, S, D), jnp.float32)
        ln_w = jnp.ones((D,), jnp.float32)
        ln_b = jnp.zeros((D,), jnp.float32)
        W_in = jax.random.normal(k1, (D, 3 * D), jnp.float32) * D ** (-0.5)
        b_in = jnp.zeros((3 * D,), jnp.float32)
        W_out = jax.random.normal(k2, (D, D), jnp.float32) * D ** (-0.5)
        b_out = jnp.zeros((D,), jnp.float32)
        return {'X': X, 'ln_w': ln_w, 'ln_b': ln_b, 'W_in': W_in, 'b_in': b_in, 'W_out': W_out, 'b_out': b_out}
    _L1_attn_in = _L1_attn_setup()

    def _L1_ffn_setup():
        import jax, jax.numpy as jnp
        import numpy as np
        ZERO_POINT = 128.0

        def _dequant(wq, scale):
            return (wq.astype(jnp.float32) - ZERO_POINT) * scale[:, None]
        key = jax.random.key(seed)
        ks = jax.random.split(key, 7)
        H, I = (256, 1024)
        B, S = (2, 256)
        hidden_state = jax.random.normal(ks[0], (B, S, H), dtype=jnp.float32)
        gate_w = jax.random.randint(ks[1], (I, H), 0, 32, dtype=jnp.int32)
        up_w = jax.random.randint(ks[2], (I, H), 0, 32, dtype=jnp.int32)
        down_w = jax.random.randint(ks[3], (H, I), 0, 32, dtype=jnp.int32)
        gate_scale = jax.random.uniform(ks[4], (I,), dtype=jnp.float32) * 0.02
        up_scale = jax.random.uniform(ks[5], (I,), dtype=jnp.float32) * 0.02
        down_scale = jax.random.uniform(ks[6], (H,), dtype=jnp.float32) * 0.02
        return {'hidden_state': hidden_state, 'gate_w': gate_w, 'gate_scale': gate_scale, 'up_w': up_w, 'up_scale': up_scale, 'down_w': down_w, 'down_scale': down_scale}
    _L1_ffn_in = _L1_ffn_setup()
    _d = {'L0_attn_x': _L0_attn_in['x'], 'L0_attn_W_in': _L0_attn_in['W_in'], 'L0_attn_W_out': _L0_attn_in['W_out'], 'L0_attn_dt_bias': _L0_attn_in['dt_bias'], 'L0_attn_A_log': _L0_attn_in['A_log'], 'L0_attn_D_param': _L0_attn_in['D_param'], 'L0_attn_B_bias': _L0_attn_in['B_bias'], 'L0_attn_C_bias': _L0_attn_in['C_bias'], 'L0_attn_rope_freqs': _L0_attn_in['rope_freqs'], 'L0_attn_norm_w': _L0_attn_in['norm_w'], 'L0_ffn_gate_w': _L0_ffn_in['gate_w'], 'L0_ffn_w1': _L0_ffn_in['w1'], 'L0_ffn_w2': _L0_ffn_in['w2'], 'L0_ffn_w3': _L0_ffn_in['w3'], 'L0_ffn_sw1': _L0_ffn_in['sw1'], 'L0_ffn_sw2': _L0_ffn_in['sw2'], 'L0_ffn_sw3': _L0_ffn_in['sw3'], 'L0_ffn_expert_bias': _L0_ffn_in['expert_bias'], 'L1_attn_ln_w': _L1_attn_in['ln_w'], 'L1_attn_ln_b': _L1_attn_in['ln_b'], 'L1_attn_W_in': _L1_attn_in['W_in'], 'L1_attn_b_in': _L1_attn_in['b_in'], 'L1_attn_W_out': _L1_attn_in['W_out'], 'L1_attn_b_out': _L1_attn_in['b_out'], 'L1_ffn_gate_w': _L1_ffn_in['gate_w'], 'L1_ffn_gate_scale': _L1_ffn_in['gate_scale'], 'L1_ffn_up_w': _L1_ffn_in['up_w'], 'L1_ffn_up_scale': _L1_ffn_in['up_scale'], 'L1_ffn_down_w': _L1_ffn_in['down_w'], 'L1_ffn_down_scale': _L1_ffn_in['down_scale']}
    _x0 = _d['L0_attn_x']
    _d['L0_attn_x'] = jax.random.normal(jax.random.fold_in(jax.random.key(seed), 1), (2, 2048, 256), dtype=_x0.dtype)
    del _x0
    return _d

def reference(L0_attn_x, L0_attn_W_in, L0_attn_W_out, L0_attn_dt_bias, L0_attn_A_log, L0_attn_D_param, L0_attn_B_bias, L0_attn_C_bias, L0_attn_rope_freqs, L0_attn_norm_w, L0_ffn_gate_w, L0_ffn_w1, L0_ffn_w2, L0_ffn_w3, L0_ffn_sw1, L0_ffn_sw2, L0_ffn_sw3, L0_ffn_expert_bias, L1_attn_ln_w, L1_attn_ln_b, L1_attn_W_in, L1_attn_b_in, L1_attn_W_out, L1_attn_b_out, L1_ffn_gate_w, L1_ffn_gate_scale, L1_ffn_up_w, L1_ffn_up_scale, L1_ffn_down_w, L1_ffn_down_scale):

    def _L0_attn_ref(x, W_in, W_out, dt_bias, A_log, D_param, B_bias, C_bias, rope_freqs, norm_w):
        import jax, jax.numpy as jnp
        import numpy as np
        D_MODEL = 256
        D_STATE = 64
        EXPAND = 2
        N_HEADS = 64
        NGROUPS = 1
        MIMO_RANK = 1
        D_INNER = EXPAND * D_MODEL
        HEAD_DIM = D_INNER // N_HEADS
        HEADS_PER_GROUP = N_HEADS // NGROUPS
        SSD_SCALE = (D_STATE * MIMO_RANK) ** (-0.5)
        EPS = 1e-06
        BATCH, SEQ = (2, 256)

        def _rms(v):
            return v * jax.lax.rsqrt(jnp.mean(v * v, axis=-1, keepdims=True) + EPS)

        def _rope(v, phi):
            v1, v2 = (v[..., 0::2], v[..., 1::2])
            c, s = (jnp.cos(phi), jnp.sin(phi))
            r1 = v1 * c - v2 * s
            r2 = v1 * s + v2 * c
            return jnp.stack([r1, r2], axis=-1).reshape(v.shape)
        Bsz, T, _ = x.shape
        zxbcdt = x @ W_in
        z = zxbcdt[..., :D_INNER]
        xs = zxbcdt[..., D_INNER:2 * D_INNER]
        o = 2 * D_INNER
        gn = NGROUPS * D_STATE
        Braw = zxbcdt[..., o:o + gn].reshape(Bsz, T, NGROUPS, D_STATE)
        Craw = zxbcdt[..., o + gn:o + 2 * gn].reshape(Bsz, T, NGROUPS, D_STATE)
        dt_raw = zxbcdt[..., o + 2 * gn:]
        dt = jax.nn.softplus(dt_raw + dt_bias)
        a = jnp.exp(-jnp.exp(A_log) * dt)
        Bh = jnp.repeat(_rms(Braw), HEADS_PER_GROUP, axis=2) + B_bias
        Ch = jnp.repeat(_rms(Craw), HEADS_PER_GROUP, axis=2) + C_bias
        phi = jnp.cumsum(dt, axis=1)[..., None] * rope_freqs
        Bh = _rope(Bh, phi)
        Ch = _rope(Ch, phi)
        xh = xs.reshape(Bsz, T, N_HEADS, HEAD_DIM)
        u = xh * dt[..., None]

        def step(h, inp):
            a_t, u_t, b_t, c_t = inp
            h = a_t[..., None, None] * h + u_t[..., None] * b_t[:, :, None, :]
            y = jnp.einsum('bhpn,bhn->bhp', h, c_t)
            return (h, y)
        h0 = jnp.zeros((Bsz, N_HEADS, HEAD_DIM, D_STATE), x.dtype)
        xs_time = (a.transpose(1, 0, 2), u.transpose(1, 0, 2, 3), Bh.transpose(1, 0, 2, 3), Ch.transpose(1, 0, 2, 3))
        _, ys = jax.lax.scan(step, h0, xs_time)
        ys = ys.transpose(1, 0, 2, 3)
        y = SSD_SCALE * ys + D_param[None, None, :, None] * xh
        y = y.reshape(Bsz, T, D_INNER)
        g = y * jax.nn.silu(z)
        y = g * jax.lax.rsqrt(jnp.mean(g * g, axis=-1, keepdims=True) + EPS) * norm_w
        return y @ W_out

    def _L0_ffn_ref(x, gate_w, w1, w2, w3, sw1, sw2, sw3, expert_bias):
        import jax, jax.numpy as jnp
        import numpy as np
        BS, SLEN, DIM, HID, E, TOPK = (4, 256, 256, 224, 8, 2)
        bs, slen, dim = x.shape
        T = bs * slen
        xf = x.reshape(T, dim)
        scores = jax.nn.softmax((xf @ gate_w).astype(jnp.float32), axis=-1)
        _, sel = jax.lax.top_k(scores + expert_bias[None, :], TOPK)
        top_scores = jnp.take_along_axis(scores, sel, axis=1)
        flat_sel = sel.reshape(-1)
        counts = jnp.bincount(flat_sel, length=E).astype(jnp.int32)
        order = jnp.argsort(flat_sel, stable=True)
        top_scores_sorted = top_scores.reshape(-1)[order]
        token_idx = order // TOPK
        routed_in = xf[token_idx] * top_scores_sorted[:, None]
        h = jax.nn.silu(jax.lax.ragged_dot(routed_in, w1, counts)) * jax.lax.ragged_dot(routed_in, w3, counts)
        routed_out = jax.lax.ragged_dot(h, w2, counts)
        out = jax.nn.silu(xf @ sw1) * (xf @ sw3) @ sw2
        out = out.at[token_idx].add(routed_out)
        return out.reshape(bs, slen, dim)

    def _L1_attn_ref(X, ln_w, ln_b, W_in, b_in, W_out, b_out):
        import jax, jax.numpy as jnp
        import numpy as np
        B, S, D = (4, 512, 256)
        THETA = 10000.0
        LN_EPS = 1e-05

        def _layernorm(x, w, b):
            mu = jnp.mean(x, axis=-1, keepdims=True)
            var = jnp.mean(jnp.square(x - mu), axis=-1, keepdims=True)
            return (x - mu) * jax.lax.rsqrt(var + LN_EPS) * w + b

        def _rope_half(x):
            rot_dim = x.shape[-1] // 2
            seq = x.shape[-2]
            inv_freq = 1.0 / THETA ** (jnp.arange(0, rot_dim, 2, dtype=jnp.float32) / rot_dim)
            freqs = jnp.arange(seq, dtype=jnp.float32)[:, None] * inv_freq[None, :]
            freqs = jnp.repeat(freqs, 2, axis=-1)
            cos, sin = (jnp.cos(freqs), jnp.sin(freqs))
            xl, xr = (x[..., :rot_dim], x[..., rot_dim:])
            x1, x2 = (xl[..., 0::2], xl[..., 1::2])
            rh = jnp.stack((-x2, x1), axis=-1).reshape(xl.shape)
            return jnp.concatenate([xl * cos + rh * sin, xr], axis=-1)

        def _cos_sim(x):
            return x / jnp.linalg.norm(x, axis=-1, keepdims=True)
        h = _layernorm(X, ln_w, ln_b)
        qkv = h @ W_in + b_in
        Q, K, V = jnp.split(qkv, 3, axis=-1)
        Q = _rope_half(Q)
        K = _rope_half(K)
        A = jnp.sum(_cos_sim(K) * V, axis=-2)
        Y = A[:, None, :] * Q
        Y = Y @ W_out + b_out
        return Y + X

    def _L1_ffn_ref(hidden_state, gate_w, gate_scale, up_w, up_scale, down_w, down_scale):
        import jax, jax.numpy as jnp
        import numpy as np
        ZERO_POINT = 128.0

        def _dequant(wq, scale):
            return (wq.astype(jnp.float32) - ZERO_POINT) * scale[:, None]
        Wg = _dequant(gate_w, gate_scale)
        Wu = _dequant(up_w, up_scale)
        Wd = _dequant(down_w, down_scale)
        g = jnp.einsum('bsh,ih->bsi', hidden_state, Wg)
        u = jnp.einsum('bsh,ih->bsi', hidden_state, Wu)
        h = jax.nn.silu(g) * u
        return jnp.einsum('bsi,hi->bsh', h, Wd)
    x = L0_attn_x
    x = _layernorm(x + _L0_attn_ref(x, L0_attn_W_in, L0_attn_W_out, L0_attn_dt_bias, L0_attn_A_log, L0_attn_D_param, L0_attn_B_bias, L0_attn_C_bias, L0_attn_rope_freqs, L0_attn_norm_w), axis=-1)
    x = _layernorm(x + _L0_ffn_ref(x, L0_ffn_gate_w, L0_ffn_w1, L0_ffn_w2, L0_ffn_w3, L0_ffn_sw1, L0_ffn_sw2, L0_ffn_sw3, L0_ffn_expert_bias), axis=-1)
    x = _layernorm(x + _L1_attn_ref(x, L1_attn_ln_w, L1_attn_ln_b, L1_attn_W_in, L1_attn_b_in, L1_attn_W_out, L1_attn_b_out), axis=-1)
    x = _layernorm(x + _L1_ffn_ref(x, L1_ffn_gate_w, L1_ffn_gate_scale, L1_ffn_up_w, L1_ffn_up_scale, L1_ffn_down_w, L1_ffn_down_scale), axis=-1)
    return x

_drawn_inputs = setup_inputs


def setup_inputs(seed=0):
    import zlib

    import numpy as np

    out = dict(_drawn_inputs(seed))
    spreads = {'L0_attn_D_param': (1.0, 0.2),
     'L0_attn_norm_w': (1.0, 0.2),
     'L0_ffn_expert_bias': (0.0, 0.8),
     'L1_attn_ln_w': (1.0, 0.2),
     'L1_attn_ln_b': (0.0, 0.1),
     'L1_attn_b_in': (0.0, 0.1),
     'L1_attn_b_out': (0.0, 0.1)}
    factors = {'L0_ffn_gate_w': 8.0, 'L0_ffn_w1': 8.0, 'L0_ffn_w2': 8.0, 'L0_ffn_w3': 8.0}
    for name, (base, spread) in spreads.items():
        noise = np.random.default_rng([zlib.crc32(name.encode()), seed]).standard_normal(out[name].shape)
        drawn = base * np.exp(spread * noise) if base else spread * noise
        out[name] = jnp.asarray(drawn.astype(out[name].dtype))
    for name, factor in factors.items():
        out[name] = (out[name] * factor).astype(out[name].dtype)
    return out
```

```python
import math
from contextlib import ExitStack

import concourse.bass as bass
from concourse import mybir

F32 = mybir.dt.float32
BF16 = mybir.dt.bfloat16
ALU = mybir.AluOpType
ACT = mybir.ActivationFunctionType

BATCH, SEQ, DM = 2, 2048, 256
TOK = BATCH * SEQ
P = 128
KT = DM // P
L = 128
NC = SEQ // L
CT = BATCH * L
NH, HD, NS = 64, 8, 64
DI = NH * HD
NB = 4
HB = NH // NB
NG = HB // 2
NQ = HB // 4
QA = NH // 4
MAGIC = 12582912.0
TWO_PI = 6.283185
EPS_RMS = 1e-6
EPS_LN = 1e-5


def at_least(e, sem, t, per, n, beside=None):
    v = t * per + n
    if isinstance(v, int) and v <= 0:
        return
    if beside is not None:
        e.wait_ge(beside, 1)
    e.wait_ge(sem, v)


def spread(ap, n):
    return bass.AP(tensor=ap.tensor, offset=ap.offset, ap=[list(z) for z in ap.ap] + [[0, n]])


def repeat(ap, n):
    pairs = [list(z) for z in ap.ap]
    return bass.AP(tensor=ap.tensor, offset=ap.offset, ap=[pairs[0], [0, n]] + pairs[1:])


def skew(ap, by):
    pairs = [list(z) for z in ap.ap]
    pairs[-2][0] += by
    return bass.AP(tensor=ap.tensor, offset=ap.offset, ap=pairs)


def on_all_partitions(ap):
    return bass.AP(tensor=ap.tensor, offset=ap.offset, ap=[[0, P]] + [list(z) for z in ap.ap])


def two_step_loop(e, body, steps, first=2, last=0):
    for t in range(first):
        body(t, t % 2)
    with e.Fori(first // 2, (steps - last) // 2) as j:
        body(j * 2, 0)
        body(j * 2 + 1, 1)
    for t in range(steps - last, steps):
        body(t, t % 2)


def project_and_decay(nc, held, I, W):
    with ExitStack() as ctx:
        def sb(name, shape, dt=F32):
            return ctx.enter_context(nc.sbuf_tensor("p0_" + name, shape, dt))

        def ps(name, n=512):
            return ctx.enter_context(nc.psum_tensor("p0_" + name, [P, n], F32))

        names = ("const_in prep x_in dt_mm bc_mm xs_mm ssq_mm cum_mm et_mm bc_sq rstd_ln rstd_ok v_ok vmax_ok vabs_ok vexp_ok "
                 "vln_ok dt_ok dtp_ok bcn_ok phi_ok carry_ok cumA_ok r1_ok piece_ok sufA_ok w_ok dec_ok decx_ok et_ok u_ok wu_ok "
                 "neg_ok").split()
        S = {n: signal(nc, held, "p0_" + n) for n in names}
        x_in = [signal(nc, held, f"p0_x_in{p}") for p in range(2)]
        stored = [signal(nc, held, f"p0_stored{p}") for p in range(2)]

        xT = sb("xT", [P, 2, KT, BATCH, L])
        w_bc = sb("w_bc", [P, KT, P])
        w_dt = sb("w_dt", [P, KT, NH])
        w_xs = sb("w_xs", [P, KT, DI])
        bias = sb("bias", [P, NH])
        nA_bc = sb("nA_bc", [P, NH])
        nA_hm = sb("nA_hm", [NH, 1])
        triu = sb("triu", [P, P])
        tril = sb("tril", [P, P])
        sel = sb("sel", [NH, NB, P])
        ones = sb("ones", [P, P])
        blk = sb("blk", [P, P])
        epsr = sb("epsr", [P, 1])
        carry = sb("carry", [NH, 2, BATCH])
        sq = sb("sq", [P, CT])
        lnv = sb("lnv", [P, CT])
        rstd = sb("rstd", [P, CT])
        bcn = sb("bcn", [P, 2, CT])
        v = sb("v", [P, BATCH, NH])
        vmax = sb("vmax", [P, BATCH, NH])
        vabs = sb("vabs", [P, BATCH, NH])
        vexp = sb("vexp", [P, BATCH, NH])
        vln = sb("vln", [P, BATCH, NH])
        dt = sb("dt", [P, BATCH, NH])
        dtp = sb("dtp", [P, BATCH, NH])
        phi = sb("phi", [NH, 2, CT])
        cumA = sb("cumA", [NH, CT])
        r1 = sb("r1", [NH, CT])
        r2 = sb("r2", [NH, CT])
        pieces = sb("pieces", [NH, 2, 3, CT], BF16)
        negs = sb("negs", [NH, 2, 3, CT], BF16)
        none = sb("none", [NH, CT], BF16)
        expo = sb("expo", [P, 2, BATCH, NH])
        w = sb("w", [P, BATCH, NH])
        dec = sb("dec", [P, BATCH, NH])
        decx = sb("decx", [P, 2, QA, BATCH, 2])
        zero = sb("zero", [P, NB, CT])
        et = sb("et", [P, 2, NB, CT])
        u = sb("u", [P, 2, BATCH, DI])
        wu = sb("wu", [P, 2, BATCH, DI])

        bc_ps = ps("bc_ps")
        dt_ps = ps("dt_ps")
        cum_ps = ps("cum_ps")
        ph_ps = ps("ph_ps")
        xs_ps = [ps(f"xs_ps{b}") for b in range(BATCH)]
        et_ps = [ps(f"et_ps{b}") for b in range(2)]
        NST = 11

        block = ctx.enter_context(nc.Block())

        @block.sync
        def _(e):
            for dst, src in ((w_bc, I["w_bc"]), (w_dt, I["w_dt"]), (w_xs, I["w_xs"])):
                e.dma_start(dst[:, :, :], src.rearrange("(k p) n -> p k n", p=P)).then_inc(S["const_in"], 16)
            e.dma_start(bias[:, :], on_all_partitions(I["dt_bias"])).then_inc(S["const_in"], 16)
            e.dma_start(nA_bc[:, :], on_all_partitions(I["A_log"])).then_inc(S["const_in"], 16)
            e.dma_start(nA_hm[:, :], I["A_hm"]).then_inc(S["const_in"], 16)
            e.dma_start(triu[:, :], I["c_triu"]).then_inc(S["const_in"], 16)
            e.dma_start(tril[:, :], I["c_tril"]).then_inc(S["const_in"], 16)
            e.dma_start(blk[:, :], I["c_blk"]).then_inc(S["const_in"], 16)
            e.dma_start(sel[:, :, :], I["c_sel"]).then_inc(S["const_in"], 16)

            def load(t, p):
                at_least(e, S["xs_mm"], t, 2, -2)
                for b in range(BATCH):
                    e.dma_start(xT[:, p, :, b, :],
                                I["xT"].rearrange("(k p) (b c l) -> p k b c l", p=P, b=BATCH, l=L)[:, :, b, bass.ds(t, 1), :]
                                .rearrange("p k c l -> p k (c l)")).then_inc(x_in[p], 16)

            def store(t, p):
                c = bass.ds(t, 1)
                def out(dst, src):
                    e.dma_start(dst, src).then_inc(stored[p], 16)
                at_least(e, S["bcn_ok"], t, 1, 1)
                bcd = W["bc"][c, :, :].rearrange("c r t -> (c r) t")
                out(bcd[0:64, :], bcn[0:64, p, :])
                out(bcd[64:96, :], bcn[0:32, p, :])
                out(bcd[96:160, :], bcn[64:128, p, :])
                out(bcd[160:192, :], bcn[64:96, p, :])
                at_least(e, S["phi_ok"], t, 2, 2)
                out(W["phi"][c, :, :].rearrange("c r t -> (c r) t"), phi[:, p, :])
                at_least(e, S["neg_ok"], t, 1, 1, S["prep"])
                out(W["pieces"][c, :, :, :].rearrange("c a r t -> (c r) a t"), pieces[:, p, :, :])
                out(W["negs"][c, :, :, :].rearrange("c a r t -> (c r) a t"), negs[:, p, :, :])
                at_least(e, S["decx_ok"], t, 2, 2)
                out(W["dec"][c, :, :].rearrange("c r t -> (c r) t"), (zero[:, 0, 0:NH] if isinstance(t, int) and t == 0
                     else decx[:, p, :, :, :].rearrange("p q b e -> p (q b e)")))
                at_least(e, S["et_ok"], t, 2, 2)
                out(W["et"][c, :, :, :].rearrange("c k r t -> (c r) k t"),
                    zero[:, :, :] if isinstance(t, int) and t == 0 else et[:, p, :, :])
                at_least(e, S["u_ok"], t, 2, 2)
                out(W["u"][c, :, :, :].rearrange("c b l d -> (c l) b d"), u[:, p, :, :])
                at_least(e, S["wu_ok"], t, 2, 2)
                out(W["wu"][c, :, :, :].rearrange("c b l d -> (c l) b d"), wu[:, p, :, :])

            e.wait_ge(S["prep"], 9)
            load(0, 0)
            load(1, 1)

            def step(t, p, more=True):
                store(t, p)
                if more:
                    load(t + 2, p)
            step(0, 0)
            step(1, 1)
            with e.Fori(1, NC // 2 - 1) as j:
                step(j * 2, 0)
                step(j * 2 + 1, 1)
            step(NC - 2, 0, False)
            step(NC - 1, 1, False)
            for p in range(2):
                e.wait_ge(stored[p], 16 * NST * NC // 2)

        @block.gpsimd
        def _(e):
            e.memset(ones[:, :], 1.0).then_inc(S["prep"], 1)
            e.memset(carry[:, :, :], 0.0).then_inc(S["prep"], 1)
            e.memset(epsr[:, :], EPS_RMS).then_inc(S["prep"], 1)
            e.memset(zero[:, :, :], 0.0).then_inc(S["prep"], 1)
            e.memset(none[:, :], 0.0).then_inc(S["prep"], 1)

            def step(t, p):
                if not (isinstance(t, int) and t < 2):
                    at_least(e, stored[p], (t - p) , 8 * NST, 0)
                at_least(e, S["piece_ok"], t, 3, 3)
                e.tensor_tensor(negs[:, p, :, :], repeat(none[:, :], 3), pieces[:, p, :, :], ALU.subtract).then_inc(S["neg_ok"], 1)
                at_least(e, S["u_ok"], t, 2, 2)
                at_least(e, S["w_ok"], t, 1, 1)
                for b in range(BATCH):
                    e.tensor_tensor(wu[:, p, b, :].rearrange("p (h d) -> p h d", d=HD),
                                    u[:, p, b, :].rearrange("p (h d) -> p h d", d=HD),
                                    spread(w[:, b, :], HD), ALU.mult).then_inc(S["wu_ok"], 1)
            two_step_loop(e, step, NC)

        @block.tensor
        def _(e):
            e.wait_ge(S["const_in"], 16 * 10)
            e.wait_ge(S["prep"], 9)

            def step(t, p):
                at_least(e, x_in[p], t - p, 16, 32)
                at_least(e, S["v_ok"], t, 1, 0)
                for b in range(BATCH):
                    for k in range(KT):
                        m = e.matmul(dt_ps[:, b * NH:(b + 1) * NH], xT[:, p, k, b, :], w_dt[:, k, :],
                                     start=(k == 0), stop=(k == KT - 1))
                m.then_inc(S["dt_mm"], 1)
                at_least(e, S["bcn_ok"], t, 1, 0)
                for k in range(KT):
                    m = e.matmul(bc_ps[:, 0:CT], w_bc[:, k, :], xT[:, p, k, :, :].rearrange("p b l -> p (b l)"),
                                 start=(k == 0), stop=(k == KT - 1))
                m.then_inc(S["bc_mm"], 1)
                for b in range(BATCH):
                    at_least(e, S["u_ok"], t, 2, b - 1)
                    for k in range(KT):
                        m = e.matmul(xs_ps[b][:, :], xT[:, p, k, b, :], w_xs[:, k, :],
                                     start=(k == 0), stop=(k == KT - 1))
                    m.then_inc(S["xs_mm"], 1)
                at_least(e, S["bc_sq"], t, 1, 1)
                e.matmul(bc_ps[:, CT:2 * CT], blk[:, :], sq[:, :], start=True, stop=True).then_inc(S["ssq_mm"], 1)
                at_least(e, S["dt_ok"], t, 1, 1)
                at_least(e, S["dtp_ok"], t, 2, 2)
                at_least(e, S["carry_ok"], t, 1, 0)
                at_least(e, S["cumA_ok"], t, 1, 0)
                at_least(e, S["sufA_ok"], t, 2, 0)
                for b in range(BATCH):
                    e.matmul(ph_ps[0:NH, b * L:(b + 1) * L], dtp[:, b, :],
                             triu[:, :], start=True, stop=True)
                e.matmul(cum_ps[:, 0:2 * NH], tril[:, :], dt[:, :, :].rearrange("p b h -> p (b h)"), start=True, stop=True)
                e.matmul(cum_ps[:, 2 * NH:4 * NH], ones[:, :], dt[:, :, :].rearrange("p b h -> p (b h)"),
                         start=True, stop=True).then_inc(S["cum_mm"], 1)
                at_least(e, S["cumA_ok"], t, 1, 1)
                at_least(e, S["et_ok"], t, 2, 0)
                for n in range(NB):
                    m = e.matmul(et_ps[n // 2][:, n % 2 * CT:(n % 2 + 1) * CT], sel[:, n, :], cumA[:, :],
                                 start=True, stop=True)
                m.then_inc(S["et_mm"], 1)
            two_step_loop(e, step, NC)

        @block.scalar
        def _(e):
            e.wait_ge(S["const_in"], 16 * 10)
            e.activation(nA_bc[:, :], nA_bc[:, :], ACT.Exp).then_inc(S["prep"], 1)
            e.activation(nA_hm[:, :], nA_hm[:, :], ACT.Exp).then_inc(S["prep"], 1)
            e.wait_ge(S["prep"], 9)

            def step(t, p):
                at_least(e, S["bc_mm"], t, 1, 1)
                e.activation(sq[:, :], bc_ps[:, 0:CT], ACT.Square).then_inc(S["bc_sq"], 1)
                at_least(e, S["v_ok"], t, 1, 1)
                e.activation(vabs[:, :, :], v[:, :, :], ACT.Abs).then_inc(S["vabs_ok"], 1)
                at_least(e, S["vabs_ok"], t, 1, 1)
                e.activation(vexp[:, :, :], vabs[:, :, :], ACT.Exp, scale=-1.0).then_inc(S["vexp_ok"], 1)
                at_least(e, S["vexp_ok"], t, 1, 1)
                at_least(e, S["dt_ok"], t, 1, 0)
                e.activation(vln[:, :, :], vexp[:, :, :], ACT.Ln, bias=1.0).then_inc(S["vln_ok"], 1)
                at_least(e, S["ssq_mm"], t, 1, 1)
                e.activation(lnv[:, :], bc_ps[:, CT:2 * CT], ACT.Ln, bias=epsr[:, :], scale=1.0 / NS).then_inc(S["rstd_ln"], 1)
                at_least(e, S["rstd_ln"], t, 1, 1)
                at_least(e, S["bcn_ok"], t, 1, 0)
                e.activation(rstd[:, :], lnv[:, :], ACT.Exp, scale=-0.5).then_inc(S["rstd_ok"], 1)
                at_least(e, S["sufA_ok"], t, 2, 2)
                at_least(e, S["wu_ok"], t, 2, 0)
                e.activation(w[:, :, :], expo[:, 0, :, :], ACT.Exp).then_inc(S["w_ok"], 1)
                at_least(e, S["decx_ok"], t, 2, 0)
                e.activation(dec[:, :, :], expo[:, 1, :, :], ACT.Exp).then_inc(S["dec_ok"], 1)
                at_least(e, S["et_mm"], t, 1, 1)
                if not (isinstance(t, int) and t < 2):
                    at_least(e, stored[p], (t - p), 8 * NST, 0)
                for n in range(2):
                    e.activation(et[:, p, 2 * n:2 * n + 2, :], et_ps[n][:, :].rearrange("p (k t) -> p k t", k=2),
                                 ACT.Exp, scale=1.0).then_inc(S["et_ok"], 1)
            two_step_loop(e, step, NC)

        @block.vector
        def _(e):
            e.wait_ge(S["prep"], 7)
            e.tensor_scalar(nA_bc[:, :], nA_bc[:, :], -1.0, None, ALU.mult).then_inc(S["prep"], 1)
            e.tensor_scalar(nA_hm[:, :], nA_hm[:, :], -1.0, None, ALU.mult).then_inc(S["prep"], 1)
            e.wait_ge(S["prep"], 9)

            def step(t, p):
                at_least(e, S["dt_mm"], t, 1, 1)
                at_least(e, S["vabs_ok"], t, 1, 0)
                e.tensor_tensor(v[:, :, :], dt_ps[:, 0:2 * NH].rearrange("p (b h) -> p b h", b=BATCH),
                                repeat(bias[:, :], BATCH), ALU.add).then_inc(S["v_ok"], 1)
                at_least(e, S["v_ok"], t, 1, 1)
                e.tensor_scalar(vmax[:, :, :], v[:, :, :], 0.0, None, ALU.max).then_inc(S["vmax_ok"], 1)
                at_least(e, S["vmax_ok"], t, 1, 1)
                at_least(e, S["vln_ok"], t, 1, 1)
                at_least(e, S["cum_mm"], t, 1, 0)
                at_least(e, S["u_ok"], t, 2, 0)
                for b in range(BATCH):
                    e.tensor_tensor(dtp[:, b, :].rearrange("p (h q) -> p q h", h=4), vmax[:, b, :].rearrange("p (q h) -> p q h", h=4),
                                    vln[:, b, :].rearrange("p (q h) -> p q h", h=4), ALU.add).then_inc(S["dtp_ok"], 1)
                e.tensor_tensor(dt[:, :, :], vmax[:, :, :], vln[:, :, :], ALU.add).then_inc(S["dt_ok"], 1)
                if not (isinstance(t, int) and t < 2):
                    at_least(e, stored[p], (t - p), 8 * NST, 0)
                at_least(e, S["rstd_ok"], t, 1, 1)
                e.tensor_tensor(bcn[:, p, :], bc_ps[:, 0:CT], rstd[:, :], ALU.mult).then_inc(S["bcn_ok"], 1)
                at_least(e, S["cum_mm"], t, 1, 1)
                at_least(e, S["carry_ok"], t, 1, 0)
                at_least(e, S["et_mm"], t, 1, 0)
                e.tensor_scalar(cumA[:, :], ph_ps[0:NH, 0:CT], nA_hm[:, :], None, ALU.mult).then_inc(S["cumA_ok"], 1)
                for b in range(BATCH):
                    e.tensor_scalar(phi[:, p, b * L:(b + 1) * L], ph_ps[0:NH, b * L:(b + 1) * L], carry[:, p, b:b + 1],
                                    1.0 / (2.0 * math.pi), ALU.add, ALU.mult).then_inc(S["phi_ok"], 1)
                e.tensor_tensor(carry[:, 1 - p, :], ph_ps[0:NH, 0:CT].rearrange("p (b l) -> p b l", b=BATCH)[:, :, L - 1],
                                carry[:, p, :], ALU.add).then_inc(S["carry_ok"], 1)
                at_least(e, S["cumA_ok"], t, 1, 1)
                e.tensor_copy(pieces[:, p, 0, :], cumA[:, :]).then_inc(S["piece_ok"], 1)
                at_least(e, S["piece_ok"], t, 3, 1)
                e.tensor_tensor(r1[:, :], cumA[:, :], pieces[:, p, 0, :], ALU.subtract).then_inc(S["r1_ok"], 1)
                at_least(e, S["r1_ok"], t, 2, 1)
                e.tensor_copy(pieces[:, p, 1, :], r1[:, :]).then_inc(S["piece_ok"], 1)
                at_least(e, S["piece_ok"], t, 3, 2)
                e.tensor_tensor(r2[:, :], r1[:, :], pieces[:, p, 1, :], ALU.subtract).then_inc(S["r1_ok"], 1)
                at_least(e, S["r1_ok"], t, 2, 2)
                e.tensor_copy(pieces[:, p, 2, :], r2[:, :]).then_inc(S["piece_ok"], 1)
                at_least(e, S["w_ok"], t, 1, 0)
                at_least(e, S["dec_ok"], t, 1, 0)
                for n in range(2):
                    e.tensor_tensor(expo[:, n, :, :], cum_ps[:, n * 2 * NH:(n + 1) * 2 * NH].rearrange("p (b h) -> p b h", b=BATCH),
                                    repeat(nA_bc[:, :], BATCH), ALU.mult).then_inc(S["sufA_ok"], 1)
                for b in range(BATCH):
                    at_least(e, S["xs_mm"], t, 2, b + 1)
                    at_least(e, S["dt_ok"], t, 1, 1)
                    e.tensor_tensor(u[:, p, b, :].rearrange("p (h d) -> p h d", d=HD),
                                    xs_ps[b][:, :].rearrange("p (h d) -> p h d", d=HD),
                                    spread(dt[:, b, :], HD), ALU.mult).then_inc(S["u_ok"], 1)
                at_least(e, S["dec_ok"], t, 1, 1)
                for h in range(2):
                    e.tensor_copy(decx[h * 64:(h + 1) * 64, p, :, :, :],
                                  dec[h * 64:(h + 1) * 64, :, :].rearrange("p b (q e h) -> p q b e h", e=2, h=2)[:, :, :, :, h]
                                  ).then_inc(S["decx_ok"], 1)
            two_step_loop(e, step, NC)


def state_space_scan(nc, held, I, W):
    T = NB * NC
    with ExitStack() as ctx:
        def sb(name, shape, dt=F32):
            return ctx.enter_context(nc.sbuf_tensor("p1_" + name, shape, dt))

        def ps(name):
            return ctx.enter_context(nc.psum_tensor("p1_ps_" + name, [P, 512], F32))

        names = ("const_in prep zeroed ph_mm mg_ok rn_ok abs_ok sin_ok cos_ok prodC rotC prodB rotB tr_mm bt_ok sc_mm g_mm d_ok "
                 "m_ok yi_mm yx_mm ns_mm ustage st_dec st_ok yx_ok y_ok").split()
        S = {n: signal(nc, held, "p1_" + n) for n in names}

        def sem2(n):
            return [signal(nc, held, f"p1_{n}{p}") for p in range(2)]
        trig_in, rot_in, dec_in, y_out = sem2("trig_in"), sem2("rot_in"), sem2("dec_in"), sem2("y_out")

        ident = sb("ident", [P, P])
        identb = sb("identb", [P, P], BF16)
        maskf = sb("maskf", [P, P])
        mask4 = sb("mask4", [P, 4, P], BF16)
        ind = sb("ind", [15, 4])
        turn = sb("turn", [P, 1])
        quart = sb("quart", [P, 1])
        one = sb("one", [P, HD])
        phi = sb("phi", [NH, 2, CT])
        freq = sb("freq", [NH, 2, NG, P])
        beta = sb("beta", [P, 2, 4, NG])
        bc = sb("bc", [P, 2, 4, CT])
        GR = sb("GR", [15, 2, 4, NQ * CT], BF16)
        GL = sb("GL", [15, 2, NQ * CT], BF16)
        u_in = sb("u_in", [P, 2, BATCH, HB * HD])
        wu = sb("wu", [P, 2, BATCH, HB * HD])
        dec = sb("dec", [P, 2, NG * BATCH])
        et = sb("et", [P, 2, CT])
        uexp = sb("uexp", [P, 2, BATCH, HB, 32])
        mg = sb("mg", [P, 2, 512])
        rn = sb("rn", [P, 2, 512])
        ab = sb("ab", [P, 2, 512])
        sn = sb("sn", [P, 2, NG, CT])
        cs = sb("cs", [P, 2, NG, CT])
        pc = sb("pc", [P, 2, 2, CT])
        pb = sb("pb", [P, 2, 2, CT])
        CR = sb("CR", [P, 4, CT])
        BR = sb("BR", [P, 4, CT])
        BT = sb("BT", [P, 2, 4, P])
        D = sb("D", [P, 2, 512])
        M = sb("M", [P, 4, 512])
        ST = sb("ST", [P, NQ, BATCH, 2, 32])
        yx = sb("yx", [P, 2, CT])
        y = sb("y", [P, 2, CT])

        ph_ps, bt_ps, g_ps, yi_ps, yx_ps, ns_ps = (ps(n) for n in ("ph", "bt", "g", "yi", "yx", "ns"))
        sc_ps = [ps(f"sc{n}") for n in range(2)]
        block = ctx.enter_context(nc.Block())
        U = NQ * BATCH

        @block.sync
        def _(e):
            e.dma_start(ident[:, :], I["c_ident"]).then_inc(S["const_in"], 16)
            e.dma_start(maskf[:, :], I["c_mask"]).then_inc(S["const_in"], 16)
            e.dma_start(ind[:, :], I["c_ind"]).then_inc(S["const_in"], 16)
            e.dma_start(turn[:, :], I["c_turn"]).then_inc(S["const_in"], 16)
            e.wait_ge(S["prep"], 5)

            def store(t, p):
                e.dma_start(W["y"][bass.ds(t, 1), :, :].rearrange("c r t -> (c r) t"), y[:, p, :]).then_inc(y_out[p], 16)

            def load_trig(k, c, t, p):
                at_least(e, S["ph_mm"], t, 4, -4)
                cc = bass.ds(c, 1)
                e.dma_start(phi[:, p, :], W["phi"][cc, :, :].rearrange("c r t -> (c r) t")).then_inc(trig_in[p], 16)
                e.dma_start(freq[:, p, :, :], I["freq"][bass.ds(k, 1), :, :, :].rearrange("k r g m -> (k r) g m")
                            ).then_inc(trig_in[p], 16)

            def load_rest(k, c, t, p):
                kk, cc = bass.ds(k, 1), bass.ds(c, 1)
                at_least(e, S["rotB"], t, NG, -NG)
                at_least(e, S["rotC"], t, NG, -NG)
                e.dma_start(beta[:, p, :, :], I["beta"][kk, :, :, :].rearrange("k p a g -> (k p) a g")).then_inc(rot_in[p], 16)
                for n, row in enumerate((0, 32, 96, 128)):
                    for h in range(2):
                        e.dma_start(bc[h * 64:(h + 1) * 64, p, n, :],
                                    W["bc"][cc, row:row + 64, :].rearrange("c r t -> (c r) t")).then_inc(rot_in[p], 16)
                at_least(e, S["g_mm"], t, U, -U, S["prep"])
                for a in range(3):
                    e.dma_start(GR[a:a + 1, p, :, :],
                                W["pieces"][cc, a, :, :].rearrange("c (h k q) t -> c k h (q t)", h=4, k=NB)[:, kk, :, :]
                                .rearrange("c k h n -> (c k) h n")).then_inc(rot_in[p], 16)
                    e.dma_start(GL[3 + 4 * a:7 + 4 * a, p, :],
                                W["negs"][cc, a, :, :].rearrange("c (h k q) t -> c k h (q t)", h=4, k=NB)[:, kk, :, :]
                                .rearrange("c k h n -> (c k h) n")).then_inc(rot_in[p], 16)
                at_least(e, S["ns_mm"], t, NQ, -NQ)
                e.dma_start(u_in[:, p, :, :], W["u"][cc, :, :, :].rearrange("c b l (k d) -> c k l b d", k=NB)[:, kk, :, :, :]
                            .rearrange("c k l b d -> (c k l) b d")).then_inc(rot_in[p], 16)
                e.dma_start(wu[:, p, :, :], W["wu"][cc, :, :, :].rearrange("c b l (k d) -> c k l b d", k=NB)[:, kk, :, :, :]
                            .rearrange("c k l b d -> (c k l) b d")).then_inc(rot_in[p], 16)
                at_least(e, S["y_ok"], t, 1, -1)
                if not (isinstance(t, int) and t < 2):
                    store(t - 2, p)
                e.dma_start(dec[:, p, :], W["dec"][cc, :, :].rearrange("c p (k n) -> c k p n", k=NB)[:, kk, :, :]
                            .rearrange("c k p n -> (c k p) n")).then_inc(dec_in[p], 16)
                e.dma_start(et[:, p, :], W["et"][cc, :, :, :][:, kk, :, :].rearrange("c k p t -> (c k p) t")
                            ).then_inc(dec_in[p], 16)

            for c in range(2):
                load_trig(0, c, c, c)
                load_rest(0, c, c, c)
            with e.Fori(1, NC // 2) as j:
                for p in range(2):
                    load_trig(0, j * 2 + p, j * 2 + p, p)
                    load_rest(0, j * 2 + p, j * 2 + p, p)
            with e.Fori(1, NB) as k:
                with e.Fori(0, NC // 2) as j:
                    for p in range(2):
                        load_trig(k, j * 2 + p, k * NC + j * 2 + p, p)
                        load_rest(k, j * 2 + p, k * NC + j * 2 + p, p)
            for p in range(2):
                at_least(e, S["y_ok"], T, 1, p - 1)
                store(T - 2 + p, p)
                e.wait_ge(y_out[p], 16 * T // 2)

        @block.gpsimd
        def _(e):
            e.memset(quart[:, :], math.pi / 2).then_inc(S["zeroed"], 1)
            e.memset(one[:, :], 1.0).then_inc(S["zeroed"], 1)
            e.memset(GL[:, :, :], 1.0).then_inc(S["prep"], 1)
            e.memset(uexp[:, :, :, :, :], 0.0).then_inc(S["zeroed"], 1)
            e.memset(ST[:, :, :, :, :], 0.0).then_inc(S["zeroed"], 1)
            e.wait_ge(S["zeroed"], 4)

            def stage_u(t, p):
                at_least(e, rot_in[p], t - p, 8 * 17, 16 * 17)
                at_least(e, S["yi_mm"], t, U, -U)
                for b in range(BATCH):
                    for q in range(NQ):
                        e.tensor_tensor(skew(uexp[:, p, b, 4 * q:4 * q + 4, 0:HD], HD),
                                        u_in[:, p, b, q * 32:(q + 1) * 32].rearrange("p (h d) -> p h d", d=HD),
                                        repeat(one[:, :], 4), ALU.mult).then_inc(S["ustage"], 1)

            def step(t, p):
                stage_u(t, p)
                for g in range(NG):
                    at_least(e, S["prodC"], t, 2 * NG, 2 * g + 2)
                    at_least(e, S["yx_mm"], t, U, ((g - 4) // 2 + 1) * 2)
                    at_least(e, S["sc_mm"], t, U, ((g - 4) // 2 + 1) * 2)
                    e.tensor_tensor(CR[:, g % 4, :], pc[:, g % 2, 0, :], pc[:, g % 2, 1, :], ALU.add).then_inc(S["rotC"], 1)
                    at_least(e, S["prodB"], t, 2 * NG, 2 * g + 2)
                    at_least(e, S["tr_mm"], t, NG, g - 3)
                    e.tensor_tensor(BR[:, g % 4, :], pb[:, g % 2, 0, :], pb[:, g % 2, 1, :], ALU.add).then_inc(S["rotB"], 1)
            two_step_loop(e, step, T)

        @block.tensor
        def _(e):
            e.wait_ge(S["prep"], 5)
            e.wait_ge(S["zeroed"], 4)
            e.wait_ge(S["const_in"], 64)

            def phases(t, p):
                at_least(e, trig_in[p], t - p, 16, 32)
                for n in range(4):
                    at_least(e, S["rn_ok"], t, 4, n)
                    for g in range(2):
                        m = e.matmul(ph_ps[:, g * CT:(g + 1) * CT], freq[:, p, 2 * n + g, :], phi[:, p, :],
                                     start=True, stop=True)
                    m.then_inc(S["ph_mm"], 1)

            def quad(t, p, q):
                for g in (2 * q, 2 * q + 1):
                    at_least(e, S["rotB"], t, NG, g + 1)
                    at_least(e, S["bt_ok"], t, NQ, q)
                    for b in range(BATCH):
                        m = e.transpose(bt_ps[:, (g % 2 * 2 + b) * P:(g % 2 * 2 + b + 1) * P],
                                        BR[:, g % 4, b * L:(b + 1) * L], ident[:, :])
                    m.then_inc(S["tr_mm"], 1)
                for half in range(2):
                    n = 2 * q + half
                    at_least(e, rot_in[p], t - p, 8 * 17, 16 * 17)
                    at_least(e, S["d_ok"], t, U, n)
                    e.matmul(g_ps[:, :], identb[:, :], mask4[:, :, :].rearrange("p h l -> p (h l)"), start=True, stop=False)
                    for b in range(BATCH):
                        cols = slice(q * CT + b * L, q * CT + b * L + L)
                        m = e.matmul(g_ps[:, :].rearrange("p (g b l) -> p g b l", g=2, b=BATCH)[:, :, b, :], GL[:, p, cols],
                                     GR[:, p, half:4:2, cols], start=False, stop=(b == 1))
                    m.then_inc(S["g_mm"], 1)
                    at_least(e, S["rotC"], t, NG, 2 * q + 2)
                    at_least(e, S["m_ok"], t, U, n - 1)
                    for g in range(2):
                        for b in range(BATCH):
                            m = e.matmul(sc_ps[half][:, (g * 2 + b) * L:(g * 2 + b + 1) * L],
                                         BR[half * 64:half * 64 + 64, (2 * q + g) % 4, b * L:(b + 1) * L],
                                         CR[half * 64:half * 64 + 64, (2 * q + g) % 4, b * L:(b + 1) * L], start=True, stop=True)
                    m.then_inc(S["sc_mm"], 1)
                if q == 0:
                    at_least(e, S["st_ok"], t, 2, 0)
                    at_least(e, S["yx_ok"], t, 1, 0)
                for b in range(BATCH):
                    for g in range(2):
                        m = e.matmul(yx_ps[32 * q:32 * q + 32, b * L:(b + 1) * L], ST[:, q, b, g, :],
                                     CR[:, (2 * q + g) % 4, b * L:(b + 1) * L], start=(g == 0), stop=(g == 1))
                    m.then_inc(S["yx_mm"], 1)

            def outputs(t, p, q):
                for b in range(BATCH):
                    if q == 0 and b == 0:
                        at_least(e, S["y_ok"], t, 1, 0)
                        at_least(e, S["ustage"], t, U, U)
                    at_least(e, S["m_ok"], t, U, 2 * q + 2)
                    for h in range(4):
                        m = e.matmul(yi_ps[32 * q:32 * q + 32, b * L:(b + 1) * L], uexp[:, p, b, 4 * q + h, :],
                                     M[:, 2 * (q % 2) + h % 2, (h // 2 * 2 + b) * L:(h // 2 * 2 + b + 1) * L], start=(h == 0), stop=(h == 3))
                    m.then_inc(S["yi_mm"], 1)
                if q == 0:
                    at_least(e, S["st_ok"], t, 2, 0)
                at_least(e, S["bt_ok"], t, NQ, q + 1)
                for g in range(2):
                    for b in range(BATCH):
                        m = e.matmul(ns_ps[:, ((q * 2 + b) * 2 + g) * 16:((q * 2 + b) * 2 + g) * 16 + 16], BT[:, q % 2, g * 2 + b, :],
                                     wu[:, p, b, (2 * q + g) * 16:(2 * q + g) * 16 + 16], start=True, stop=True)
                m.then_inc(S["ns_mm"], 1)

            def step(t, p, ahead=True):
                for q in range(NQ):
                    quad(t, p, q)
                    if q:
                        outputs(t, p, q - 1)
                if ahead:
                    phases(t + 1, 1 - p)
                outputs(t, p, NQ - 1)
            phases(0, 0)
            step(0, 0)
            step(1, 1)
            with e.Fori(1, T // 2 - 1) as j:
                step(j * 2, 0)
                step(j * 2 + 1, 1)
            step(T - 2, 0)
            step(T - 1, 1, False)

        @block.scalar
        def _(e):
            e.wait_ge(S["zeroed"], 4)
            e.wait_ge(S["const_in"], 64)

            def trig(t, p):
                for n in range(4):
                    at_least(e, S["ph_mm"], t, 4, n + 1)
                    at_least(e, S["rn_ok"], t, 4, n - 1)
                    e.activation(mg[:, n % 2, :], ph_ps[:, :], ACT.Copy, bias=MAGIC).then_inc(S["mg_ok"], 1)
                    at_least(e, S["rn_ok"], t, 4, n + 1)
                    at_least(e, S["cos_ok"], t, 4, n - 1)
                    e.activation(ab[:, n % 2, :], rn[:, n % 2, :], ACT.Abs).then_inc(S["abs_ok"], 1)
                    at_least(e, S["prodB"], t, 2 * NG, -2 * NG)
                    at_least(e, S["prodC"], t, 2 * NG, -2 * NG)
                    e.activation(sn[:, p, 2 * n:2 * n + 2, :].rearrange("p g t -> p (g t)"), rn[:, n % 2, :], ACT.Sin,
                                 scale=turn[:, :]).then_inc(S["sin_ok"], 1)
                    at_least(e, S["abs_ok"], t, 4, n + 1)
                    e.activation(cs[:, p, 2 * n:2 * n + 2, :].rearrange("p g t -> p (g t)"), ab[:, n % 2, :], ACT.Sin,
                                 bias=quart[:, :], scale=-TWO_PI).then_inc(S["cos_ok"], 1)

            def step(t, p, ahead=True):
                for q in range(NQ):
                    for b in range(BATCH):
                        n = 2 * q + b
                        at_least(e, S["g_mm"], t, U, n + 1)
                        at_least(e, S["m_ok"], t, U, n - 1)
                        e.activation(D[:, n % 2, :], g_ps[:, :], ACT.Exp).then_inc(S["d_ok"], 1)
                    at_least(e, S["tr_mm"], t, NG, 2 * q + 2)
                    at_least(e, S["ns_mm"], t, NQ, q - 1)
                    e.activation(BT[:, q % 2, :, :].rearrange("p a n -> p (a n)"), bt_ps[:, :], ACT.Copy).then_inc(S["bt_ok"], 1)
                if ahead:
                    trig(t + 1, 1 - p)
            trig(0, 0)
            step(0, 0)
            step(1, 1)
            with e.Fori(1, T // 2 - 1) as j:
                step(j * 2, 0)
                step(j * 2 + 1, 1)
            step(T - 2, 0)
            step(T - 1, 1, False)

        @block.vector
        def _(e):
            e.wait_ge(S["const_in"], 64)
            e.tensor_copy(GR[:, :, :, :].rearrange("p a h n -> p (a h) n")[:, 0:4, :], spread(ind[:, :], NQ * CT)
                          ).then_inc(S["prep"], 1)
            e.tensor_copy(GR[:, :, :, :].rearrange("p a h n -> p (a h) n")[:, 4:8, :], spread(ind[:, :], NQ * CT)
                          ).then_inc(S["prep"], 1)
            e.tensor_copy(mask4[:, :, :], repeat(maskf[:, :], 4)).then_inc(S["prep"], 1)
            e.tensor_copy(identb[:, :], ident[:, :]).then_inc(S["prep"], 1)
            e.wait_ge(S["zeroed"], 4)

            def trig(t, n):
                at_least(e, S["mg_ok"], t, 4, n + 1)
                at_least(e, S["cos_ok"], t, 4, n - 1)
                at_least(e, S["sin_ok"], t, 4, n - 1)
                e.scalar_tensor_tensor(out=rn[:, n % 2, :], in0=mg[:, n % 2, :], scalar=MAGIC, in1=ph_ps[:, :],
                                       op0=ALU.subtract, op1=ALU.subtract).then_inc(S["rn_ok"], 1)

            def products(t, p, g):
                at_least(e, S["cos_ok"], t, 4, g // 2 + 1)
                at_least(e, S["sin_ok"], t, 4, g // 2 + 1)
                at_least(e, rot_in[p], t - p, 8 * 17, 16 * 17)
                at_least(e, S["rotC"], t, NG, g - 1)
                for n, tr in ((2, cs), (3, sn)):
                    e.scalar_tensor_tensor(out=pc[:, g % 2, n - 2, :], in0=bc[:, p, n, :], scalar=beta[:, p, n, g:g + 1],
                                           in1=tr[:, p, g, :], op0=ALU.add, op1=ALU.mult).then_inc(S["prodC"], 1)
                at_least(e, S["rotB"], t, NG, g - 1)
                for n, tr in ((0, cs), (1, sn)):
                    e.scalar_tensor_tensor(out=pb[:, g % 2, n, :], in0=bc[:, p, n, :], scalar=beta[:, p, n, g:g + 1],
                                           in1=tr[:, p, g, :], op0=ALU.add, op1=ALU.mult).then_inc(S["prodB"], 1)

            def decayed(t, n):
                at_least(e, S["sc_mm"], t, U, n + 1)
                at_least(e, S["d_ok"], t, U, n + 1)
                at_least(e, S["yi_mm"], t, U, n // 2 * 2 - 2)
                e.tensor_tensor(M[:, n % 4, :], sc_ps[n % 2][:, :], D[:, n % 2, :], ALU.mult).then_inc(S["m_ok"], 1)

            def finish(t, p):
                at_least(e, dec_in[p], t - p, 16, 32)
                at_least(e, S["yx_mm"], t, U, U)
                for h in range(2):
                    r = slice(h * 64, h * 64 + 64)
                    e.tensor_tensor(state_blocks(r, h), state_blocks(r, h),
                                    spread(dec[r, p, :].rearrange("p (n e) -> p n e", e=2), HD), ALU.mult).then_inc(S["st_dec"], 1)
                at_least(e, S["ns_mm"], t, NQ, NQ)
                at_least(e, S["st_dec"], t, 2, 2)
                for h in range(2):
                    r = slice(h * 64, h * 64 + 64)
                    e.tensor_tensor(state_blocks(r, h), state_blocks(r, h),
                                    ns_ps[r, 0:NQ * BATCH * 32].rearrange("p (n e d) -> p n e d", e=2, d=16)[:, :, :, h * HD:(h + 1) * HD],
                                    ALU.add).then_inc(S["st_ok"], 1)
                e.tensor_tensor(yx[:, p, :], yx_ps[:, 0:CT], et[:, p, :], ALU.mult).then_inc(S["yx_ok"], 1)
                at_least(e, S["yx_ok"], t, 1, 1)
                at_least(e, S["yi_mm"], t, U, U)
                if not (isinstance(t, int) and t < 2):
                    at_least(e, y_out[p], t - p, 8, 0)
                e.tensor_tensor(y[:, p, :], yi_ps[:, 0:CT], yx[:, p, :], ALU.add).then_inc(S["y_ok"], 1)

            def state_blocks(r, h):
                return skew(ST[r, :, :, :, h * HD:(h + 1) * HD].rearrange("p q b e d -> p (q b) e d"), 16)

            def step(t, p, ahead=True):
                for g in range(NG):
                    products(t, p, g)
                    if g % 2 == 0 and g:
                        decayed(t, g - 2)
                        decayed(t, g - 1)
                if ahead:
                    trig(t + 1, 0)
                decayed(t, 2 * NQ - 2)
                decayed(t, 2 * NQ - 1)
                if ahead:
                    for n in range(1, 4):
                        trig(t + 1, n)
                finish(t, p)
            for n in range(4):
                trig(0, n)
            step(0, 0)
            step(1, 1)
            with e.Fori(1, T // 2 - 1) as j:
                step(j * 2, 0)
                step(j * 2 + 1, 1)
            step(T - 2, 0)
            step(T - 1, 1, False)



def norm_names():
    return "ln_stat ln_mv ln_var ln_rs ln_out".split()


def norm_tiles(sb, n=""):
    return dict(st=sb(f"ln{n}_st", [P, BATCH, 6]), mv=sb(f"ln{n}_mv", [P, BATCH, 2]), ve=sb(f"ln{n}_ve", [P, BATCH]),
                rs=sb(f"ln{n}_rs", [P, BATCH]), go=sb(f"ln{n}_go", [P, 1]))


def norm_vector(e, S, N, t, src, dst, free):
    at_least(e, S["ln_out"], t, 2, 0)
    for b in range(BATCH):
        e.bn_stats(N["st"][:, b, :], src[:, b, :]).then_inc(S["ln_stat"], 1)
    at_least(e, S["ln_stat"], t, 2, 2)
    e.memset(N["go"][:, :], 0.0).then_inc(S["ln_mv"], 1)
    for b in range(BATCH):
        e.bn_aggr(N["mv"][:, b, :], N["st"][:, b, :]).then_inc(S["ln_mv"], 1)
    at_least(e, S["ln_mv"], t, 3, 3)
    e.tensor_scalar(N["ve"][:, :], N["mv"][:, :, 1], EPS_LN, None, ALU.add).then_inc(S["ln_var"], 1)
    at_least(e, S["ln_rs"], t, 1, 1)
    free()
    for b in range(BATCH):
        e.tensor_scalar(dst[:, b, :], src[:, b, :], N["mv"][:, b, 0:1], N["rs"][:, b:b + 1], ALU.subtract, ALU.mult
                        ).then_inc(S["ln_out"], 1)


def norm_pool(e, S, N, t, mhalf):
    at_least(e, S["ln_var"], t, 1, 1)
    e.tensor_tensor(N["rs"][:, :], N["ve"][:, :], mhalf[:, 0:BATCH], ALU.pow).then_inc(S["ln_rs"], 1)


def tokens_of(ap, t):
    return ap[bass.ds(t, 1), :, :, :].rearrange("c b l d -> (c l) b d")


def turned_of(ap, t):
    return ap[bass.ds(t, 1), :, :, :].rearrange("c p k t -> (c p) k t")


def signal(nc, held, name):
    held.append(nc.alloc_semaphore(name=name))
    return held[-1]


class Phase:

    def __init__(self, nc, ctx, held, prefix, names, pairs):
        self.nc, self.ctx, self.prefix = nc, ctx, prefix
        self.S = {n: signal(nc, held, f"{prefix}_{n}") for n in names.split()}
        for n in pairs.split():
            self.S[n] = [signal(nc, held, f"{prefix}_{n}{p}") for p in range(2)]

    def sb(self, name, shape, dt=F32):
        return self.ctx.enter_context(self.nc.sbuf_tensor(f"{self.prefix}_{name}", shape, dt))

    def ps(self, name):
        return self.ctx.enter_context(self.nc.psum_tensor(f"{self.prefix}_ps_{name}", [P, 512], F32))


def finish_mixer(nc, held, I, W):
    with ExitStack() as ctx:
        F = Phase(nc, ctx, held, "p2", "const_in prep fold xs_mm z_mm silu_ok mix_ok g_ok g2_ok o_mm ms_ok rms_ok xr_ok tr_mm xt_ok "
                  + " ".join(norm_names()), "x_in stored")
        S, sb, ps = F.S, F.sb, F.ps
        w_xs, w_z = sb("w_xs", [P, KT, DI]), sb("w_z", [P, KT, DI])
        w_out = sb("w_out", [P, NB, DM])
        d_bc = sb("d_bc", [P, DI])
        nw = sb("nw", [P, NB])
        ident = sb("ident", [P, P])
        ones = sb("ones", [P, 1])
        mhalf = sb("mhalf", [P, 2])
        xT = sb("xT", [P, 2, KT, BATCH, L])
        x = sb("x", [P, 2, BATCH, DM])
        y = sb("y", [P, 2, NB, CT])
        sz = sb("sz", [P, NB, CT])
        mix = sb("mix", [P, NB, CT])
        g = sb("g", [P, NB, CT])
        g2 = sb("g2", [P, NB, CT])
        ms, rms = sb("ms", [P, BATCH]), sb("rms", [P, BATCH])
        xr = sb("xr", [P, BATCH, DM])
        x1 = sb("x1", [P, 2, BATCH, DM])
        x1T = sb("x1T", [P, 2, KT, CT])
        N = norm_tiles(sb)
        xs_ps, z_ps = [ps(f"xs{n}") for n in range(2)], [ps(f"z{n}") for n in range(2)]
        o_ps, q_ps, t_ps = ps("o"), ps("q"), ps("t")
        block = ctx.enter_context(nc.Block())

        @block.sync
        def _(e):
            for dst, src in ((w_xs, I["w_xs"]), (w_z, I["w_z"]), (w_out, I["w_out"])):
                e.dma_start(dst[:, :, :], src.rearrange("(k p) n -> p k n", p=P)).then_inc(S["const_in"], 16)
            e.dma_start(d_bc[:, :], on_all_partitions(I["d_rep"])).then_inc(S["const_in"], 16)
            e.dma_start(nw[:, :], I["norm_w"]).then_inc(S["const_in"], 16)
            e.dma_start(ident[:, :], I["c_ident"]).then_inc(S["const_in"], 16)

            def load(t, p):
                at_least(e, S["z_mm"], t, 1, -1)
                at_least(e, S["mix_ok"], t, 2, -2)
                at_least(e, S["xr_ok"], t, 2, -2)
                for b in range(BATCH):
                    e.dma_start(xT[:, p, :, b, :],
                                I["xT"].rearrange("(k p) (b c l) -> p k b c l", p=P, b=BATCH, l=L)[:, :, b, bass.ds(t, 1), :]
                                .rearrange("p k c l -> p k (c l)")).then_inc(S["x_in"][p], 16)
                e.dma_start(x[:, p, :, :], I["x"].rearrange("b (c l) d -> c b l d", l=L)[bass.ds(t, 1), :, :, :]
                            .rearrange("c b l d -> (c l) b d")).then_inc(S["x_in"][p], 16)
                e.dma_start(y[:, p, :, :], W["y"].rearrange("(k c) r t -> c r k t", k=NB)[bass.ds(t, 1), :, :, :]
                            .rearrange("c r k t -> (c r) k t")).then_inc(S["x_in"][p], 16)

            def store(t, p):
                at_least(e, S["ln_out"], t, 2, 2)
                e.dma_start(tokens_of(W["x1"], t), x1[:, p, :, :]).then_inc(S["stored"][p], 16)
                at_least(e, S["xt_ok"], t, 1, 1)
                e.dma_start(turned_of(W["x1T"], t), x1T[:, p, :, :]).then_inc(S["stored"][p], 16)
            stream(e, load, store)
            for p in range(2):
                e.wait_ge(S["stored"][p], 16 * 2 * NC // 2)

        @block.gpsimd
        def _(e):
            e.memset(ones[:, :], 1.0).then_inc(S["prep"], 1)
            e.memset(mhalf[:, :], -0.5).then_inc(S["prep"], 1)
            e.wait_ge(S["prep"], 2)

            def step(t, p):
                at_least(e, S["ms_ok"], t, 1, 1)
                e.tensor_tensor(rms[:, :], ms[:, :], mhalf[:, :], ALU.pow).then_inc(S["rms_ok"], 1)
                norm_pool(e, S, N, t, mhalf)
            two_step_loop(e, step, NC)

        @block.tensor
        def _(e):
            e.wait_ge(S["const_in"], 16 * 6)
            e.wait_ge(S["prep"], 2)
            e.wait_ge(S["fold"], 2)

            def turn(t, p):
                at_least(e, S["ln_out"], t, 2, 2)
                at_least(e, S["xt_ok"], t, 1, 0)
                for k in range(KT):
                    for b in range(BATCH):
                        m = e.transpose(t_ps[:, (k * 2 + b) * P:(k * 2 + b + 1) * P], x1[:, p, b, k * P:(k + 1) * P], ident[:, :])
                m.then_inc(S["tr_mm"], 1)

            def step(t, p):
                at_least(e, S["x_in"][p], t - p, 32, 64)
                at_least(e, S["mix_ok"], t, 2, 0)
                for n in range(NB):
                    for k in range(KT):
                        m = e.matmul(xs_ps[n // 2][:, n % 2 * CT:(n % 2 + 1) * CT], w_xs[:, k, n * P:(n + 1) * P],
                                     xT[:, p, k, :, :].rearrange("p b l -> p (b l)"), start=(k == 0), stop=(k == KT - 1))
                m.then_inc(S["xs_mm"], 1)
                at_least(e, S["silu_ok"], t, 2, 0)
                for n in range(NB):
                    for k in range(KT):
                        m = e.matmul(z_ps[n // 2][:, n % 2 * CT:(n % 2 + 1) * CT], w_z[:, k, n * P:(n + 1) * P],
                                     xT[:, p, k, :, :].rearrange("p b l -> p (b l)"), start=(k == 0), stop=(k == KT - 1))
                m.then_inc(S["z_mm"], 1)
                if not (isinstance(t, int) and t == 0):
                    turn(t - 1, 1 - p)
                at_least(e, S["g2_ok"], t, 2, 2)
                at_least(e, S["xr_ok"], t, 2, 0)
                for b in range(BATCH):
                    for n in range(NB):
                        m = e.matmul(o_ps[:, b * DM:(b + 1) * DM], g[:, n, b * L:(b + 1) * L], w_out[:, n, :],
                                     start=(n == 0), stop=(n == NB - 1))
                for b in range(BATCH):
                    for n in range(NB):
                        m = e.matmul(q_ps[:, b:b + 1], g2[:, n, b * L:(b + 1) * L], ones[:, :], start=(n == 0), stop=(n == NB - 1))
                m.then_inc(S["o_mm"], 1)
            two_step_loop(e, step, NC)
            turn(NC - 1, 1)

        @block.scalar
        def _(e):
            def copy_turned(t, p):
                at_least(e, S["tr_mm"], t, 1, 1)
                if not (isinstance(t, int) and t < 2):
                    at_least(e, S["stored"][p], t - p, 16, 0)
                e.activation(x1T[:, p, :, :].rearrange("p k t -> p (k t)"), t_ps[:, :], ACT.Copy).then_inc(S["xt_ok"], 1)

            def step(t, p):
                at_least(e, S["z_mm"], t, 1, 1)
                at_least(e, S["g_ok"], t, 2, 0)
                for n in range(2):
                    e.activation(sz[:, 2 * n:2 * n + 2, :].rearrange("p n t -> p (n t)"), z_ps[n][:, :], ACT.Silu).then_inc(S["silu_ok"], 1)
                if not (isinstance(t, int) and t == 0):
                    copy_turned(t - 1, 1 - p)
                at_least(e, S["o_mm"], t, 1, 0)
                for n in range(2):
                    at_least(e, S["g_ok"], t, 2, n + 1)
                    e.activation(g2[:, 2 * n:2 * n + 2, :], g[:, 2 * n:2 * n + 2, :], ACT.Square).then_inc(S["g2_ok"], 1)
            two_step_loop(e, step, NC)
            copy_turned(NC - 1, 1)

        @block.vector
        def _(e):
            e.wait_ge(S["const_in"], 16 * 6)
            e.tensor_tensor(w_xs[:, :, :], w_xs[:, :, :], repeat(d_bc[:, :], KT), ALU.mult).then_inc(S["fold"], 1)
            e.tensor_tensor(w_out[:, :, :], w_out[:, :, :], spread(nw[:, :], DM), ALU.mult).then_inc(S["fold"], 1)

            def step(t, p):
                at_least(e, S["x_in"][p], t - p, 32, 64)
                at_least(e, S["xs_mm"], t, 1, 1)
                at_least(e, S["g_ok"], t, 2, 0)
                for n in range(2):
                    e.scalar_tensor_tensor(out=mix[:, 2 * n:2 * n + 2, :].rearrange("p n t -> p (n t)"),
                                           in0=y[:, p, 2 * n:2 * n + 2, :].rearrange("p n t -> p (n t)"), scalar=NS ** -0.5,
                                           in1=xs_ps[n][:, :], op0=ALU.mult, op1=ALU.add).then_inc(S["mix_ok"], 1)
                at_least(e, S["mix_ok"], t, 2, 2)
                at_least(e, S["o_mm"], t, 1, 0)
                at_least(e, S["g2_ok"], t, 2, 0)
                for n in range(2):
                    at_least(e, S["silu_ok"], t, 2, n + 1)
                    e.tensor_tensor(g[:, 2 * n:2 * n + 2, :], mix[:, 2 * n:2 * n + 2, :], sz[:, 2 * n:2 * n + 2, :], ALU.mult
                                    ).then_inc(S["g_ok"], 1)
                at_least(e, S["o_mm"], t, 1, 1)
                at_least(e, S["rms_ok"], t, 1, 0)
                e.tensor_scalar(ms[:, :], q_ps[:, 0:BATCH], 1.0 / DI, EPS_RMS, ALU.mult, ALU.add).then_inc(S["ms_ok"], 1)
                at_least(e, S["rms_ok"], t, 1, 1)
                at_least(e, S["ln_out"], t, 2, 0)
                for b in range(BATCH):
                    e.scalar_tensor_tensor(out=xr[:, b, :], in0=o_ps[:, b * DM:(b + 1) * DM], scalar=rms[:, b:b + 1],
                                           in1=x[:, p, b, :], op0=ALU.mult, op1=ALU.add).then_inc(S["xr_ok"], 1)
                at_least(e, S["xr_ok"], t, 2, 2)

                def free():
                    if not (isinstance(t, int) and t < 2):
                        at_least(e, S["stored"][p], t - p, 16, 0)
                        at_least(e, S["tr_mm"], t, 1, -1)
                norm_vector(e, S, N, t, xr, x1[:, p, :, :], free)
            two_step_loop(e, step, NC)


def stream(e, load, store):
    load(0, 0)
    load(1, 1)
    for p in range(2):
        load(2 + p, p)
        store(p, p)
    with e.Fori(1, NC // 2 - 1) as j:
        for p in range(2):
            load(j * 2 + 2 + p, p)
            store(j * 2 + p, p)
    for p in range(2):
        store(NC - 2 + p, p)


def mixture_of_experts(nc, held, I, W):
    E, HID = 8, 224
    HH = HID // 2
    with ExitStack() as ctx:
        F = Phase(nc, ctx, held, "p3", "const_in prep gate_mm gmax_ok gexp_ok gsum_ok score_ok sb_ok top_ok topi_ok topf_ok eq_ok wt_ok "
                  "wtT_mm wtT_ok sbc_mm xin_ok a_mm b_mm silu_ok h_ok o_mm xr_ok tr_mm xt_ok " + " ".join(norm_names()), "x_in stored")
        S, sb, ps = F.S, F.sb, F.ps
        w1, w3 = sb("w1", [P, KT, E + 1, HID]), sb("w3", [P, KT, E + 1, HID])
        w2 = sb("w2", [HH, 2, E + 1, DM])
        gw = sb("gw", [P, KT, E])
        ebias = sb("ebias", [P, E])
        iota = sb("iota", [P, E])
        ident = sb("ident", [P, P])
        row = sb("row", [E, E, P])
        mhalf = sb("mhalf", [P, 2])
        x1 = sb("x1", [P, 2, BATCH, DM])
        x1T = sb("x1T", [P, 2, KT, CT])
        gmax, gsum, grec = sb("gmax", [P, BATCH]), sb("gsum", [P, BATCH]), sb("grec", [P, BATCH])
        gsh = sb("gsh", [P, BATCH, E])
        gexp, score, sbias = sb("gexp", [P, BATCH, E]), sb("score", [P, BATCH, E]), sb("sbias", [P, BATCH, E])
        top = sb("top", [P, BATCH, 8])
        topi = sb("topi", [P, BATCH, 8], mybir.dt.uint32)
        topf = sb("topf", [P, BATCH, 8])
        eq = sb("eq", [P, BATCH, 2, E])
        wt = sb("wt", [P, BATCH, E])
        wtT = sb("wtT", [E, CT])
        xin = sb("xin", [P, 2, KT, CT])
        sa = sb("sa", [HH, 2, 2, CT])
        h = sb("h", [HH, 2, 2, CT])
        xr = sb("xr", [P, BATCH, DM])
        x2 = sb("x2", [P, 2, BATCH, DM])
        x2T = sb("x2T", [P, 2, KT, CT])
        N = norm_tiles(sb)
        g_ps, s_ps = ps("g"), ps("s")
        a_ps, b_ps = [ps(f"a{n}") for n in range(2)], [ps(f"b{n}") for n in range(2)]
        o_ps = [ps(f"o{b}") for b in range(BATCH)]
        block = ctx.enter_context(nc.Block())
        X = E + 1

        @block.sync
        def _(e):
            e.dma_start(w1[:, :, :, :], I["w1"].rearrange("(k p) e n -> p k e n", p=P)).then_inc(S["const_in"], 16)
            e.dma_start(w3[:, :, :, :], I["w3"].rearrange("(k p) e n -> p k e n", p=P)).then_inc(S["const_in"], 16)
            e.dma_start(w2[:, :, :, :], I["w2"].rearrange("(k p) e n -> p k e n", p=HH)).then_inc(S["const_in"], 16)
            e.dma_start(gw[:, :, :], I["gate"].rearrange("(k p) n -> p k n", p=P)).then_inc(S["const_in"], 16)
            e.dma_start(ebias[:, :], on_all_partitions(I["expert_bias"])).then_inc(S["const_in"], 16)
            e.dma_start(iota[:, :], on_all_partitions(I["c_iota"])).then_inc(S["const_in"], 16)
            e.dma_start(ident[:, :], I["c_ident"]).then_inc(S["const_in"], 16)
            e.dma_start(row[:, :, :], I["c_row"]).then_inc(S["const_in"], 16)

            def load(t, p):
                at_least(e, S["a_mm"], t, X, -X)
                at_least(e, S["xin_ok"], t, E, -E)
                at_least(e, S["xr_ok"], t, 2, -2)
                e.dma_start(x1[:, p, :, :], tokens_of(W["x1"], t)).then_inc(S["x_in"][p], 16)
                e.dma_start(x1T[:, p, :, :], turned_of(W["x1T"], t)).then_inc(S["x_in"][p], 16)

            def store(t, p):
                at_least(e, S["ln_out"], t, 2, 2)
                e.dma_start(tokens_of(W["x2"], t), x2[:, p, :, :]).then_inc(S["stored"][p], 16)
            stream(e, load, store)
            for p in range(2):
                e.wait_ge(S["stored"][p], 16 * NC // 2)

        @block.gpsimd
        def _(e):
            e.memset(mhalf[:, :], -0.5).then_inc(S["prep"], 1)
            e.wait_ge(S["prep"], 1)
            two_step_loop(e, lambda t, p: norm_pool(e, S, N, t, mhalf), NC)

        @block.tensor
        def _(e):
            e.wait_ge(S["const_in"], 16 * 8)

            def gate(t, p):
                at_least(e, S["x_in"][p], t - p, 16, 32)
                at_least(e, S["wtT_ok"], t, 1, 0)
                for b in range(BATCH):
                    for k in range(KT):
                        m = e.matmul(g_ps[:, b * E:(b + 1) * E], x1T[:, p, k, b * L:(b + 1) * L], gw[:, k, :],
                                     start=(k == 0), stop=(k == KT - 1))
                m.then_inc(S["gate_mm"], 1)

            def up(t, p, x):
                n = t * X + x
                if x:
                    at_least(e, S["xin_ok"], t, E, x)
                at_least(e, S["h_ok"], t, X, x - 1)
                src = x1T[:, p, :, :] if x == 0 else xin[:, x % 2, :, :]
                for w, out, done in ((w1, a_ps, "a_mm"), (w3, b_ps, "b_mm")):
                    for hh in range(2):
                        for k in range(KT):
                            m = e.matmul(out[x % 2][0:HH, hh * CT:(hh + 1) * CT], w[:, k, x, hh * HH:(hh + 1) * HH], src[:, k, :],
                                         start=(k == 0), stop=(k == KT - 1))
                    m.then_inc(S[done], 1)

            def down(t, x):
                at_least(e, S["h_ok"], t, X, x + 1)
                if x == 0:
                    at_least(e, S["xr_ok"], t, 2, 0)
                for b in range(BATCH):
                    for hh in range(2):
                        m = e.matmul(o_ps[b][:, 0:DM], h[:, x % 2, hh, b * L:(b + 1) * L], w2[:, hh, x, :],
                                     start=(x == 0 and hh == 0), stop=(x == E and hh == 1))
                m.then_inc(S["o_mm"], 1)

            def scores(t, x):
                at_least(e, S["xin_ok"], t, E, x - 1)
                e.matmul(s_ps[:, 0:CT], row[:, x - 1, :], wtT[:, :], start=True, stop=True).then_inc(S["sbc_mm"], 1)

            def step(t, p, last=False):
                if not (isinstance(t, int) and t == 0):
                    at_least(e, S["h_ok"], t, X, 0)
                up(t, p, 0)
                at_least(e, S["wt_ok"], t, 2, 2)
                for b in range(BATCH):
                    m = e.transpose(g_ps[0:E, 128 + b * L:128 + (b + 1) * L], wt[:, b, :], ident[:, :])
                m.then_inc(S["wtT_mm"], 1)
                down(t, 0)
                at_least(e, S["wtT_ok"], t, 1, 1)
                scores(t, 1)
                for x in range(1, X):
                    up(t, p, x)
                    if x < E:
                        scores(t, x + 1)
                    elif not last:
                        gate(t + 1, 1 - p)
                    if x > 1:
                        down(t, x - 1)
                down(t, E)
            gate(0, 0)
            step(0, 0)
            step(1, 1)
            with e.Fori(1, NC // 2 - 1) as j:
                step(j * 2, 0)
                step(j * 2 + 1, 1)
            step(NC - 2, 0)
            step(NC - 1, 1, True)

        @block.scalar
        def _(e):
            def gate(t):
                at_least(e, S["gmax_ok"], t, 2, 2)
                at_least(e, S["score_ok"], t, 2, 0)
                for b in range(BATCH):
                    e.activation(gexp[:, b, :], gsh[:, b, :], ACT.Exp, accum_out=gsum[:, b:b + 1]).then_inc(S["gexp_ok"], 1)

            def step(t, p, last=False):
                for x in range(X):
                    at_least(e, S["a_mm"], t, X, x + 1)
                    at_least(e, S["h_ok"], t, X, x - 1)
                    if x == 0:
                        at_least(e, S["h_ok"], t, X, 0)
                    e.activation(sa[:, x % 2, :, :].rearrange("p n t -> p (n t)"), a_ps[x % 2][0:HH, :], ACT.Silu).then_inc(S["silu_ok"], 1)
                    if x == 0:
                        at_least(e, S["wtT_mm"], t, 1, 1)
                        at_least(e, S["sbc_mm"], t, E, 0)
                        e.activation(wtT[:, :], g_ps[0:E, 128:128 + CT], ACT.Copy).then_inc(S["wtT_ok"], 1)
                if not last:
                    gate(t + 1)
            gate(0)
            step(0, 0)
            step(1, 1)
            with e.Fori(1, NC // 2 - 1) as j:
                step(j * 2, 0)
                step(j * 2 + 1, 1)
            step(NC - 2, 0)
            step(NC - 1, 1, True)

        @block.vector
        def _(e):
            e.wait_ge(S["const_in"], 16 * 8)

            def gate_a(t):
                at_least(e, S["gate_mm"], t, 1, 1)
                at_least(e, S["gmax_ok"], t, 2, 0)
                for b in range(BATCH):
                    e.tensor_reduce(gmax[:, b:b + 1], g_ps[:, b * E:(b + 1) * E], mybir.AxisListType.X, ALU.max).then_inc(S["gsum_ok"], 1)
                at_least(e, S["gsum_ok"], t, 4, 2)
                at_least(e, S["gexp_ok"], t, 2, 0)
                for b in range(BATCH):
                    e.tensor_scalar(gsh[:, b, :], g_ps[:, b * E:(b + 1) * E], gmax[:, b:b + 1], None, ALU.subtract).then_inc(S["gmax_ok"], 1)

            def gate_b(t):
                at_least(e, S["gexp_ok"], t, 2, 2)
                for b in range(BATCH):
                    e.reciprocal(grec[:, b:b + 1], gsum[:, b:b + 1]).then_inc(S["gsum_ok"], 1)
                at_least(e, S["gsum_ok"], t, 4, 4)
                for b in range(BATCH):
                    e.tensor_scalar(score[:, b, :], gexp[:, b, :], grec[:, b:b + 1], None, ALU.mult).then_inc(S["score_ok"], 1)
                at_least(e, S["score_ok"], t, 2, 2)
                for b in range(BATCH):
                    e.tensor_tensor(sbias[:, b, :], score[:, b, :], ebias[:, :], ALU.add).then_inc(S["sb_ok"], 1)
                at_least(e, S["sb_ok"], t, 2, 2, S["const_in"])
                for b in range(BATCH):
                    e.max(top[:, b, :], sbias[:, b, :]).then_inc(S["top_ok"], 1)
                at_least(e, S["top_ok"], t, 2, 2, S["const_in"])
                for b in range(BATCH):
                    e.max_index(topi[:, b, :], top[:, b, :], sbias[:, b, :]).then_inc(S["topi_ok"], 1)
                at_least(e, S["topi_ok"], t, 2, 2)
                e.tensor_copy(topf[:, :, :], topi[:, :, :]).then_inc(S["topf_ok"], 1)
                at_least(e, S["topf_ok"], t, 1, 1)
                for b in range(BATCH):
                    for n in range(2):
                        e.tensor_scalar(eq[:, b, n, :], iota[:, :], topf[:, b, n:n + 1], None, ALU.is_equal).then_inc(S["eq_ok"], 1)
                at_least(e, S["eq_ok"], t, 6, 4)
                for b in range(BATCH):
                    e.tensor_tensor(eq[:, b, 0, :], eq[:, b, 0, :], eq[:, b, 1, :], ALU.add).then_inc(S["eq_ok"], 1)
                at_least(e, S["eq_ok"], t, 6, 6)
                at_least(e, S["wtT_mm"], t, 1, 0)
                for b in range(BATCH):
                    e.tensor_tensor(wt[:, b, :], eq[:, b, 0, :], score[:, b, :], ALU.mult).then_inc(S["wt_ok"], 1)

            def scaled(t, p, x):
                at_least(e, S["sbc_mm"], t, E, x)
                at_least(e, S["a_mm"], t, X, x - 1)
                at_least(e, S["b_mm"], t, X, x - 1)
                e.tensor_tensor(xin[:, x % 2, :, :], x1T[:, p, :, :], repeat(s_ps[:, 0:CT], KT), ALU.mult).then_inc(S["xin_ok"], 1)

            def gated(t, x):
                at_least(e, S["silu_ok"], t, X, x + 1)
                at_least(e, S["b_mm"], t, X, x + 1)
                at_least(e, S["o_mm"], t, X, x - 1)
                if x == 0:
                    at_least(e, S["o_mm"], t, X, 0)
                e.tensor_tensor(h[:, x % 2, :, :].rearrange("p n t -> p (n t)"), sa[:, x % 2, :, :].rearrange("p n t -> p (n t)"),
                                b_ps[x % 2][0:HH, :], ALU.mult).then_inc(S["h_ok"], 1)

            def finish(t, p):
                at_least(e, S["o_mm"], t, X, X)
                at_least(e, S["ln_out"], t, 2, 0)
                for b in range(BATCH):
                    e.tensor_tensor(xr[:, b, :], o_ps[b][:, 0:DM], x1[:, p, b, :], ALU.add).then_inc(S["xr_ok"], 1)
                at_least(e, S["xr_ok"], t, 2, 2)

                def free():
                    if not (isinstance(t, int) and t < 2):
                        at_least(e, S["stored"][p], t - p, 8, 0)
                norm_vector(e, S, N, t, xr, x2[:, p, :, :], free)

            def step(t, p, last=False):
                at_least(e, S["x_in"][p], t - p, 16, 32)
                gate_b(t)
                gated(t, 0)
                for x in range(1, X):
                    scaled(t, p, x)
                    if x > 1:
                        gated(t, x - 1)
                gated(t, E)
                if not last:
                    gate_a(t + 1)
                finish(t, p)
            gate_a(0)
            step(0, 0)
            step(1, 1)
            with e.Fori(1, NC // 2 - 1) as j:
                step(j * 2, 0)
                step(j * 2 + 1, 1)
            step(NC - 2, 0)
            step(NC - 1, 1, True)


def key_value_product(nc, held, I, W):
    with ExitStack() as ctx:
        F = Phase(nc, ctx, held, "p4", "const_in prep hn_tr hT_ok q_mm q_ok q_rot q_done k_mm v_mm kb_ok vb_ok k_rot kr_ok kk_ok kn_ok "
                  "kv_ok A_mm A_ok A_out " + " ".join(norm_names()), "x_in stored")
        S, sb, ps = F.S, F.sb, F.ps
        wq = sb("wq", [P, KT, 3 * P])
        wk = sb("wk", [P, KT, 3 * P])
        wv = sb("wv", [P, KT, DM])
        bq = sb("bq", [P, 3])
        bk, bv = sb("bk", [P, 3 * P]), sb("bv", [P, DM])
        lw, lb = sb("lw", [P, KT]), sb("lb", [P, KT])
        ident = sb("ident", [P, P])
        mhalf = sb("mhalf", [P, 2])
        x2 = sb("x2", [P, 2, BATCH, DM])
        ck = sb("ck", [P, 2, 2, P])
        cq = sb("cq", [P, 2, 2, L])
        hn = sb("hn", [P, BATCH, DM])
        hT = sb("hT", [P, KT, CT])
        q = sb("q", [P, 3, CT])
        qr = sb("qr", [P, 2, CT])
        qo = sb("qo", [P, 2, KT, CT])
        kb, vb = sb("kb", [P, BATCH, 3 * P]), sb("vb", [P, BATCH, DM])
        kt = sb("kt", [P, 2, BATCH, P])
        kr = sb("kr", [P, BATCH, DM])
        kk = sb("kk", [P, DM])
        kn, kni = sb("kn", [P, BATCH]), sb("kni", [P, BATCH])
        kv = sb("kv", [P, BATCH, DM])
        A = sb("A", [P, KT * BATCH])
        N = norm_tiles(sb)
        t_ps, A_ps = ps("t"), ps("A")
        q_ps, k_ps = [ps(f"q{n}") for n in range(2)], [ps(f"k{n}") for n in range(2)]
        v_ps = ps("v")
        block = ctx.enter_context(nc.Block())

        @block.sync
        def _(e):
            for dst, src in ((wq, I["w_q"]), (wk, I["w_k"]), (wv, I["w_v"])):
                e.dma_start(dst[:, :, :], src.rearrange("(k p) n -> p k n", p=P)).then_inc(S["const_in"], 16)
            e.dma_start(bq[:, :], I["b_q"]).then_inc(S["const_in"], 16)
            e.dma_start(bk[:, :], on_all_partitions(I["b_k"])).then_inc(S["const_in"], 16)
            e.dma_start(bv[:, :], on_all_partitions(I["b_v"])).then_inc(S["const_in"], 16)
            e.dma_start(lw[:, :], I["ln_w"]).then_inc(S["const_in"], 16)
            e.dma_start(lb[:, :], I["ln_b"]).then_inc(S["const_in"], 16)
            e.dma_start(ident[:, :], I["c_ident"]).then_inc(S["const_in"], 16)

            def load(t, p):
                at_least(e, S["ln_out"], t, 2, -2)
                at_least(e, S["q_rot"], t, 2, -2)
                at_least(e, S["k_rot"], t, 4, -4)
                e.dma_start(x2[:, p, :, :], tokens_of(W["x2"], t)).then_inc(S["x_in"][p], 16)
                e.dma_start(ck[:, p, :, :], I["c_rope_k"].rearrange("a (c l) d -> c l a d", l=L)[bass.ds(t, 1), :, :, :]
                            .rearrange("c l a d -> (c l) a d")).then_inc(S["x_in"][p], 16)
                e.dma_start(cq[:, p, :, :], I["c_rope_q"].rearrange("a p (c l) -> c p a l", l=L)[bass.ds(t, 1), :, :, :]
                            .rearrange("c p a l -> (c p) a l")).then_inc(S["x_in"][p], 16)

            def store(t, p):
                at_least(e, S["q_done"], t, 2, 2)
                e.dma_start(turned_of(W["q"], t), qo[:, p, :, :]).then_inc(S["stored"][p], 16)
            stream(e, load, store)
            for p in range(2):
                e.wait_ge(S["stored"][p], 16 * NC // 2)
            e.wait_ge(S["A_ok"], NC + 1)
            e.dma_start(W["A"], A[:, :]).then_inc(S["A_out"], 16)
            e.wait_ge(S["A_out"], 16)

        @block.gpsimd
        def _(e):
            e.memset(mhalf[:, :], -0.5).then_inc(S["prep"], 1)
            e.memset(A[:, :], 0.0).then_inc(S["A_ok"], 1)
            e.wait_ge(S["prep"], 1)

            def step(t, p):
                norm_pool(e, S, N, t, mhalf)
                at_least(e, S["kk_ok"], t, 2, 2)
                at_least(e, S["A_mm"], t, 1, 0)
                e.tensor_tensor(kni[:, :], kn[:, :], mhalf[:, :], ALU.pow).then_inc(S["kn_ok"], 1)
            two_step_loop(e, step, NC)

        @block.tensor
        def _(e):
            e.wait_ge(S["const_in"], 16 * 9)

            def step(t, p):
                at_least(e, S["ln_out"], t, 2, 2)
                at_least(e, S["hT_ok"], t, 2, 0)
                for k in range(KT):
                    for b in range(BATCH):
                        m = e.transpose(t_ps[:, (k * 2 + b) * P:(k * 2 + b + 1) * P], hn[:, b, k * P:(k + 1) * P], ident[:, :])
                m.then_inc(S["hn_tr"], 1)
                at_least(e, S["hT_ok"], t, 2, 2)
                at_least(e, S["kb_ok"], t, 2, 0)
                for b in range(BATCH):
                    for k in range(KT):
                        m = e.matmul(k_ps[b][:, 0:3 * P], hT[:, k, b * L:(b + 1) * L], wk[:, k, :], start=(k == 0), stop=(k == KT - 1))
                    m.then_inc(S["k_mm"], 1)
                at_least(e, S["vb_ok"], t, 2, 0)
                for b in range(BATCH):
                    for k in range(KT):
                        m = e.matmul(v_ps[:, b * DM:(b + 1) * DM], hT[:, k, b * L:(b + 1) * L], wv[:, k, :], start=(k == 0), stop=(k == KT - 1))
                m.then_inc(S["v_mm"], 1)
                at_least(e, S["q_ok"], t, 3, 0)
                for n in range(3):
                    for k in range(KT):
                        m = e.matmul(q_ps[n // 2][:, n % 2 * CT:(n % 2 + 1) * CT], wq[:, k, n * P:(n + 1) * P], hT[:, k, :],
                                     start=(k == 0), stop=(k == KT - 1))
                m.then_inc(S["q_mm"], 1)
                at_least(e, S["kn_ok"], t, 1, 1)
                at_least(e, S["kv_ok"], t, 2, 2)
                if isinstance(t, int) and t == 0:
                    e.wait_ge(S["A_ok"], 1)
                else:
                    at_least(e, S["A_ok"], t, 1, 1)
                for k in range(KT):
                    for b in range(BATCH):
                        m = e.matmul(A_ps[:, k * BATCH + b:k * BATCH + b + 1], kv[:, b, k * P:(k + 1) * P], kni[:, b:b + 1],
                                     start=True, stop=True)
                m.then_inc(S["A_mm"], 1)
            two_step_loop(e, step, NC)

        @block.scalar
        def _(e):
            e.wait_ge(S["const_in"], 16 * 9)

            def step(t, p):
                at_least(e, S["hn_tr"], t, 1, 1)
                at_least(e, S["q_mm"], t, 1, 0)
                for k in range(KT):
                    e.activation(hT[:, k, :], t_ps[:, k * CT:(k + 1) * CT], ACT.Identity, bias=lb[:, k:k + 1], scale=lw[:, k:k + 1]
                                 ).then_inc(S["hT_ok"], 1)
                at_least(e, S["q_mm"], t, 1, 1)
                at_least(e, S["q_rot"], t, 2, 0)
                if not (isinstance(t, int) and t < 2):
                    at_least(e, S["stored"][p], t - p, 8, 0)
                for n in range(3):
                    e.activation(q[:, n, :] if n < 2 else qo[:, p, 1, :], q_ps[n // 2][:, n % 2 * CT:(n % 2 + 1) * CT],
                                 ACT.Identity, bias=bq[:, n:n + 1]).then_inc(S["q_ok"] if n < 2 else S["q_ok"], 1)
                at_least(e, S["kr_ok"], t, 4, 4)
                at_least(e, S["kn_ok"], t, 1, 0)
                for b in range(BATCH):
                    at_least(e, S["kk_ok"], t, 2, b)
                    e.activation(kk[:, :], kr[:, b, :], ACT.Square, accum_out=kn[:, b:b + 1]).then_inc(S["kk_ok"], 1)
            two_step_loop(e, step, NC)

        @block.vector
        def _(e):
            e.wait_ge(S["const_in"], 16 * 9)

            def norm(t, p):
                at_least(e, S["x_in"][p], t - p, 24, 48)

                def free():
                    at_least(e, S["hn_tr"], t, 1, 0)
                norm_vector(e, S, N, t, x2[:, p, :, :], hn, free)

            def step(t, p, last=False):
                for b in range(BATCH):
                    at_least(e, S["k_mm"], t, 2, b + 1)
                    at_least(e, S["k_rot"], t, 4, 0)
                    at_least(e, S["kr_ok"], t, 4, 0)
                    e.tensor_tensor(kb[:, b, :], k_ps[b][:, 0:3 * P], bk[:, :], ALU.add).then_inc(S["kb_ok"], 1)
                at_least(e, S["v_mm"], t, 1, 1)
                at_least(e, S["kv_ok"], t, 2, 0)
                for b in range(BATCH):
                    e.tensor_tensor(vb[:, b, :], v_ps[:, b * DM:(b + 1) * DM], bv[:, :], ALU.add).then_inc(S["vb_ok"], 1)
                at_least(e, S["kb_ok"], t, 2, 2)
                for b in range(BATCH):
                    e.tensor_tensor(kt[:, 0, b, :], kb[:, b, 0:P], ck[:, p, 0, :], ALU.mult).then_inc(S["k_rot"], 1)
                    e.tensor_tensor(kt[:, 1, b, :], kb[:, b, P:2 * P], ck[:, p, 1, :], ALU.mult).then_inc(S["k_rot"], 1)
                at_least(e, S["k_rot"], t, 4, 4)
                at_least(e, S["kk_ok"], t, 2, 0)
                for b in range(BATCH):
                    e.tensor_tensor(kr[:, b, 0:P], kt[:, 0, b, :], kt[:, 1, b, :], ALU.add).then_inc(S["kr_ok"], 1)
                    e.tensor_copy(kr[:, b, P:DM], kb[:, b, 2 * P:3 * P]).then_inc(S["kr_ok"], 1)
                at_least(e, S["kr_ok"], t, 4, 4)
                at_least(e, S["vb_ok"], t, 2, 2)
                at_least(e, S["A_mm"], t, 1, 0)
                for b in range(BATCH):
                    e.tensor_tensor(kv[:, b, :], kr[:, b, :], vb[:, b, :], ALU.mult).then_inc(S["kv_ok"], 1)
                if not last:
                    norm(t + 1, 1 - p)
                at_least(e, S["q_ok"], t, 3, 3)
                at_least(e, S["q_done"], t, 2, 0)
                for n in range(2):
                    e.tensor_tensor(qr[:, n, :].rearrange("p (b l) -> p b l", b=BATCH), q[:, n, :].rearrange("p (b l) -> p b l", b=BATCH),
                                    repeat(cq[:, p, n, :], BATCH), ALU.mult).then_inc(S["q_rot"], 1)
                at_least(e, S["q_rot"], t, 2, 2)
                if not (isinstance(t, int) and t < 2):
                    at_least(e, S["stored"][p], t - p, 8, 0)
                e.tensor_tensor(qo[:, p, 0, :], qr[:, 0, :], qr[:, 1, :], ALU.add).then_inc(S["q_done"], 2)
                at_least(e, S["A_mm"], t, 1, 1)
                at_least(e, S["A_ok"], t, 1, 1)
                e.tensor_tensor(A[:, :], A[:, :], A_ps[:, 0:KT * BATCH], ALU.add).then_inc(S["A_ok"], 1)
            norm(0, 0)
            step(0, 0)
            step(1, 1)
            with e.Fori(1, NC // 2 - 1) as j:
                step(j * 2, 0)
                step(j * 2 + 1, 1)
            step(NC - 2, 0)
            step(NC - 1, 1, True)


def output_and_ffn(nc, held, I, W):
    HI = 1024
    NI = HI // P
    with ExitStack() as ctx:
        F = Phase(nc, ctx, held, "p5", "const_in prep deq WA_ok Y_mm s1_ok xr_ok tr_mm xt_ok g_mm u_mm silu_ok h_ok o_mm xs_ok "
                  + " ".join(norm_names()) + " " + " ".join("b" + n for n in norm_names()), "x_in stored")
        S, sb, ps = F.S, F.sb, F.ps
        S2 = {n: S["b" + n] for n in norm_names()}
        raw = sb("raw", [P, KT, HI], mybir.dt.int32)
        rawd = sb("rawd", [P, NI, DM], mybir.dt.int32)
        rawu = sb("rawu", [P, KT, HI], mybir.dt.int32)
        wg, wu, wd = sb("wg", [P, KT, HI]), sb("wu", [P, KT, HI]), sb("wd", [P, NI, DM])
        gs, us = sb("gs", [P, NI]), sb("us", [P, NI])
        ds = sb("ds", [P, DM])
        wo = sb("wo", [P, KT, DM])
        bo = sb("bo", [P, DM])
        A = sb("A", [P, KT * BATCH])
        WA = sb("WA", [P, BATCH, KT, DM])
        ident = sb("ident", [P, P])
        mhalf = sb("mhalf", [P, 2])
        q = sb("q", [P, 2, KT, CT])
        x2 = sb("x2", [P, 2, BATCH, DM])
        s1 = sb("s1", [P, BATCH, DM])
        xr = sb("xr", [P, BATCH, DM])
        x3 = sb("x3", [P, 2, BATCH, DM])
        x3T = sb("x3T", [P, KT, CT])
        sg = sb("sg", [P, 2, 2, CT])
        h = sb("h", [P, 2, 2, CT])
        xs = sb("xs", [P, BATCH, DM])
        x4 = sb("x4", [P, 2, BATCH, DM])
        N = norm_tiles(sb)
        N2 = norm_tiles(sb, 2)
        Yt_ps = ps("Y")
        t_ps = ps("t")
        g_ps, u_ps = [ps(f"g{n}") for n in range(2)], [ps(f"u{n}") for n in range(2)]
        o_ps = [ps(f"o{b}") for b in range(BATCH)]
        block = ctx.enter_context(nc.Block())
        NU = NI // 2

        @block.sync
        def _(e):
            e.dma_start(raw[:, :, :], I["gate_w"].rearrange("(k p) n -> p k n", p=P)).then_inc(S["const_in"], 16)
            e.dma_start(rawu[:, :, :], I["up_w"].rearrange("(k p) n -> p k n", p=P)).then_inc(S["const_in"], 16)
            e.dma_start(rawd[:, :, :], I["down_w"].rearrange("(k p) n -> p k n", p=P)).then_inc(S["const_in"], 16)
            e.dma_start(gs[:, :], I["gate_scale"]).then_inc(S["const_in"], 16)
            e.dma_start(us[:, :], I["up_scale"]).then_inc(S["const_in"], 16)
            e.dma_start(ds[:, :], on_all_partitions(I["down_scale"])).then_inc(S["const_in"], 16)
            e.dma_start(wo[:, :, :], I["w_o"].rearrange("(k p) n -> p k n", p=P)).then_inc(S["const_in"], 16)
            e.dma_start(bo[:, :], on_all_partitions(I["b_out"])).then_inc(S["const_in"], 16)
            e.dma_start(A[:, :], W["A"]).then_inc(S["const_in"], 16)
            e.dma_start(ident[:, :], I["c_ident"]).then_inc(S["const_in"], 16)

            def load(t, p):
                at_least(e, S["Y_mm"], t, 1, -1)
                at_least(e, S["s1_ok"], t, 1, -1)
                e.dma_start(q[:, p, :, :], turned_of(W["q"], t)).then_inc(S["x_in"][p], 16)
                e.dma_start(x2[:, p, :, :], tokens_of(W["x2"], t)).then_inc(S["x_in"][p], 16)

            def store(t, p):
                at_least(e, S["bln_out"], t, 2, 2)
                e.dma_start(W["out"].rearrange("b (c l) d -> c b l d", l=L)[bass.ds(t, 1), :, :, :].rearrange("c b l d -> (c l) b d"),
                            x4[:, p, :, :]).then_inc(S["stored"][p], 16)
            stream(e, load, store)
            for p in range(2):
                e.wait_ge(S["stored"][p], 16 * NC // 2)

        @block.gpsimd
        def _(e):
            e.memset(mhalf[:, :], -0.5).then_inc(S["prep"], 1)
            e.wait_ge(S["prep"], 1)

            def step(t, p):
                if not (isinstance(t, int) and t == 0):
                    norm_pool(e, S2, N2, t - 1, mhalf)
            norm_pool(e, S, N, 0, mhalf)

            def both(t, p):
                norm_pool(e, S, N, t + 1, mhalf)
                norm_pool(e, S2, N2, t, mhalf)
            both(0, 0)
            both(1, 1)
            with e.Fori(1, NC // 2 - 1) as j:
                both(j * 2, 0)
                both(j * 2 + 1, 1)
            both(NC - 2, 0)
            norm_pool(e, S2, N2, NC - 1, mhalf)

        @block.tensor
        def _(e):
            e.wait_ge(S["const_in"], 16 * 10)
            e.wait_ge(S["WA_ok"], BATCH)
            e.wait_ge(S["deq"], 3)

            def project(t, p):
                at_least(e, S["x_in"][p], t - p, 16, 32)
                at_least(e, S["xr_ok"], t, 2, 0)
                for b in range(BATCH):
                    for k in range(KT):
                        m = e.matmul(Yt_ps[:, b * DM:(b + 1) * DM], q[:, p, k, b * L:(b + 1) * L], WA[:, b, k, :],
                                     start=(k == 0), stop=(k == KT - 1))
                m.then_inc(S["Y_mm"], 1)

            def turn(t, p):
                at_least(e, S["ln_out"], t, 2, 2)
                at_least(e, S["xt_ok"], t, 1, 0)
                for k in range(KT):
                    for b in range(BATCH):
                        m = e.transpose(t_ps[:, (k * 2 + b) * P:(k * 2 + b + 1) * P], x3[:, p, b, k * P:(k + 1) * P], ident[:, :])
                m.then_inc(S["tr_mm"], 1)

            def up(t, n):
                at_least(e, S["h_ok"], t, 2 * NU, 2 * n - 2)
                for w, o, done in ((wg, g_ps, "g_mm"), (wu, u_ps, "u_mm")):
                    for i in range(2):
                        for k in range(KT):
                            m = e.matmul(o[n % 2][:, i * CT:(i + 1) * CT], w[:, k, (2 * n + i) * P:(2 * n + i + 1) * P], x3T[:, k, :],
                                         start=(k == 0), stop=(k == KT - 1))
                    m.then_inc(S[done], 1)

            def down(t, n):
                at_least(e, S["h_ok"], t, 2 * NU, 2 * n + 2)
                if n == 0:
                    at_least(e, S["xs_ok"], t, 2, 0)
                for b in range(BATCH):
                    for i in range(2):
                        m = e.matmul(o_ps[b][:, 0:DM], h[:, n % 2, i, b * L:(b + 1) * L], wd[:, 2 * n + i, :],
                                     start=(n == 0 and i == 0), stop=(n == NU - 1 and i == 1))
                m.then_inc(S["o_mm"], 1)

            def step(t, p, last=False):
                turn(t, p)
                at_least(e, S["xt_ok"], t, 1, 1)
                up(t, 0)
                if not last:
                    project(t + 1, 1 - p)
                for n in range(1, NU):
                    up(t, n)
                    down(t, n - 1)
                down(t, NU - 1)
            project(0, 0)
            step(0, 0)
            step(1, 1)
            with e.Fori(1, NC // 2 - 1) as j:
                step(j * 2, 0)
                step(j * 2 + 1, 1)
            step(NC - 2, 0)
            step(NC - 1, 1, True)

        @block.scalar
        def _(e):
            e.wait_ge(S["const_in"], 16 * 10)

            def step(t, p):
                at_least(e, S["tr_mm"], t, 1, 1)
                at_least(e, S["u_mm"], t, NU, 0)
                e.activation(x3T[:, :, :].rearrange("p k t -> p (k t)"), t_ps[:, :], ACT.Copy).then_inc(S["xt_ok"], 1)
                for n in range(NU):
                    at_least(e, S["g_mm"], t, NU, n + 1)
                    at_least(e, S["h_ok"], t, 2 * NU, 2 * n - 2)
                    for i in range(2):
                        e.activation(sg[:, n % 2, i, :], g_ps[n % 2][:, i * CT:(i + 1) * CT], ACT.Silu,
                                     scale=gs[:, 2 * n + i:2 * n + i + 1]).then_inc(S["silu_ok"], 1)
            two_step_loop(e, step, NC)

        @block.vector
        def _(e):
            e.wait_ge(S["const_in"], 16 * 10)
            e.tensor_scalar(wg[:, :, :], raw[:, :, :], -128.0, None, ALU.add).then_inc(S["deq"], 1)
            e.tensor_scalar(wu[:, :, :], rawu[:, :, :], -128.0, None, ALU.add).then_inc(S["deq"], 1)
            e.scalar_tensor_tensor(out=wd[:, :, :], in0=rawd[:, :, :], scalar=-128.0, in1=repeat(ds[:, :], NI),
                                   op0=ALU.add, op1=ALU.mult).then_inc(S["deq"], 1)
            for b in range(BATCH):
                e.tensor_tensor(WA[:, b, :, :], wo[:, :, :],
                                spread(A[:, :].rearrange("p (k b) -> p k b", b=BATCH)[:, :, b], DM), ALU.mult).then_inc(S["WA_ok"], 1)

            def attention(t, p):
                at_least(e, S["x_in"][p], t - p, 16, 32)
                at_least(e, S["xr_ok"], t, 2, 0)
                e.scalar_tensor_tensor(out=s1[:, :, :], in0=x2[:, p, :, :], scalar=2.0, in1=repeat(bo[:, :], BATCH),
                                       op0=ALU.mult, op1=ALU.add).then_inc(S["s1_ok"], 1)
                at_least(e, S["Y_mm"], t, 1, 1)
                at_least(e, S["s1_ok"], t, 1, 1)
                at_least(e, S["ln_out"], t, 2, 0)
                for b in range(BATCH):
                    e.tensor_tensor(xr[:, b, :], s1[:, b, :], Yt_ps[:, b * DM:(b + 1) * DM], ALU.add).then_inc(S["xr_ok"], 1)
                at_least(e, S["xr_ok"], t, 2, 2)

                def free():
                    at_least(e, S["tr_mm"], t, 1, -1)
                    at_least(e, S["xs_ok"], t, 2, -2)
                norm_vector(e, S, N, t, xr, x3[:, p, :, :], free)

            def step(t, p, last=False):
                for n in range(NU):
                    at_least(e, S["u_mm"], t, NU, n + 1)
                    at_least(e, S["o_mm"], t, NU, n - 1)
                    for i in range(2):
                        at_least(e, S["silu_ok"], t, 2 * NU, 2 * n + i + 1)
                        e.scalar_tensor_tensor(out=h[:, n % 2, i, :], in0=u_ps[n % 2][:, i * CT:(i + 1) * CT],
                                               scalar=us[:, 2 * n + i:2 * n + i + 1], in1=sg[:, n % 2, i, :],
                                               op0=ALU.mult, op1=ALU.mult).then_inc(S["h_ok"], 1)
                if not last:
                    attention(t + 1, 1 - p)
                at_least(e, S["o_mm"], t, NU, NU)
                at_least(e, S["bln_out"], t, 2, 0)
                for b in range(BATCH):
                    e.tensor_tensor(xs[:, b, :], o_ps[b][:, 0:DM], x3[:, p, b, :], ALU.add).then_inc(S["xs_ok"], 1)
                at_least(e, S["xs_ok"], t, 2, 2)

                def free():
                    if not (isinstance(t, int) and t < 2):
                        at_least(e, S["stored"][p], t - p, 8, 0)
                norm_vector(e, S2, N2, t, xs, x4[:, p, :, :], free)
            attention(0, 0)
            step(0, 0)
            step(1, 1)
            with e.Fori(1, NC // 2 - 1) as j:
                step(j * 2, 0)
                step(j * 2 + 1, 1)
            step(NC - 2, 0)
            step(NC - 1, 1, True)


def build(nc, I, out):
    def scratch(name, shape, dt=F32):
        return nc.dram_tensor("scratch_" + name, shape, dt, kind="Internal").ap()
    W = {"bc": scratch("bc", (NC, 192, CT)), "phi": scratch("phi", (NC, NH, CT)),
         "pieces": scratch("pieces", (NC, 3, NH, CT), BF16), "negs": scratch("negs", (NC, 3, NH, CT), BF16),
         "dec": scratch("dec", (NC, P, NH)), "et": scratch("et", (NC, NB, P, CT)),
         "u": scratch("u", (NC, BATCH, L, DI)), "wu": scratch("wu", (NC, BATCH, L, DI)),
         "y": scratch("y", (NB * NC, P, CT)),
         "x1": scratch("x1", (NC, BATCH, L, DM)), "x1T": scratch("x1T", (NC, P, KT, CT)),
         "x2": scratch("x2", (NC, BATCH, L, DM)), "q": scratch("q", (NC, P, KT, CT)), "A": scratch("A", (P, KT * BATCH)),
         "out": out}
    for phases in ((project_and_decay, state_space_scan), (finish_mixer, mixture_of_experts), (key_value_product, output_and_ffn)):
        held = []
        for phase in phases:
            phase(nc, held, I, W)
        nc.clear_and_free_semaphores(held)
        nc.all_engine_barrier()


def laid_out(x):
    import numpy as np
    f = np.float32
    A = {}
    A["xT"] = np.ascontiguousarray(x["L0_attn_x"].reshape(TOK, DM).T)
    w = x["L0_attn_W_in"]
    o = 2 * DI
    A["w_bc"] = np.concatenate([w[:, o:o + NS:2], w[:, o + 1:o + NS:2], w[:, o + NS:o + 2 * NS:2], w[:, o + NS + 1:o + 2 * NS:2]], axis=1)
    A["w_dt"] = w[:, o + 2 * NS:]
    A["w_xs"] = w[:, DI:2 * DI]
    A["w_z"] = w[:, :DI]
    A["dt_bias"] = x["L0_attn_dt_bias"]
    A["A_log"] = x["L0_attn_A_log"]
    A["A_hm"] = x["L0_attn_A_log"].reshape(QA, 4).T.reshape(NH, 1)
    r = np.arange(P)
    A["c_ident"] = np.eye(P, dtype=f)
    A["c_triu"] = (r[:, None] <= r[None, :]).astype(f)
    A["c_tril"] = (r[:, None] > r[None, :]).astype(f)
    A["c_mask"] = np.where(r[:, None] > r[None, :], f(-1e30), f(0)).astype(f)
    A["c_blk"] = (r[:, None] // NS == r[None, :] // NS).astype(f)
    row_head = np.array([4 * q + h for h in range(4) for q in range(QA)])
    sel = np.zeros((NH, NB, P), f)
    for k in range(NB):
        sel[:, k, :] = row_head[:, None] == (HB * k + r // HD)[None, :]
    A["c_sel"] = sel
    ind = np.zeros((15, 4), f)
    for a in range(3):
        ind[a, :] = 1
        for h in range(4):
            ind[3 + 4 * a + h, h] = 1
    A["c_ind"] = ind
    A["c_turn"] = np.where(r % NS < NS // 2, f(TWO_PI), f(-TWO_PI)).astype(f).reshape(P, 1)
    fr = x["L0_attn_rope_freqs"]
    freq = np.zeros((NB, NH, NG, P), f)
    for i, h in enumerate(row_head):
        k, g, half = h // HB, h % HB // 2, h % 2
        for m in range(2):
            freq[k, i, g, half * NS + m * 32:half * NS + m * 32 + 32] = fr[h]
    A["freq"] = freq
    beta = np.zeros((NB, P, 4, NG), f)
    for n, b in enumerate((x["L0_attn_B_bias"], x["L0_attn_C_bias"])):
        for h in range(NH):
            k, g, half = h // HB, h % HB // 2, h % 2
            for m in range(2):
                beta[k, half * NS + m * 32:half * NS + m * 32 + 32, 2 * n, g] = b[h, m::2]
                beta[k, half * NS + m * 32:half * NS + m * 32 + 32, 2 * n + 1, g] = b[h, 1 - m::2]
    A["beta"] = beta
    A["x"] = x["L0_attn_x"]
    A["w_out"] = x["L0_attn_W_out"]
    A["d_rep"] = np.repeat(x["L0_attn_D_param"], HD)
    A["norm_w"] = x["L0_attn_norm_w"].reshape(NB, P).T
    for n, (w, s) in {"w1": ("w1", "sw1"), "w3": ("w3", "sw3")}.items():
        A[n] = np.concatenate([x["L0_ffn_" + s][:, None, :], x["L0_ffn_" + w].transpose(1, 0, 2)], axis=1)
    A["w2"] = np.concatenate([x["L0_ffn_sw2"][:, None, :], x["L0_ffn_w2"].transpose(1, 0, 2)], axis=1)
    A["gate"] = x["L0_ffn_gate_w"]
    A["expert_bias"] = x["L0_ffn_expert_bias"]
    A["c_iota"] = np.arange(8, dtype=f)
    A["c_row"] = np.repeat(np.eye(8, dtype=f)[:, :, None], P, axis=2)
    e, o, rest = np.arange(0, P, 2), np.arange(1, P, 2), np.arange(P, DM)
    cols = np.concatenate([e, o, o, e, rest])
    perm = np.concatenate([e, o, rest])
    w, b = x["L1_attn_W_in"], x["L1_attn_b_in"]
    A["w_q"], A["w_k"], A["w_v"] = w[:, cols], w[:, DM + cols], w[:, 2 * DM + perm]
    A["b_q"], A["b_k"], A["b_v"] = b[cols].reshape(3, P).T, b[DM + cols], b[2 * DM + perm]
    A["ln_w"], A["ln_b"] = x["L1_attn_ln_w"].reshape(KT, P).T, x["L1_attn_ln_b"].reshape(KT, P).T
    A["w_o"], A["b_out"] = x["L1_attn_W_out"][perm, :], x["L1_attn_b_out"]
    rot = DM // 2
    inv = (f(1.0) / np.power(f(10000.0), np.arange(0, rot, 2, dtype=f) / f(rot))).astype(f)
    ang = (np.arange(SEQ, dtype=f)[:, None] * inv[None, :]).astype(f)
    cos, sin = np.cos(ang), np.sin(ang)
    A["c_rope_k"] = np.stack([np.concatenate([cos, cos], 1), np.concatenate([-sin, sin], 1)]).astype(f)
    A["c_rope_q"] = A["c_rope_k"].transpose(0, 2, 1)
    A["gate_w"], A["up_w"], A["down_w"] = x["L1_ffn_gate_w"].T, x["L1_ffn_up_w"].T, x["L1_ffn_down_w"].T
    A["gate_scale"], A["up_scale"] = x["L1_ffn_gate_scale"].reshape(-1, P).T, x["L1_ffn_up_scale"].reshape(-1, P).T
    A["down_scale"] = x["L1_ffn_down_scale"]
    return {k: np.ascontiguousarray(a) for k, a in A.items()}


def kernel(**inputs):
    import numpy as _np
    import concourse.bacc as _bacc
    from concourse import mybir as _mybir
    from concourse.bass_utils import run_bass_kernel_spmd as _run

    nc = _bacc.Bacc("TRN2", target_bir_lowering=False, num_devices=1)
    arrays, I = {}, {}
    for name, a in laid_out({k: _np.asarray(v) for k, v in inputs.items()}).items():
        arrays[f"in_{name}"] = a
        I[name] = nc.dram_tensor(f"in_{name}", a.shape, _mybir.dt.from_np(a.dtype), kind="ExternalInput").ap()
    out = nc.dram_tensor("out_0", (BATCH, SEQ, DM), F32, kind="ExternalOutput").ap()
    build(nc, I, out)
    r = _run(nc, [arrays], core_ids=[0])
    return r.results[0]["out_0"]
```

```python
import math
from contextlib import ExitStack

import concourse.bass as bass
from concourse import mybir

F32 = mybir.dt.float32
F32R = mybir.dt.float32r
BF16 = mybir.dt.bfloat16
ALU = mybir.AluOpType
ACT = mybir.ActivationFunctionType

BATCH, SEQ, DM = 2, 2048, 256
TOK = BATCH * SEQ
P = 128
KT = DM // P
L = 128
NC = SEQ // L
CT = BATCH * L
NH, HD, NS = 64, 8, 64
DI = NH * HD
NB = 4
HB = NH // NB
NG = HB // 2
NQ = HB // 4
QA = NH // 4
MAGIC = 12582912.0
TWO_PI = 6.283185
EPS_RMS = 1e-6
EPS_LN = 1e-5


def at_least(e, sem, t, per, n, beside=None):
    v = t * per + n
    if isinstance(v, int) and v <= 0:
        return
    if beside is not None:
        e.wait_ge(beside, 1)
    e.wait_ge(sem, v)


def spread(ap, n):
    return bass.AP(tensor=ap.tensor, offset=ap.offset, ap=[list(z) for z in ap.ap] + [[0, n]])


def repeat(ap, n):
    pairs = [list(z) for z in ap.ap]
    return bass.AP(tensor=ap.tensor, offset=ap.offset, ap=[pairs[0], [0, n]] + pairs[1:])


def skew(ap, by):
    pairs = [list(z) for z in ap.ap]
    pairs[-2][0] += by
    return bass.AP(tensor=ap.tensor, offset=ap.offset, ap=pairs)


def on_all_partitions(ap):
    return bass.AP(tensor=ap.tensor, offset=ap.offset, ap=[[0, P]] + [list(z) for z in ap.ap])


def two_step_loop(e, body, steps, first=2, last=0):
    for t in range(first):
        body(t, t % 2)
    with e.Fori(first // 2, (steps - last) // 2) as j:
        body(j * 2, 0)
        body(j * 2 + 1, 1)
    for t in range(steps - last, steps):
        body(t, t % 2)


def project_and_decay(nc, held, I, W):
    with ExitStack() as ctx:
        def sb(name, shape, dt=F32):
            return ctx.enter_context(nc.sbuf_tensor("p0_" + name, shape, dt))

        def ps(name, n=512):
            return ctx.enter_context(nc.psum_tensor("p0_" + name, [P, n], F32))

        names = ("const_in prep x_in dt_mm bc_mm xs_mm ssq_mm cum_mm et_mm bc_sq rstd_ln rstd_ok v_ok vmax_ok vabs_ok vexp_ok "
                 "vln_ok dt_ok dtp_ok bcn_ok phi_ok carry_ok cumA_ok r1_ok piece_ok sufA_ok w_ok dec_ok decx_ok et_ok u_ok wu_ok "
                 "neg_ok pp_ok f_ok").split()
        S = {n: signal(nc, held, "p0_" + n) for n in names}
        x_in = [signal(nc, held, f"p0_x_in{p}") for p in range(2)]
        stored = [signal(nc, held, f"p0_stored{p}") for p in range(2)]

        xT = sb("xT", [P, 2, KT, BATCH, L])
        w_bc = sb("w_bc", [P, KT, P])
        w_dt = sb("w_dt", [P, KT, NH])
        w_xs = sb("w_xs", [P, KT, DI])
        bias = sb("bias", [P, NH])
        nA_bc = sb("nA_bc", [P, NH])
        nA_hm = sb("nA_hm", [NH, 1])
        triu = sb("triu", [P, P])
        tril = sb("tril", [P, P])
        sel = sb("sel", [NH, NB, P])
        ones = sb("ones", [P, P])
        blk = sb("blk", [P, P])
        epsr = sb("epsr", [P, 1])
        carry = sb("carry", [NH, 2, BATCH])
        sq = sb("sq", [P, CT])
        lnv = sb("lnv", [P, CT])
        rstd = sb("rstd", [P, CT])
        bcn = sb("bcn", [P, 2, CT])
        v = sb("v", [P, BATCH, NH])
        vmax = sb("vmax", [P, BATCH, NH])
        vabs = sb("vabs", [P, BATCH, NH])
        vexp = sb("vexp", [P, BATCH, NH])
        vln = sb("vln", [P, BATCH, NH])
        dt = sb("dt", [P, BATCH, NH])
        dtp = sb("dtp", [P, BATCH, NH])
        phi = sb("phi", [NH, CT])
        f1, f2 = sb("f1", [NH, CT]), sb("f2", [NH, CT])
        pp = sb("pp", [NH, 2, 3, CT], BF16)
        cumA = sb("cumA", [NH, CT])
        r1 = sb("r1", [NH, CT])
        r2 = sb("r2", [NH, CT])
        pieces = sb("pieces", [NH, 2, 3, CT], BF16)
        negs = sb("negs", [NH, 2, 3, CT], BF16)
        none = sb("none", [NH, CT], BF16)
        expo = sb("expo", [P, 2, BATCH, NH])
        w = sb("w", [P, BATCH, NH])
        dec = sb("dec", [P, BATCH, NH])
        decx = sb("decx", [P, 2, QA, BATCH, 2])
        zero = sb("zero", [P, NB, CT])
        et = sb("et", [P, 2, NB, CT])
        u = sb("u", [P, 2, BATCH, DI])
        wu = sb("wu", [P, 2, BATCH, DI])

        bc_ps = ps("bc_ps")
        dt_ps = ps("dt_ps")
        cum_ps = ps("cum_ps")
        ph_ps = ps("ph_ps")
        xs_ps = [ps(f"xs_ps{b}") for b in range(BATCH)]
        et_ps = [ps(f"et_ps{b}") for b in range(2)]
        NST = 11

        block = ctx.enter_context(nc.Block())

        @block.sync
        def _(e):
            for dst, src in ((w_bc, I["w_bc"]), (w_dt, I["w_dt"]), (w_xs, I["w_xs"])):
                e.dma_start(dst[:, :, :], src.rearrange("(k p) n -> p k n", p=P)).then_inc(S["const_in"], 16)
            e.dma_start(bias[:, :], on_all_partitions(I["dt_bias"])).then_inc(S["const_in"], 16)
            e.dma_start(nA_bc[:, :], on_all_partitions(I["A_log"])).then_inc(S["const_in"], 16)
            e.dma_start(nA_hm[:, :], I["A_hm"]).then_inc(S["const_in"], 16)
            e.dma_start(triu[:, :], I["c_triu"]).then_inc(S["const_in"], 16)
            e.dma_start(tril[:, :], I["c_tril"]).then_inc(S["const_in"], 16)
            e.dma_start(blk[:, :], I["c_blk"]).then_inc(S["const_in"], 16)
            e.dma_start(sel[:, :, :], I["c_sel"]).then_inc(S["const_in"], 16)

            def load(t, p):
                at_least(e, S["xs_mm"], t, 2, -2)
                for b in range(BATCH):
                    e.dma_start(xT[:, p, :, b, :],
                                I["xT"].rearrange("(k p) (b c l) -> p k b c l", p=P, b=BATCH, l=L)[:, :, b, bass.ds(t, 1), :]
                                .rearrange("p k c l -> p k (c l)")).then_inc(x_in[p], 16)

            def store(t, p):
                c = bass.ds(t, 1)
                def out(dst, src):
                    e.dma_start(dst, src).then_inc(stored[p], 16)
                at_least(e, S["bcn_ok"], t, 1, 1)
                bcd = W["bc"][c, :, :].rearrange("c r t -> (c r) t")
                out(bcd[0:64, :], bcn[0:64, p, :])
                out(bcd[64:96, :], bcn[0:32, p, :])
                out(bcd[96:160, :], bcn[64:128, p, :])
                out(bcd[160:192, :], bcn[64:96, p, :])
                at_least(e, S["neg_ok"], t, 1, 1, S["prep"])
                out(W["pieces"][c, :, :, :].rearrange("c a r t -> (c r) a t"), pieces[:, p, :, :])
                out(W["negs"][c, :, :, :].rearrange("c a r t -> (c r) a t"), negs[:, p, :, :])
                at_least(e, S["pp_ok"], t, 3, 3)
                out(W["phi"][c, :, :, :].rearrange("c a r t -> (c r) a t"), pp[:, p, :, :])
                at_least(e, S["decx_ok"], t, 2, 2)
                out(W["dec"].rearrange("(k c) r n -> c r k n", k=NB)[c, :, :, :].rearrange("c r k n -> (c r) k n"),
                    zero[:, :, 0:NG * BATCH] if isinstance(t, int) and t == 0
                    else decx[:, p, :, :, :].rearrange("p (k q) b e -> p k (q b e)", k=NB))
                at_least(e, S["et_ok"], t, 2, 2)
                out(W["et"].rearrange("(k c) r t -> c r k t", k=NB)[c, :, :, :].rearrange("c r k t -> (c r) k t"),
                    zero[:, :, :] if isinstance(t, int) and t == 0 else et[:, p, :, :])
                at_least(e, S["u_ok"], t, 2, 2)
                out(W["u"][c, :, :, :].rearrange("c b l d -> (c l) b d"), u[:, p, :, :])
                at_least(e, S["wu_ok"], t, 2, 2)
                out(W["wu"][c, :, :, :].rearrange("c b l d -> (c l) b d"), wu[:, p, :, :])

            e.wait_ge(S["prep"], 9)
            load(0, 0)
            load(1, 1)

            def step(t, p, more=True):
                store(t, p)
                if more:
                    load(t + 2, p)
            step(0, 0)
            step(1, 1)
            with e.Fori(1, NC // 2 - 1) as j:
                step(j * 2, 0)
                step(j * 2 + 1, 1)
            step(NC - 2, 0, False)
            step(NC - 1, 1, False)
            for p in range(2):
                e.wait_ge(stored[p], 16 * NST * NC // 2)

        @block.gpsimd
        def _(e):
            e.memset(ones[:, :], 1.0).then_inc(S["prep"], 1)
            e.memset(carry[:, :, :], 0.0).then_inc(S["prep"], 1)
            e.memset(epsr[:, :], EPS_RMS).then_inc(S["prep"], 1)
            e.memset(zero[:, :, :], 0.0).then_inc(S["prep"], 1)
            e.memset(none[:, :], 0.0).then_inc(S["prep"], 1)

            def step(t, p):
                if not (isinstance(t, int) and t < 2):
                    at_least(e, stored[p], (t - p) , 8 * NST, 0)
                at_least(e, S["piece_ok"], t, 3, 3)
                e.tensor_tensor(negs[:, p, :, :], repeat(none[:, :], 3), pieces[:, p, :, :], ALU.subtract).then_inc(S["neg_ok"], 1)
                at_least(e, S["u_ok"], t, 2, 2)
                at_least(e, S["w_ok"], t, 1, 1)
                for b in range(BATCH):
                    e.tensor_tensor(wu[:, p, b, :].rearrange("p (h d) -> p h d", d=HD),
                                    u[:, p, b, :].rearrange("p (h d) -> p h d", d=HD),
                                    spread(w[:, b, :], HD), ALU.mult).then_inc(S["wu_ok"], 1)
            two_step_loop(e, step, NC)

        @block.tensor
        def _(e):
            e.wait_ge(S["const_in"], 16 * 10)
            e.wait_ge(S["prep"], 9)

            def step(t, p):
                at_least(e, x_in[p], t - p, 16, 32)
                at_least(e, S["v_ok"], t, 1, 0)
                for b in range(BATCH):
                    for k in range(KT):
                        m = e.matmul(dt_ps[:, b * NH:(b + 1) * NH], xT[:, p, k, b, :], w_dt[:, k, :],
                                     start=(k == 0), stop=(k == KT - 1))
                m.then_inc(S["dt_mm"], 1)
                at_least(e, S["bcn_ok"], t, 1, 0)
                for k in range(KT):
                    m = e.matmul(bc_ps[:, 0:CT], w_bc[:, k, :], xT[:, p, k, :, :].rearrange("p b l -> p (b l)"),
                                 start=(k == 0), stop=(k == KT - 1))
                m.then_inc(S["bc_mm"], 1)
                for b in range(BATCH):
                    at_least(e, S["u_ok"], t, 2, b - 1)
                    for k in range(KT):
                        m = e.matmul(xs_ps[b][:, :], xT[:, p, k, b, :], w_xs[:, k, :],
                                     start=(k == 0), stop=(k == KT - 1))
                    m.then_inc(S["xs_mm"], 1)
                at_least(e, S["bc_sq"], t, 1, 1)
                e.matmul(bc_ps[:, CT:2 * CT], blk[:, :], sq[:, :], start=True, stop=True).then_inc(S["ssq_mm"], 1)
                at_least(e, S["dt_ok"], t, 1, 1)
                at_least(e, S["dtp_ok"], t, 2, 2)
                at_least(e, S["phi_ok"], t, 2, 0)
                at_least(e, S["carry_ok"], t, 1, 0)
                at_least(e, S["cumA_ok"], t, 1, 0)
                at_least(e, S["sufA_ok"], t, 2, 0)
                for b in range(BATCH):
                    e.matmul(ph_ps[0:NH, b * L:(b + 1) * L], dtp[:, b, :], triu[:, :], start=True, stop=True)
                    e.matmul(ph_ps[0:NH, CT + b * L:CT + (b + 1) * L], dt[:, b, :], triu[:, :], start=True, stop=True)
                e.matmul(cum_ps[:, 0:2 * NH], tril[:, :], dt[:, :, :].rearrange("p b h -> p (b h)"), start=True, stop=True)
                e.matmul(cum_ps[:, 2 * NH:4 * NH], ones[:, :], dt[:, :, :].rearrange("p b h -> p (b h)"),
                         start=True, stop=True).then_inc(S["cum_mm"], 1)
                at_least(e, S["cumA_ok"], t, 1, 1)
                at_least(e, S["et_ok"], t, 2, 0)
                for n in range(NB):
                    m = e.matmul(et_ps[n // 2][:, n % 2 * CT:(n % 2 + 1) * CT], sel[:, n, :], cumA[:, :],
                                 start=True, stop=True)
                m.then_inc(S["et_mm"], 1)
            two_step_loop(e, step, NC)

        @block.scalar
        def _(e):
            e.wait_ge(S["const_in"], 16 * 10)
            e.activation(nA_bc[:, :], nA_bc[:, :], ACT.Exp).then_inc(S["prep"], 1)
            e.activation(nA_hm[:, :], nA_hm[:, :], ACT.Exp).then_inc(S["prep"], 1)
            e.wait_ge(S["prep"], 9)

            def step(t, p):
                at_least(e, S["bc_mm"], t, 1, 1)
                e.activation(sq[:, :], bc_ps[:, 0:CT], ACT.Square).then_inc(S["bc_sq"], 1)
                at_least(e, S["v_ok"], t, 1, 1)
                e.activation(vabs[:, :, :], v[:, :, :], ACT.Abs).then_inc(S["vabs_ok"], 1)
                at_least(e, S["vabs_ok"], t, 1, 1)
                e.activation(vexp[:, :, :], vabs[:, :, :], ACT.Exp, scale=-1.0).then_inc(S["vexp_ok"], 1)
                at_least(e, S["vexp_ok"], t, 1, 1)
                at_least(e, S["dt_ok"], t, 1, 0)
                e.activation(vln[:, :, :], vexp[:, :, :], ACT.Ln, bias=1.0).then_inc(S["vln_ok"], 1)
                at_least(e, S["ssq_mm"], t, 1, 1)
                e.activation(lnv[:, :], bc_ps[:, CT:2 * CT], ACT.Ln, bias=epsr[:, :], scale=1.0 / NS).then_inc(S["rstd_ln"], 1)
                at_least(e, S["rstd_ln"], t, 1, 1)
                at_least(e, S["bcn_ok"], t, 1, 0)
                e.activation(rstd[:, :], lnv[:, :], ACT.Exp, scale=-0.5).then_inc(S["rstd_ok"], 1)
                at_least(e, S["sufA_ok"], t, 2, 2)
                at_least(e, S["wu_ok"], t, 2, 0)
                e.activation(w[:, :, :], expo[:, 0, :, :], ACT.Exp).then_inc(S["w_ok"], 1)
                at_least(e, S["decx_ok"], t, 2, 0)
                e.activation(dec[:, :, :], expo[:, 1, :, :], ACT.Exp).then_inc(S["dec_ok"], 1)
                at_least(e, S["et_mm"], t, 1, 1)
                if not (isinstance(t, int) and t < 2):
                    at_least(e, stored[p], (t - p), 8 * NST, 0)
                for n in range(2):
                    e.activation(et[:, p, 2 * n:2 * n + 2, :], et_ps[n][:, :].rearrange("p (k t) -> p k t", k=2),
                                 ACT.Exp, scale=1.0).then_inc(S["et_ok"], 1)
            two_step_loop(e, step, NC)

        @block.vector
        def _(e):
            e.wait_ge(S["prep"], 7)
            e.tensor_scalar(nA_bc[:, :], nA_bc[:, :], -1.0, None, ALU.mult).then_inc(S["prep"], 1)
            e.tensor_scalar(nA_hm[:, :], nA_hm[:, :], -1.0, None, ALU.mult).then_inc(S["prep"], 1)
            e.wait_ge(S["prep"], 9)

            def step(t, p):
                at_least(e, S["dt_mm"], t, 1, 1)
                at_least(e, S["vabs_ok"], t, 1, 0)
                e.tensor_tensor(v[:, :, :], dt_ps[:, 0:2 * NH].rearrange("p (b h) -> p b h", b=BATCH),
                                repeat(bias[:, :], BATCH), ALU.add).then_inc(S["v_ok"], 1)
                at_least(e, S["v_ok"], t, 1, 1)
                e.tensor_scalar(vmax[:, :, :], v[:, :, :], 0.0, None, ALU.max).then_inc(S["vmax_ok"], 1)
                at_least(e, S["vmax_ok"], t, 1, 1)
                at_least(e, S["vln_ok"], t, 1, 1)
                at_least(e, S["cum_mm"], t, 1, 0)
                at_least(e, S["u_ok"], t, 2, 0)
                for b in range(BATCH):
                    e.tensor_tensor(dtp[:, b, :].rearrange("p (h q) -> p q h", h=4), vmax[:, b, :].rearrange("p (q h) -> p q h", h=4),
                                    vln[:, b, :].rearrange("p (q h) -> p q h", h=4), ALU.add).then_inc(S["dtp_ok"], 1)
                e.tensor_tensor(dt[:, :, :], vmax[:, :, :], vln[:, :, :], ALU.add).then_inc(S["dt_ok"], 1)
                if not (isinstance(t, int) and t < 2):
                    at_least(e, stored[p], (t - p), 8 * NST, 0)
                at_least(e, S["rstd_ok"], t, 1, 1)
                e.tensor_tensor(bcn[:, p, :], bc_ps[:, 0:CT], rstd[:, :], ALU.mult).then_inc(S["bcn_ok"], 1)
                at_least(e, S["cum_mm"], t, 1, 1)
                at_least(e, S["carry_ok"], t, 1, 0)
                at_least(e, S["et_mm"], t, 1, 0)
                at_least(e, S["f_ok"], t, 2, 0)
                e.tensor_scalar(cumA[:, :], ph_ps[0:NH, 0:CT], nA_hm[:, :], None, ALU.mult).then_inc(S["cumA_ok"], 1)
                for b in range(BATCH):
                    e.tensor_scalar(phi[:, b * L:(b + 1) * L], ph_ps[0:NH, CT + b * L:CT + (b + 1) * L], carry[:, p, b:b + 1],
                                    1.0 / (2.0 * math.pi), ALU.add, ALU.mult).then_inc(S["phi_ok"], 1)
                e.tensor_tensor(carry[:, 1 - p, :], ph_ps[0:NH, CT:2 * CT].rearrange("p (b l) -> p b l", b=BATCH)[:, :, L - 1],
                                carry[:, p, :], ALU.add).then_inc(S["carry_ok"], 1)
                at_least(e, S["cumA_ok"], t, 1, 1)
                e.tensor_copy(pieces[:, p, 0, :], cumA[:, :]).then_inc(S["piece_ok"], 1)
                at_least(e, S["piece_ok"], t, 3, 1)
                e.tensor_tensor(r1[:, :], cumA[:, :], pieces[:, p, 0, :], ALU.subtract).then_inc(S["r1_ok"], 1)
                at_least(e, S["r1_ok"], t, 2, 1)
                e.tensor_copy(pieces[:, p, 1, :], r1[:, :]).then_inc(S["piece_ok"], 1)
                at_least(e, S["piece_ok"], t, 3, 2)
                e.tensor_tensor(r2[:, :], r1[:, :], pieces[:, p, 1, :], ALU.subtract).then_inc(S["r1_ok"], 1)
                at_least(e, S["r1_ok"], t, 2, 2)
                e.tensor_copy(pieces[:, p, 2, :], r2[:, :]).then_inc(S["piece_ok"], 1)
                at_least(e, S["phi_ok"], t, 2, 2)
                e.tensor_copy(pp[:, p, 0, :], phi[:, :]).then_inc(S["pp_ok"], 1)
                at_least(e, S["pp_ok"], t, 3, 1)
                e.tensor_tensor(f1[:, :], phi[:, :], pp[:, p, 0, :], ALU.subtract).then_inc(S["f_ok"], 1)
                at_least(e, S["f_ok"], t, 2, 1)
                e.tensor_copy(pp[:, p, 1, :], f1[:, :]).then_inc(S["pp_ok"], 1)
                at_least(e, S["pp_ok"], t, 3, 2)
                e.tensor_tensor(f2[:, :], f1[:, :], pp[:, p, 1, :], ALU.subtract).then_inc(S["f_ok"], 1)
                at_least(e, S["f_ok"], t, 2, 2)
                e.tensor_copy(pp[:, p, 2, :], f2[:, :]).then_inc(S["pp_ok"], 1)
                at_least(e, S["w_ok"], t, 1, 0)
                at_least(e, S["dec_ok"], t, 1, 0)
                for n in range(2):
                    e.tensor_tensor(expo[:, n, :, :], cum_ps[:, n * 2 * NH:(n + 1) * 2 * NH].rearrange("p (b h) -> p b h", b=BATCH),
                                    repeat(nA_bc[:, :], BATCH), ALU.mult).then_inc(S["sufA_ok"], 1)
                for b in range(BATCH):
                    at_least(e, S["xs_mm"], t, 2, b + 1)
                    at_least(e, S["dt_ok"], t, 1, 1)
                    e.tensor_tensor(u[:, p, b, :].rearrange("p (h d) -> p h d", d=HD),
                                    xs_ps[b][:, :].rearrange("p (h d) -> p h d", d=HD),
                                    spread(dt[:, b, :], HD), ALU.mult).then_inc(S["u_ok"], 1)
                at_least(e, S["dec_ok"], t, 1, 1)
                for h in range(2):
                    e.tensor_copy(decx[h * 64:(h + 1) * 64, p, :, :, :],
                                  dec[h * 64:(h + 1) * 64, :, :].rearrange("p b (q e h) -> p q b e h", e=2, h=2)[:, :, :, :, h]
                                  ).then_inc(S["decx_ok"], 1)
            two_step_loop(e, step, NC)


def state_space_scan(nc, held, I, W):
    T = NB * NC
    with ExitStack() as ctx:
        def sb(name, shape, dt=F32):
            return ctx.enter_context(nc.sbuf_tensor("p1_" + name, shape, dt))

        def ps(name):
            return ctx.enter_context(nc.psum_tensor("p1_ps_" + name, [P, 512], F32))

        names = ("const_in fq freq_out prep zeroed ph_mm mg_ok rn_ok abs_ok sin_ok cos_ok prodC rotC prodB rotB tr_mm bt_ok sc_mm g_mm d_ok "
                 "m_ok yi_mm yx_mm ns_mm ustage st_dec st_ok yx_ok y_ok").split()
        S = {n: signal(nc, held, "p1_" + n) for n in names}

        def sem2(n):
            return [signal(nc, held, f"p1_{n}{p}") for p in range(2)]
        freq_in = [signal(nc, held, f"p1_freq_in{k}") for k in range(NB)]
        trig_in, rot_in, dec_in, y_out = sem2("trig_in"), sem2("rot_in"), sem2("dec_in"), sem2("y_out")

        ident = sb("ident", [P, P])
        identb = sb("identb", [P, P], BF16)
        maskf = sb("maskf", [P, P])
        mask4 = sb("mask4", [P, 4, P], BF16)
        ind = sb("ind", [15, 4])
        turn = sb("turn", [P, 1])
        quart = sb("quart", [P, 1])
        one = sb("one", [P, HD])
        phi = sb("phi", [P, 2, CT], BF16)
        fp = sb("fp", [P, 2, NG * P], BF16)
        freq = sb("freq", [P, NB, NG * P])
        fa = sb("fa", [P, 2, NG * P], BF16)
        fo = sb("fo", [P, NB, NG * P], BF16)
        less = sb("less", [P, 2])
        beta = sb("beta", [P, 2, 4, NG])
        bc = sb("bc", [P, 2, 4, CT])
        GR = sb("GR", [15, 2, 4, NQ * CT], BF16)
        GL = sb("GL", [15, 2, NQ * CT], BF16)
        u_in = sb("u_in", [P, 2, BATCH, HB * HD])
        wu = sb("wu", [P, 2, BATCH, HB * HD])
        dec = sb("dec", [P, 2, NG * BATCH])
        et = sb("et", [P, 2, CT])
        uexp = sb("uexp", [P, 2, BATCH, HB, 32])
        mg = sb("mg", [P, 2, 512])
        rn = sb("rn", [P, 2, 4, 512])
        ab = sb("ab", [P, 4, 512])
        sn = sb("sn", [P, 2, NG, CT])
        cs = sb("cs", [P, 2, NG, CT])
        pc = sb("pc", [P, 2, 2, CT])
        pb = sb("pb", [P, 2, 2, CT])
        CR = sb("CR", [P, NG, CT])
        BR = sb("BR", [P, NG, CT])
        BT = sb("BT", [P, 2, 4, P])
        D = sb("D", [P, 4, 512])
        M = sb("M", [P, 4, 512])
        ST = sb("ST", [P, NQ, BATCH, 2, 32])
        yx = sb("yx", [P, 2, CT])
        y = sb("y", [P, 2, CT])

        ph_ps, bt_ps, y_ps, ns_ps = (ps(n) for n in ("ph", "bt", "y", "ns"))
        yi_ps, yx_ps = y_ps[:, 0:CT], y_ps[:, CT:2 * CT]
        g_ps, sc_ps = ([ps(f"{n}{i}") for i in range(2)] for n in ("g", "sc"))
        block = ctx.enter_context(nc.Block())
        U = NQ * BATCH

        @block.sync
        def _(e):
            e.dma_start(ident[:, :], I["c_ident"]).then_inc(S["const_in"], 16)
            e.dma_start(maskf[:, :], I["c_mask"]).then_inc(S["const_in"], 16)
            e.dma_start(ind[:, :], I["c_ind"]).then_inc(S["const_in"], 16)
            e.dma_start(turn[:, :], I["c_turn"]).then_inc(S["const_in"], 16)
            e.dma_start(less[:, :], I["c_less"]).then_inc(S["const_in"], 16)
            for k in range(NB):
                e.dma_start(freq[:, k, :], I["freq"][k, :, :]).then_inc(freq_in[k], 16)
            for k in range(NB):
                e.wait_ge(S["fq"], 5 * k + 5)
                e.dma_start(W["freq"][k, :, :], fo[:, k, :]).then_inc(S["freq_out"], 16)
            e.wait_ge(S["freq_out"], 16 * NB)
            e.wait_ge(S["prep"], 5)

            def store(t, p):
                e.dma_start(W["y"][bass.ds(t, 1), :, :].rearrange("c r t -> (c r) t"), y[:, p, :]).then_inc(y_out[p], 16)

            def load_trig(k, c, t, p):
                at_least(e, S["ph_mm"], t, 4, -4)
                cc = bass.ds(c, 1)
                for a, r in enumerate((3, 3, 2)):
                    src = W["phi"].rearrange("c a (k h) t -> c a k h t", k=NB)[cc, a, :, :, :][:, bass.ds(k, 1), :, :]
                    src = src.rearrange("c k h t -> (c k h) t")
                    e.dma_start(phi[48 * a:48 * a + HB * r, p, :],
                                bass.AP(tensor=src.tensor, offset=src.offset, ap=[[0, r]] + [list(z) for z in src.ap])
                                ).then_inc(trig_in[p], 16)
                e.dma_start(fp[:, p, :], W["freq"][bass.ds(k, 1), :, :].rearrange("k r m -> (k r) m")).then_inc(trig_in[p], 16)

            def load_rest(k, c, t, p):
                kk, cc = bass.ds(k, 1), bass.ds(c, 1)
                at_least(e, S["rotB"], t, NG, -NG)
                at_least(e, S["rotC"], t, NG, -NG)
                for n, row in ((1, 32), (0, 0), (2, 96), (3, 128)):
                    for h in range(2):
                        e.dma_start(bc[h * 64:(h + 1) * 64, p, n, :],
                                    W["bc"][cc, row:row + 64, :].rearrange("c r t -> (c r) t")).then_inc(rot_in[p], 16)
                e.dma_start(beta[:, p, :, :], I["beta"][kk, :, :, :].rearrange("k p a g -> (k p) a g")).then_inc(rot_in[p], 16)
                at_least(e, S["g_mm"], t, U, -U, S["prep"])
                for a in range(3):
                    e.dma_start(GR[a:a + 1, p, :, :],
                                W["pieces"][cc, a, :, :].rearrange("c (h k q) t -> c k h (q t)", h=4, k=NB)[:, kk, :, :]
                                .rearrange("c k h n -> (c k) h n")).then_inc(rot_in[p], 16)
                    e.dma_start(GL[3 + 4 * a:7 + 4 * a, p, :],
                                W["negs"][cc, a, :, :].rearrange("c (h k q) t -> c k h (q t)", h=4, k=NB)[:, kk, :, :]
                                .rearrange("c k h n -> (c k h) n")).then_inc(rot_in[p], 16)
                at_least(e, S["ustage"], t, U, -U)
                at_least(e, S["ns_mm"], t, NQ, -NQ)
                e.dma_start(u_in[:, p, :, :], W["u"][cc, :, :, :].rearrange("c b l (k d) -> c k l b d", k=NB)[:, kk, :, :, :]
                            .rearrange("c k l b d -> (c k l) b d")).then_inc(rot_in[p], 16)
                e.dma_start(wu[:, p, :, :], W["wu"][cc, :, :, :].rearrange("c b l (k d) -> c k l b d", k=NB)[:, kk, :, :, :]
                            .rearrange("c k l b d -> (c k l) b d")).then_inc(rot_in[p], 16)

            def load_last(t, p):
                at_least(e, S["y_ok"], t, 1, -1)
                if not (isinstance(t, int) and t < 2):
                    store(t - 2, p)
                tt = bass.ds(t, 1)
                e.dma_start(dec[:, p, :], W["dec"][tt, :, :].rearrange("c p n -> (c p) n")).then_inc(dec_in[p], 16)
                e.dma_start(et[:, p, :], W["et"][tt, :, :].rearrange("c p n -> (c p) n")).then_inc(dec_in[p], 16)

            load_trig(0, 0, 0, 0)
            load_rest(0, 0, 0, 0)
            for c in range(1, 4):
                load_trig(0, c, c, c % 2)
                load_last(c - 1, (c - 1) % 2)
                load_rest(0, c, c, c % 2)
            with e.Fori(2, NC // 2) as j:
                for p in range(2):
                    load_trig(0, j * 2 + p, j * 2 + p, p)
                    load_last(j * 2 + p - 1, 1 - p)
                    load_rest(0, j * 2 + p, j * 2 + p, p)
            with e.Fori(1, NB) as k:
                with e.Fori(0, NC // 2) as j:
                    for p in range(2):
                        load_trig(k, j * 2 + p, k * NC + j * 2 + p, p)
                        load_last(k * NC + j * 2 + p - 1, 1 - p)
                        load_rest(k, j * 2 + p, k * NC + j * 2 + p, p)
            load_last(T - 1, 1)
            for p in range(2):
                at_least(e, S["y_ok"], T, 1, p - 1)
                store(T - 2 + p, p)
                e.wait_ge(y_out[p], 16 * T // 2)

        @block.gpsimd
        def _(e):
            e.memset(quart[:, :], math.pi / 2).then_inc(S["zeroed"], 1)
            e.memset(one[:, :], 1.0).then_inc(S["zeroed"], 1)
            e.memset(GL[:, :, :], 1.0).then_inc(S["prep"], 1)
            e.memset(uexp[:, :, :, :, :], 0.0).then_inc(S["zeroed"], 1)
            e.memset(ST[:, :, :, :, :], 0.0).then_inc(S["zeroed"], 1)
            e.wait_ge(S["zeroed"], 4)

            def stage_u(t, p, q, b):
                at_least(e, rot_in[p], t - p, 8 * 17, 16 * 17)
                at_least(e, S["yi_mm"], t, U, -U)
                e.tensor_tensor(skew(uexp[:, p, b, 4 * q:4 * q + 4, 0:HD], HD),
                                u_in[:, p, b, q * 32:(q + 1) * 32].rearrange("p (h d) -> p h d", d=HD),
                                repeat(one[:, :], 4), ALU.mult).then_inc(S["ustage"], 1)

            def step(t, p):
                for g in range(NG):
                    at_least(e, S["prodC"], t, 2 * NG, 2 * g + 2)
                    at_least(e, S["yx_mm"], t, U, g // 2 * 2 + 2 - U)
                    at_least(e, S["sc_mm"], t, U, g // 2 * 2 + 2 - U)
                    e.tensor_tensor(CR[:, g, :], pc[:, g % 2, 0, :], pc[:, g % 2, 1, :], ALU.add).then_inc(S["rotC"], 1)
                    at_least(e, S["prodB"], t, 2 * NG, 2 * g + 2)
                    at_least(e, S["tr_mm"], t, NG, g + 1 - NG)
                    e.tensor_tensor(BR[:, g, :], pb[:, g % 2, 0, :], pb[:, g % 2, 1, :], ALU.add).then_inc(S["rotB"], 1)
                    stage_u(t, p, g // 2, g % 2)
            two_step_loop(e, step, T)

        @block.tensor
        def _(e):
            e.wait_ge(S["prep"], 5)
            e.wait_ge(S["zeroed"], 4)
            e.wait_ge(S["const_in"], 80)

            def phases(t, p, n):
                if n == 0:
                    at_least(e, trig_in[p], t - p, 32, 64)
                at_least(e, S["rn_ok"], t, 4, n)
                for g in range(2):
                    m = e.matmul(ph_ps[:, g * CT:(g + 1) * CT], fp[:, p, (2 * n + g) * P:(2 * n + g + 1) * P], phi[:, p, :],
                                 start=True, stop=True)
                m.then_inc(S["ph_mm"], 1)

            def turned(t, q):
                for g in (2 * q, 2 * q + 1):
                    at_least(e, S["rotB"], t, NG, g + 1)
                    at_least(e, S["bt_ok"], t, NQ, q)
                    for b in range(BATCH):
                        m = e.transpose(bt_ps[:, (g % 2 * 2 + b) * P:(g % 2 * 2 + b + 1) * P],
                                        BR[:, g, b * L:(b + 1) * L], ident[:, :])
                    m.then_inc(S["tr_mm"], 1)

            def exponents(t, p, q, halves=(0, 1)):
                for half in halves:
                    n = 2 * q + half
                    at_least(e, rot_in[p], t - p, 8 * 17, 16 * 17)
                    at_least(e, S["d_ok"], t, U, n - 1)
                    e.matmul(g_ps[half][:, :], identb[:, :], mask4[:, :, :].rearrange("p h l -> p (h l)"), start=True, stop=False)
                    for b in range(BATCH):
                        cols = slice(q * CT + b * L, q * CT + b * L + L)
                        m = e.matmul(g_ps[half][:, :].rearrange("p (g b l) -> p g b l", g=2, b=BATCH)[:, :, b, :], GL[:, p, cols],
                                     GR[:, p, half:4:2, cols], start=False, stop=(b == 1))
                    m.then_inc(S["g_mm"], 1)

            def scores(t, q, halves=(0, 1)):
                for half in halves:
                    n = 2 * q + half
                    at_least(e, S["rotC"], t, NG, 2 * q + 2)
                    at_least(e, S["m_ok"], t, U, n - 1)
                    for g in range(2):
                        for b in range(BATCH):
                            m = e.matmul(sc_ps[half][:, (g * 2 + b) * L:(g * 2 + b + 1) * L],
                                         BR[half * 64:half * 64 + 64, 2 * q + g, b * L:(b + 1) * L],
                                         CR[half * 64:half * 64 + 64, 2 * q + g, b * L:(b + 1) * L], start=True, stop=True)
                    m.then_inc(S["sc_mm"], 1)

            def of_state(t, q):
                if q == 0:
                    at_least(e, S["st_ok"], t, 2, 0)
                    at_least(e, S["y_ok"], t, 1, 0)
                for b in range(BATCH):
                    for g in range(2):
                        m = e.matmul(yx_ps[32 * q:32 * q + 32, b * L:(b + 1) * L], ST[:, q, b, g, :],
                                     CR[:, 2 * q + g, b * L:(b + 1) * L], start=(g == 0), stop=(g == 1))
                    m.then_inc(S["yx_mm"], 1)

            def new_state(t, p, q):
                if q == 0:
                    at_least(e, S["st_ok"], t, 2, 0)
                at_least(e, S["bt_ok"], t, NQ, q + 1)
                for g in range(2):
                    for b in range(BATCH):
                        m = e.matmul(ns_ps[:, ((q * 2 + b) * 2 + g) * 16:((q * 2 + b) * 2 + g) * 16 + 16], BT[:, q % 2, g * 2 + b, :],
                                     wu[:, p, b, (2 * q + g) * 16:(2 * q + g) * 16 + 16], start=True, stop=True)
                m.then_inc(S["ns_mm"], 1)

            def of_chunk(t, p, q, batches=(0, 1)):
                for b in batches:
                    at_least(e, S["ustage"], t, U, 2 * q + b + 1)
                    at_least(e, S["m_ok"], t, U, 2 * q + 2)
                    for h in range(4):
                        m = e.matmul(yi_ps[32 * q:32 * q + 32, b * L:(b + 1) * L], uexp[:, p, b, 4 * q + h, :],
                                     M[:, 2 * (q % 2) + h % 2, (h // 2 * 2 + b) * L:(h // 2 * 2 + b + 1) * L], start=(h == 0), stop=(h == 3))
                    m.then_inc(S["yi_mm"], 1)

            def step(t, p, ahead=2):
                for q in range(NQ):
                    before = (t, p, q - 1) if q else (None if isinstance(t, int) and t == 0 else (t - 1, 1 - p, NQ - 1))
                    if before and q != 1:
                        of_state(before[0], before[2])
                        new_state(*before)
                    turned(t, q)
                    exponents(t, p, q)
                    if q < 2 and ahead:
                        phases(t + 1, 1 - p, q + 2)
                    elif q >= 2 and ahead == 2:
                        phases(t + 2, p, q - 2)
                    if q == 1:
                        of_state(t, 0)
                        new_state(t, p, 0)
                    scores(t, q)
                    if before:
                        of_chunk(*before)
            for n in range(4):
                phases(0, 0, n)
            for n in range(2):
                phases(1, 1, n)
            step(0, 0)
            step(1, 1)
            with e.Fori(1, T // 2 - 1) as j:
                step(j * 2, 0)
                step(j * 2 + 1, 1)
            step(T - 2, 0, 1)
            step(T - 1, 1, 0)
            of_state(T - 1, NQ - 1)
            new_state(T - 1, 1, NQ - 1)
            of_chunk(T - 1, 1, NQ - 1)

        @block.scalar
        def _(e):
            e.wait_ge(S["zeroed"], 4)
            e.wait_ge(S["const_in"], 80)

            def shifted(t, n):
                at_least(e, S["ph_mm"], t, 4, n + 1)
                at_least(e, S["rn_ok"], t, 4, n - 1)
                e.activation(mg[:, n % 2, :], ph_ps[:, :], ACT.Copy, bias=MAGIC).then_inc(S["mg_ok"], 1)

            def magnitude(t, p, n):
                at_least(e, S["rn_ok"], t, 4, n + 1)
                at_least(e, S["cos_ok"], t, 4, n - 3)
                e.activation(ab[:, n, :], rn[:, p, n, :], ACT.Abs).then_inc(S["abs_ok"], 1)

            def sines(t, p, n):
                at_least(e, S["prodB"], t, 2 * NG, -2 * NG)
                at_least(e, S["prodC"], t, 2 * NG, -2 * NG)
                e.activation(sn[:, p, 2 * n:2 * n + 2, :].rearrange("p g t -> p (g t)"), rn[:, p, n, :], ACT.Sin,
                             scale=turn[:, :]).then_inc(S["sin_ok"], 1)
                at_least(e, S["abs_ok"], t, 4, n + 1)
                e.activation(cs[:, p, 2 * n:2 * n + 2, :].rearrange("p g t -> p (g t)"), ab[:, n, :], ACT.Sin,
                             bias=quart[:, :], scale=-TWO_PI).then_inc(S["cos_ok"], 1)

            def step(t, p, ahead=2):
                for q in range(NQ):
                    for b in range(BATCH):
                        n = 2 * q + b
                        at_least(e, S["g_mm"], t, U, n + 1)
                        at_least(e, S["m_ok"], t, U, n - 3)
                        e.activation(D[:, n % 4, :], g_ps[b][:, :], ACT.Exp).then_inc(S["d_ok"], 1)
                    at_least(e, S["tr_mm"], t, NG, 2 * q + 2)
                    at_least(e, S["ns_mm"], t, NQ, q - 1)
                    e.activation(BT[:, q % 2, :, :].rearrange("p a n -> p (a n)"), bt_ps[:, :], ACT.Copy).then_inc(S["bt_ok"], 1)
                    if q < 2 and ahead:
                        shifted(t + 1, q + 2)
                    elif q >= 2 and ahead == 2:
                        shifted(t + 2, q - 2)
                    if q < 3 and ahead:
                        magnitude(t + 1, 1 - p, q + 1)
                    elif q == 3 and ahead == 2:
                        magnitude(t + 2, p, 0)
                    if q % 2 and ahead:
                        for n in (q - 1, q):
                            sines(t + 1, 1 - p, n)
            for n in range(4):
                shifted(0, n)
                magnitude(0, 0, n)
            for n in range(4):
                sines(0, 0, n)
            shifted(1, 0)
            magnitude(1, 1, 0)
            shifted(1, 1)
            step(0, 0)
            step(1, 1)
            with e.Fori(1, T // 2 - 1) as j:
                step(j * 2, 0)
                step(j * 2 + 1, 1)
            step(T - 2, 0, 1)
            step(T - 1, 1, 0)

        @block.vector
        def _(e):
            e.wait_ge(S["const_in"], 80)
            for k in range(NB):
                e.wait_ge(freq_in[k], 16)
                e.tensor_copy(fa[:, 0, :], freq[:, k, :]).then_inc(S["fq"], 1)
                e.wait_ge(S["fq"], 5 * k + 1)
                e.scalar_tensor_tensor(out=freq[:, k, :], in0=fa[:, 0, :], scalar=less[:, 0:1], in1=freq[:, k, :],
                                       op0=ALU.mult, op1=ALU.add).then_inc(S["fq"], 1)
                e.wait_ge(S["fq"], 5 * k + 2)
                e.tensor_copy(fa[:, 1, :], freq[:, k, :]).then_inc(S["fq"], 1)
                e.wait_ge(S["fq"], 5 * k + 3)
                e.scalar_tensor_tensor(out=freq[:, k, :], in0=fa[:, 1, :], scalar=less[:, 1:2], in1=freq[:, k, :],
                                       op0=ALU.mult, op1=ALU.add).then_inc(S["fq"], 1)
                e.wait_ge(S["fq"], 5 * k + 4)
                e.tensor_copy(fo[:, k, :], freq[:, k, :]).then_inc(S["fq"], 1)
            e.tensor_copy(GR[:, :, :, :].rearrange("p a h n -> p (a h) n")[:, 0:4, :], spread(ind[:, :], NQ * CT)
                          ).then_inc(S["prep"], 1)
            e.tensor_copy(GR[:, :, :, :].rearrange("p a h n -> p (a h) n")[:, 4:8, :], spread(ind[:, :], NQ * CT)
                          ).then_inc(S["prep"], 1)
            e.tensor_copy(mask4[:, :, :], repeat(maskf[:, :], 4)).then_inc(S["prep"], 1)
            e.tensor_copy(identb[:, :], ident[:, :]).then_inc(S["prep"], 1)
            e.wait_ge(S["zeroed"], 4)

            def trig(t, p, n):
                at_least(e, S["mg_ok"], t, 4, n + 1)
                at_least(e, S["abs_ok"], t, 4, n - 7)
                at_least(e, S["sin_ok"], t, 4, n - 7)
                e.scalar_tensor_tensor(out=rn[:, p, n, :], in0=mg[:, n % 2, :], scalar=MAGIC, in1=ph_ps[:, :],
                                       op0=ALU.subtract, op1=ALU.subtract).then_inc(S["rn_ok"], 1)

            def products(t, p, g):
                at_least(e, S["cos_ok"], t, 4, g // 2 + 1)
                at_least(e, S["sin_ok"], t, 4, g // 2 + 1)
                at_least(e, rot_in[p], t - p, 8 * 17, 16 * 17)
                at_least(e, S["rotC"], t, NG, g - 1)
                for n, tr in ((2, cs), (3, sn)):
                    e.scalar_tensor_tensor(out=pc[:, g % 2, n - 2, :], in0=bc[:, p, n, :], scalar=beta[:, p, n, g:g + 1],
                                           in1=tr[:, p, g, :], op0=ALU.add, op1=ALU.mult).then_inc(S["prodC"], 1)
                at_least(e, S["rotB"], t, NG, g - 1)
                for n, tr in ((0, cs), (1, sn)):
                    e.scalar_tensor_tensor(out=pb[:, g % 2, n, :], in0=bc[:, p, n, :], scalar=beta[:, p, n, g:g + 1],
                                           in1=tr[:, p, g, :], op0=ALU.add, op1=ALU.mult).then_inc(S["prodB"], 1)

            def decayed(t, n):
                at_least(e, S["sc_mm"], t, U, n + 1)
                at_least(e, S["d_ok"], t, U, n + 1)
                at_least(e, S["yi_mm"], t, U, n // 2 * 2 - 2)
                e.tensor_tensor(M[:, n % 4, :], sc_ps[n % 2][:, :], D[:, n % 4, :], ALU.mult).then_inc(S["m_ok"], 1)

            def new_state(t, p):
                at_least(e, dec_in[p], t - p, 16, 32)
                at_least(e, S["yx_mm"], t, U, U)
                for h in range(2):
                    r = slice(h * 64, h * 64 + 64)
                    e.tensor_tensor(state_blocks(r, h), state_blocks(r, h),
                                    spread(dec[r, p, :].rearrange("p (n e) -> p n e", e=2), HD), ALU.mult).then_inc(S["st_dec"], 1)
                at_least(e, S["ns_mm"], t, NQ, NQ)
                at_least(e, S["st_dec"], t, 2, 2)
                for h in range(2):
                    r = slice(h * 64, h * 64 + 64)
                    e.tensor_tensor(state_blocks(r, h), state_blocks(r, h),
                                    ns_ps[r, 0:NQ * BATCH * 32].rearrange("p (n e d) -> p n e d", e=2, d=16)[:, :, :, h * HD:(h + 1) * HD],
                                    ALU.add).then_inc(S["st_ok"], 1)

            def outputs(t, p):
                at_least(e, dec_in[p], t - p, 16, 32)
                at_least(e, S["yi_mm"], t, U, U)
                e.tensor_tensor(yx[:, p, :], yx_ps, et[:, p, :], ALU.mult).then_inc(S["yx_ok"], 1)
                at_least(e, S["yx_ok"], t, 1, 1)
                if not (isinstance(t, int) and t < 2):
                    at_least(e, y_out[p], t - p, 8, 0)
                e.tensor_tensor(y[:, p, :], yi_ps, yx[:, p, :], ALU.add).then_inc(S["y_ok"], 1)

            def state_blocks(r, h):
                return skew(ST[r, :, :, :, h * HD:(h + 1) * HD].rearrange("p q b e d -> p (q b) e d"), 16)

            def step(t, p, ahead=2):
                later = not (isinstance(t, int) and t == 0)
                for q in range(NQ):
                    products(t, p, 2 * q)
                    products(t, p, 2 * q + 1)
                    if q:
                        if q == 1 and later:
                            outputs(t - 1, 1 - p)
                        decayed(t, 2 * q - 2)
                        decayed(t, 2 * q - 1)
                    elif later:
                        decayed(t - 1, 2 * NQ - 2)
                        decayed(t - 1, 2 * NQ - 1)
                    if q < 3 and ahead:
                        trig(t + 1, 1 - p, q + 1)
                    elif q == 3 and ahead == 2:
                        trig(t + 2, p, 0)
                    if q == 0 and later:
                        new_state(t - 1, 1 - p)
            for n in range(4):
                trig(0, 0, n)
            trig(1, 1, 0)
            step(0, 0)
            step(1, 1)
            with e.Fori(1, T // 2 - 1) as j:
                step(j * 2, 0)
                step(j * 2 + 1, 1)
            step(T - 2, 0, 1)
            step(T - 1, 1, 0)
            decayed(T - 1, 2 * NQ - 2)
            decayed(T - 1, 2 * NQ - 1)
            new_state(T - 1, 1)
            outputs(T - 1, 1)


def norm_names():
    return "ln_stat ln_mv ln_var ln_rs ln_out".split()


def norm_tiles(sb, n=""):
    return dict(st=sb(f"ln{n}_st", [P, BATCH, 6]), mv=sb(f"ln{n}_mv", [P, BATCH, 2]), ve=sb(f"ln{n}_ve", [P, BATCH]),
                rs=sb(f"ln{n}_rs", [P, BATCH]), go=sb(f"ln{n}_go", [P, 1]))


def norm_vector(e, S, N, t, src, dst, free):
    at_least(e, S["ln_out"], t, 2, 0)
    for b in range(BATCH):
        e.bn_stats(N["st"][:, b, :], src[:, b, :]).then_inc(S["ln_stat"], 1)
    at_least(e, S["ln_stat"], t, 2, 2)
    e.memset(N["go"][:, :], 0.0).then_inc(S["ln_mv"], 1)
    for b in range(BATCH):
        e.bn_aggr(N["mv"][:, b, :], N["st"][:, b, :]).then_inc(S["ln_mv"], 1)
    at_least(e, S["ln_mv"], t, 3, 3)
    e.tensor_scalar(N["ve"][:, :], N["mv"][:, :, 1], EPS_LN, None, ALU.add).then_inc(S["ln_var"], 1)
    at_least(e, S["ln_rs"], t, 1, 1)
    free()
    for b in range(BATCH):
        e.tensor_scalar(dst[:, b, :], src[:, b, :], N["mv"][:, b, 0:1], N["rs"][:, b:b + 1], ALU.subtract, ALU.mult
                        ).then_inc(S["ln_out"], 1)


def norm_pool(e, S, N, t, mhalf):
    at_least(e, S["ln_var"], t, 1, 1)
    e.tensor_tensor(N["rs"][:, :], N["ve"][:, :], mhalf[:, 0:BATCH], ALU.pow).then_inc(S["ln_rs"], 1)


def tokens_of(ap, t):
    return ap[bass.ds(t, 1), :, :, :].rearrange("c b l d -> (c l) b d")


def turned_of(ap, t):
    return ap[bass.ds(t, 1), :, :, :].rearrange("c p k t -> (c p) k t")


def signal(nc, held, name):
    held.append(nc.alloc_semaphore(name=name))
    return held[-1]


class Phase:

    def __init__(self, nc, ctx, held, prefix, names, pairs):
        self.nc, self.ctx, self.prefix = nc, ctx, prefix
        self.S = {n: signal(nc, held, f"{prefix}_{n}") for n in names.split()}
        for n in pairs.split():
            self.S[n] = [signal(nc, held, f"{prefix}_{n}{p}") for p in range(2)]

    def sb(self, name, shape, dt=F32):
        return self.ctx.enter_context(self.nc.sbuf_tensor(f"{self.prefix}_{name}", shape, dt))

    def ps(self, name):
        return self.ctx.enter_context(self.nc.psum_tensor(f"{self.prefix}_ps_{name}", [P, 512], F32))


def finish_mixer(nc, held, I, W):
    with ExitStack() as ctx:
        F = Phase(nc, ctx, held, "p2", "const_in prep fold xs_mm z_mm silu_ok mix_ok g_ok g2_ok o_mm ms_ok rms_ok xr_ok tr_mm xt_ok "
                  + " ".join(norm_names()), "x_in stored")
        S, sb, ps = F.S, F.sb, F.ps
        w_xs, w_z = sb("w_xs", [P, KT, DI]), sb("w_z", [P, KT, DI])
        w_out = sb("w_out", [P, NB, DM])
        d_bc = sb("d_bc", [P, DI])
        nw = sb("nw", [P, NB])
        ident = sb("ident", [P, P])
        ones = sb("ones", [P, 1])
        mhalf = sb("mhalf", [P, 2])
        xT = sb("xT", [P, 2, KT, BATCH, L])
        x = sb("x", [P, 2, BATCH, DM])
        y = sb("y", [P, 2, NB, CT])
        sz = sb("sz", [P, NB, CT])
        mix = sb("mix", [P, NB, CT])
        g = sb("g", [P, NB, CT])
        g2 = sb("g2", [P, NB, CT])
        ms, rms = sb("ms", [P, BATCH]), sb("rms", [P, BATCH])
        xr = sb("xr", [P, BATCH, DM])
        x1 = sb("x1", [P, 2, BATCH, DM])
        x1T = sb("x1T", [P, 2, KT, CT])
        N = norm_tiles(sb)
        xs_ps, z_ps = [ps(f"xs{n}") for n in range(2)], [ps(f"z{n}") for n in range(2)]
        o_ps, q_ps, t_ps = ps("o"), ps("q"), ps("t")
        block = ctx.enter_context(nc.Block())

        @block.sync
        def _(e):
            for dst, src in ((w_xs, I["w_xs"]), (w_z, I["w_z"]), (w_out, I["w_out"])):
                e.dma_start(dst[:, :, :], src.rearrange("(k p) n -> p k n", p=P)).then_inc(S["const_in"], 16)
            e.dma_start(d_bc[:, :], on_all_partitions(I["d_rep"])).then_inc(S["const_in"], 16)
            e.dma_start(nw[:, :], I["norm_w"]).then_inc(S["const_in"], 16)
            e.dma_start(ident[:, :], I["c_ident"]).then_inc(S["const_in"], 16)

            def load(t, p):
                at_least(e, S["z_mm"], t, 1, -1)
                at_least(e, S["mix_ok"], t, 2, -2)
                at_least(e, S["xr_ok"], t, 2, -2)
                for b in range(BATCH):
                    e.dma_start(xT[:, p, :, b, :],
                                I["xT"].rearrange("(k p) (b c l) -> p k b c l", p=P, b=BATCH, l=L)[:, :, b, bass.ds(t, 1), :]
                                .rearrange("p k c l -> p k (c l)")).then_inc(S["x_in"][p], 16)
                e.dma_start(x[:, p, :, :], I["x"].rearrange("b (c l) d -> c b l d", l=L)[bass.ds(t, 1), :, :, :]
                            .rearrange("c b l d -> (c l) b d")).then_inc(S["x_in"][p], 16)
                e.dma_start(y[:, p, :, :], W["y"].rearrange("(k c) r t -> c r k t", k=NB)[bass.ds(t, 1), :, :, :]
                            .rearrange("c r k t -> (c r) k t")).then_inc(S["x_in"][p], 16)

            def store(t, p):
                at_least(e, S["ln_out"], t, 2, 2)
                e.dma_start(tokens_of(W["x1"], t), x1[:, p, :, :]).then_inc(S["stored"][p], 16)
                at_least(e, S["xt_ok"], t, 1, 1)
                e.dma_start(turned_of(W["x1T"], t), x1T[:, p, :, :]).then_inc(S["stored"][p], 16)
            stream(e, load, store)
            for p in range(2):
                e.wait_ge(S["stored"][p], 16 * 2 * NC // 2)

        @block.gpsimd
        def _(e):
            e.memset(ones[:, :], 1.0).then_inc(S["prep"], 1)
            e.memset(mhalf[:, :], -0.5).then_inc(S["prep"], 1)
            e.wait_ge(S["prep"], 2)

            def step(t, p):
                at_least(e, S["ms_ok"], t, 1, 1)
                e.tensor_tensor(rms[:, :], ms[:, :], mhalf[:, :], ALU.pow).then_inc(S["rms_ok"], 1)
                norm_pool(e, S, N, t, mhalf)
            two_step_loop(e, step, NC)

        @block.tensor
        def _(e):
            e.wait_ge(S["const_in"], 16 * 6)
            e.wait_ge(S["prep"], 2)
            e.wait_ge(S["fold"], 2)

            def turn(t, p):
                at_least(e, S["ln_out"], t, 2, 2)
                at_least(e, S["xt_ok"], t, 1, 0)
                for k in range(KT):
                    for b in range(BATCH):
                        m = e.transpose(t_ps[:, (k * 2 + b) * P:(k * 2 + b + 1) * P], x1[:, p, b, k * P:(k + 1) * P], ident[:, :])
                m.then_inc(S["tr_mm"], 1)

            def step(t, p):
                at_least(e, S["x_in"][p], t - p, 32, 64)
                at_least(e, S["mix_ok"], t, 2, 0)
                for n in range(NB):
                    for k in range(KT):
                        m = e.matmul(xs_ps[n // 2][:, n % 2 * CT:(n % 2 + 1) * CT], w_xs[:, k, n * P:(n + 1) * P],
                                     xT[:, p, k, :, :].rearrange("p b l -> p (b l)"), start=(k == 0), stop=(k == KT - 1))
                m.then_inc(S["xs_mm"], 1)
                at_least(e, S["silu_ok"], t, 2, 0)
                for n in range(NB):
                    for k in range(KT):
                        m = e.matmul(z_ps[n // 2][:, n % 2 * CT:(n % 2 + 1) * CT], w_z[:, k, n * P:(n + 1) * P],
                                     xT[:, p, k, :, :].rearrange("p b l -> p (b l)"), start=(k == 0), stop=(k == KT - 1))
                m.then_inc(S["z_mm"], 1)
                if not (isinstance(t, int) and t == 0):
                    turn(t - 1, 1 - p)
                at_least(e, S["g2_ok"], t, 2, 2)
                at_least(e, S["xr_ok"], t, 2, 0)
                for b in range(BATCH):
                    for n in range(NB):
                        m = e.matmul(o_ps[:, b * DM:(b + 1) * DM], g[:, n, b * L:(b + 1) * L], w_out[:, n, :],
                                     start=(n == 0), stop=(n == NB - 1))
                for b in range(BATCH):
                    for n in range(NB):
                        m = e.matmul(q_ps[:, b:b + 1], g2[:, n, b * L:(b + 1) * L], ones[:, :], start=(n == 0), stop=(n == NB - 1))
                m.then_inc(S["o_mm"], 1)
            two_step_loop(e, step, NC)
            turn(NC - 1, 1)

        @block.scalar
        def _(e):
            def copy_turned(t, p):
                at_least(e, S["tr_mm"], t, 1, 1)
                if not (isinstance(t, int) and t < 2):
                    at_least(e, S["stored"][p], t - p, 16, 0)
                e.activation(x1T[:, p, :, :].rearrange("p k t -> p (k t)"), t_ps[:, :], ACT.Copy).then_inc(S["xt_ok"], 1)

            def step(t, p):
                at_least(e, S["z_mm"], t, 1, 1)
                at_least(e, S["g_ok"], t, 2, 0)
                for n in range(2):
                    e.activation(sz[:, 2 * n:2 * n + 2, :].rearrange("p n t -> p (n t)"), z_ps[n][:, :], ACT.Silu).then_inc(S["silu_ok"], 1)
                if not (isinstance(t, int) and t == 0):
                    copy_turned(t - 1, 1 - p)
                at_least(e, S["o_mm"], t, 1, 0)
                for n in range(2):
                    at_least(e, S["g_ok"], t, 2, n + 1)
                    e.activation(g2[:, 2 * n:2 * n + 2, :], g[:, 2 * n:2 * n + 2, :], ACT.Square).then_inc(S["g2_ok"], 1)
            two_step_loop(e, step, NC)
            copy_turned(NC - 1, 1)

        @block.vector
        def _(e):
            e.wait_ge(S["const_in"], 16 * 6)
            e.tensor_tensor(w_xs[:, :, :], w_xs[:, :, :], repeat(d_bc[:, :], KT), ALU.mult).then_inc(S["fold"], 1)
            e.tensor_tensor(w_out[:, :, :], w_out[:, :, :], spread(nw[:, :], DM), ALU.mult).then_inc(S["fold"], 1)

            def step(t, p):
                at_least(e, S["x_in"][p], t - p, 32, 64)
                at_least(e, S["xs_mm"], t, 1, 1)
                at_least(e, S["g_ok"], t, 2, 0)
                for n in range(2):
                    e.scalar_tensor_tensor(out=mix[:, 2 * n:2 * n + 2, :].rearrange("p n t -> p (n t)"),
                                           in0=y[:, p, 2 * n:2 * n + 2, :].rearrange("p n t -> p (n t)"), scalar=NS ** -0.5,
                                           in1=xs_ps[n][:, :], op0=ALU.mult, op1=ALU.add).then_inc(S["mix_ok"], 1)
                at_least(e, S["mix_ok"], t, 2, 2)
                at_least(e, S["o_mm"], t, 1, 0)
                at_least(e, S["g2_ok"], t, 2, 0)
                for n in range(2):
                    at_least(e, S["silu_ok"], t, 2, n + 1)
                    e.tensor_tensor(g[:, 2 * n:2 * n + 2, :], mix[:, 2 * n:2 * n + 2, :], sz[:, 2 * n:2 * n + 2, :], ALU.mult
                                    ).then_inc(S["g_ok"], 1)
                at_least(e, S["o_mm"], t, 1, 1)
                at_least(e, S["rms_ok"], t, 1, 0)
                e.tensor_scalar(ms[:, :], q_ps[:, 0:BATCH], 1.0 / DI, EPS_RMS, ALU.mult, ALU.add).then_inc(S["ms_ok"], 1)
                at_least(e, S["rms_ok"], t, 1, 1)
                at_least(e, S["ln_out"], t, 2, 0)
                for b in range(BATCH):
                    e.scalar_tensor_tensor(out=xr[:, b, :], in0=o_ps[:, b * DM:(b + 1) * DM], scalar=rms[:, b:b + 1],
                                           in1=x[:, p, b, :], op0=ALU.mult, op1=ALU.add).then_inc(S["xr_ok"], 1)
                at_least(e, S["xr_ok"], t, 2, 2)

                def free():
                    if not (isinstance(t, int) and t < 2):
                        at_least(e, S["stored"][p], t - p, 16, 0)
                        at_least(e, S["tr_mm"], t, 1, -1)
                norm_vector(e, S, N, t, xr, x1[:, p, :, :], free)
            two_step_loop(e, step, NC)


def stream(e, load, store):
    load(0, 0)
    load(1, 1)
    for p in range(2):
        load(2 + p, p)
        store(p, p)
    with e.Fori(1, NC // 2 - 1) as j:
        for p in range(2):
            load(j * 2 + 2 + p, p)
            store(j * 2 + p, p)
    for p in range(2):
        store(NC - 2 + p, p)


def mixture_of_experts(nc, held, I, W):
    E, HID = 8, 224
    HH = HID // 2
    with ExitStack() as ctx:
        F = Phase(nc, ctx, held, "p3", "const_in prep gate_mm gmax_ok gexp_ok gsum_ok score_ok sb_ok top_ok topi_ok topf_ok eq_ok wt_ok "
                  "wtT_mm wtT_ok sbc_mm xin_ok a_mm b_mm silu_ok h_ok o_mm xr_ok tr_mm xt_ok " + " ".join(norm_names()), "x_in stored")
        S, sb, ps = F.S, F.sb, F.ps
        w1, w3 = sb("w1", [P, KT, E + 1, HID]), sb("w3", [P, KT, E + 1, HID])
        w2 = sb("w2", [HH, 2, E + 1, DM])
        gw = sb("gw", [P, KT, E])
        ebias = sb("ebias", [P, E])
        iota = sb("iota", [P, E])
        ident = sb("ident", [P, P])
        row = sb("row", [E, E, P])
        mhalf = sb("mhalf", [P, 2])
        none = sb("none", [P, CT * 2], BF16)
        x1 = sb("x1", [P, 2, BATCH, DM])
        x1T = sb("x1T", [P, 2, KT, CT])
        gmax, gsum, grec = sb("gmax", [P, BATCH]), sb("gsum", [P, BATCH]), sb("grec", [P, BATCH])
        gsh = sb("gsh", [P, BATCH, E])
        gexp, score, sbias = sb("gexp", [P, BATCH, E]), sb("score", [P, BATCH, E]), sb("sbias", [P, BATCH, E])
        top = sb("top", [P, BATCH, 8])
        topi = sb("topi", [P, BATCH, 8], mybir.dt.uint32)
        topf = sb("topf", [P, BATCH, 8])
        eq = sb("eq", [P, BATCH, 2, E])
        wt = sb("wt", [P, BATCH, E])
        wtT = sb("wtT", [E, CT])
        xin = sb("xin", [P, 2, KT, CT])
        sa = sb("sa", [HH, 2, 2, CT])
        h = sb("h", [HH, 2, 2, CT])
        xr = sb("xr", [P, BATCH, DM])
        x2 = sb("x2", [P, 2, BATCH, DM])
        x2T = sb("x2T", [P, 2, KT, CT])
        N = norm_tiles(sb)
        g_ps = ps("g")
        s_ps = [ps(f"s{n}") for n in range(2)]
        a_ps, b_ps = [ps(f"a{n}") for n in range(2)], [ps(f"b{n}") for n in range(2)]
        o_ps = ps("o")
        block = ctx.enter_context(nc.Block())
        X = E + 1

        @block.sync
        def _(e):
            e.dma_start(w1[:, :, :, :], I["w1"].rearrange("(k p) e n -> p k e n", p=P)).then_inc(S["const_in"], 16)
            e.dma_start(w3[:, :, :, :], I["w3"].rearrange("(k p) e n -> p k e n", p=P)).then_inc(S["const_in"], 16)
            e.dma_start(w2[:, :, :, :], I["w2"].rearrange("(k p) e n -> p k e n", p=HH)).then_inc(S["const_in"], 16)
            e.dma_start(gw[:, :, :], I["gate"].rearrange("(k p) n -> p k n", p=P)).then_inc(S["const_in"], 16)
            e.dma_start(ebias[:, :], on_all_partitions(I["expert_bias"])).then_inc(S["const_in"], 16)
            e.dma_start(iota[:, :], on_all_partitions(I["c_iota"])).then_inc(S["const_in"], 16)
            e.dma_start(ident[:, :], I["c_ident"]).then_inc(S["const_in"], 16)
            e.dma_start(row[:, :, :], I["c_row"]).then_inc(S["const_in"], 16)

            def load(t, p):
                at_least(e, S["xr_ok"], t, 1, -1)
                e.dma_start(x1[:, p, :, :], tokens_of(W["x1"], t)).then_inc(S["x_in"][p], 16)
                e.dma_start(x1T[:, p, :, :], turned_of(W["x1T"], t)).then_inc(S["x_in"][p], 16)

            def store(t, p):
                at_least(e, S["ln_out"], t, 2, 2)
                e.dma_start(tokens_of(W["x2"], t), x2[:, p, :, :]).then_inc(S["stored"][p], 16)
            stream(e, load, store)
            for p in range(2):
                e.wait_ge(S["stored"][p], 16 * NC // 2)

        @block.gpsimd
        def _(e):
            e.memset(mhalf[:, :], -0.5).then_inc(S["prep"], 1)
            e.memset(none[:, :], 0.0).then_inc(S["prep"], 1)
            e.wait_ge(S["prep"], 2)
            two_step_loop(e, lambda t, p: norm_pool(e, S, N, t, mhalf), NC)

        @block.tensor
        def _(e):
            e.wait_ge(S["const_in"], 16 * 8)
            e.wait_ge(S["prep"], 2)

            def gate(t, p):
                at_least(e, S["x_in"][p], t - p, 16, 32)
                at_least(e, S["gmax_ok"], t, 2, 0)
                for b in range(BATCH):
                    for k in range(KT):
                        m = e.matmul(g_ps[:, b * E:(b + 1) * E], x1T[:, p, k, b * L:(b + 1) * L], gw[:, k, :],
                                     start=(k == 0), stop=(k == KT - 1))
                m.then_inc(S["gate_mm"], 1)

            def turn_scores(t):
                at_least(e, S["wt_ok"], t, 2, 2)
                at_least(e, S["wtT_ok"], t, 1, 0)
                for b in range(BATCH):
                    m = e.transpose(g_ps[0:E, 128 + b * L:128 + (b + 1) * L], wt[:, b, :], ident[:, :])
                m.then_inc(S["wtT_mm"], 1)

            def scores(t, x):
                at_least(e, S["wtT_ok"], t, 1, 1)
                at_least(e, S["xin_ok"], t, E, x - 2)
                e.matmul(s_ps[x % 2][:, 0:CT], row[:, x - 1, :], wtT[:, :], start=True, stop=True
                         ).then_inc(S["sbc_mm"], 1)

            def up(t, p, x):
                if x:
                    at_least(e, S["xin_ok"], t, E, x)
                at_least(e, S["h_ok"], t, X, x - 1)
                src = x1T[:, p, :, :] if x == 0 else xin[:, x % 2, :, :]
                for w, out, done in ((w1, a_ps, "a_mm"), (w3, b_ps, "b_mm")):
                    for hh in range(2):
                        for k in range(KT):
                            m = e.matmul(out[(p + x) % 2][0:HH, hh * CT:(hh + 1) * CT], w[:, k, x, hh * HH:(hh + 1) * HH],
                                         src[:, k, :], start=(k == 0), stop=(k == KT - 1))
                    m.then_inc(S[done], 1)

            def down(t, p, x):
                at_least(e, S["h_ok"], t, X, x + 1)
                if x == 0:
                    at_least(e, S["xr_ok"], t, 1, 0)
                    e.matmul(o_ps[:, :], none[:, 0:P], none[:, :], start=True, stop=False)
                for b in range(BATCH):
                    for hh in range(2):
                        m = e.matmul(o_ps[:, b * DM:(b + 1) * DM], h[:, (p + x) % 2, hh, b * L:(b + 1) * L], w2[:, hh, x, :],
                                     start=False, stop=(x == E and hh == 1 and b == 1))
                m.then_inc(S["o_mm"], 1)

            def step(t, p, last=False):
                for x in range(X):
                    up(t, p, x)
                    if x + 2 < X:
                        scores(t, x + 2)
                    if x == 2 and not last:
                        gate(t + 1, 1 - p)
                    if x == 7 and not last:
                        turn_scores(t + 1)
                    if x == 8 and not last:
                        scores(t + 1, 1)
                    if x:
                        down(t, p, x - 1)
                    elif not (isinstance(t, int) and t == 0):
                        down(t - 1, 1 - p, E)
            gate(0, 0)
            turn_scores(0)
            scores(0, 1)
            step(0, 0)
            step(1, 1)
            with e.Fori(1, NC // 2 - 1) as j:
                step(j * 2, 0)
                step(j * 2 + 1, 1)
            step(NC - 2, 0)
            step(NC - 1, 1, True)
            down(NC - 1, 1, E)

        @block.scalar
        def _(e):
            def gate(t):
                at_least(e, S["gmax_ok"], t, 2, 2)
                at_least(e, S["score_ok"], t, 2, 0)
                for b in range(BATCH):
                    e.activation(gexp[:, b, :], gsh[:, b, :], ACT.Exp, accum_out=gsum[:, b:b + 1]).then_inc(S["gexp_ok"], 1)

            def copy_scores(t):
                at_least(e, S["wtT_mm"], t, 1, 1)
                at_least(e, S["sbc_mm"], t, E, 0)
                e.activation(wtT[:, :], g_ps[0:E, 128:128 + CT], ACT.Copy).then_inc(S["wtT_ok"], 1)

            def step(t, p, last=False):
                for x in range(X):
                    at_least(e, S["a_mm"], t, X, x + 1)
                    at_least(e, S["h_ok"], t, X, x - 1)
                    i = (p + x) % 2
                    e.activation(sa[:, i, :, :].rearrange("p n t -> p (n t)"), a_ps[i][0:HH, :], ACT.Silu).then_inc(S["silu_ok"], 1)
                    if x == 3 and not last:
                        gate(t + 1)
                    if x == 7 and not last:
                        copy_scores(t + 1)
            gate(0)
            copy_scores(0)
            step(0, 0)
            step(1, 1)
            with e.Fori(1, NC // 2 - 1) as j:
                step(j * 2, 0)
                step(j * 2 + 1, 1)
            step(NC - 2, 0)
            step(NC - 1, 1, True)

        @block.vector
        def _(e):
            e.wait_ge(S["const_in"], 16 * 8)

            def gate_a(t):
                at_least(e, S["gate_mm"], t, 1, 1)
                at_least(e, S["gmax_ok"], t, 2, 0)
                for b in range(BATCH):
                    e.tensor_reduce(gmax[:, b:b + 1], g_ps[:, b * E:(b + 1) * E], mybir.AxisListType.X, ALU.max).then_inc(S["gsum_ok"], 1)
                at_least(e, S["gsum_ok"], t, 4, 2)
                at_least(e, S["gexp_ok"], t, 2, 0)
                for b in range(BATCH):
                    e.tensor_scalar(gsh[:, b, :], g_ps[:, b * E:(b + 1) * E], gmax[:, b:b + 1], None, ALU.subtract).then_inc(S["gmax_ok"], 1)

            def gate_b(t):
                at_least(e, S["gexp_ok"], t, 2, 2)
                for b in range(BATCH):
                    e.reciprocal(grec[:, b:b + 1], gsum[:, b:b + 1]).then_inc(S["gsum_ok"], 1)
                at_least(e, S["gsum_ok"], t, 4, 4)
                for b in range(BATCH):
                    e.tensor_scalar(score[:, b, :], gexp[:, b, :], grec[:, b:b + 1], None, ALU.mult).then_inc(S["score_ok"], 1)
                at_least(e, S["score_ok"], t, 2, 2)
                for b in range(BATCH):
                    e.tensor_tensor(sbias[:, b, :], score[:, b, :], ebias[:, :], ALU.add).then_inc(S["sb_ok"], 1)
                at_least(e, S["sb_ok"], t, 2, 2, S["const_in"])
                for b in range(BATCH):
                    e.max(top[:, b, :], sbias[:, b, :]).then_inc(S["top_ok"], 1)
                at_least(e, S["top_ok"], t, 2, 2, S["const_in"])
                for b in range(BATCH):
                    e.max_index(topi[:, b, :], top[:, b, :], sbias[:, b, :]).then_inc(S["topi_ok"], 1)
                at_least(e, S["topi_ok"], t, 2, 2)
                e.tensor_copy(topf[:, :, :], topi[:, :, :]).then_inc(S["topf_ok"], 1)
                at_least(e, S["topf_ok"], t, 1, 1)
                for b in range(BATCH):
                    for n in range(2):
                        e.tensor_scalar(eq[:, b, n, :], iota[:, :], topf[:, b, n:n + 1], None, ALU.is_equal).then_inc(S["eq_ok"], 1)
                at_least(e, S["eq_ok"], t, 6, 4)
                for b in range(BATCH):
                    e.tensor_tensor(eq[:, b, 0, :], eq[:, b, 0, :], eq[:, b, 1, :], ALU.add).then_inc(S["eq_ok"], 1)
                at_least(e, S["eq_ok"], t, 6, 6)
                at_least(e, S["wtT_mm"], t, 1, 0)
                for b in range(BATCH):
                    e.tensor_tensor(wt[:, b, :], eq[:, b, 0, :], score[:, b, :], ALU.mult).then_inc(S["wt_ok"], 1)

            def scaled(t, p, x):
                at_least(e, S["sbc_mm"], t, E, x)
                at_least(e, S["a_mm"], t, X, x - 1)
                at_least(e, S["b_mm"], t, X, x - 1)
                e.tensor_tensor(xin[:, x % 2, :, :], x1T[:, p, :, :], repeat(s_ps[x % 2][:, 0:CT], KT), ALU.mult
                                ).then_inc(S["xin_ok"], 1)

            def gated(t, p, x):
                at_least(e, S["silu_ok"], t, X, x + 1)
                at_least(e, S["b_mm"], t, X, x + 1)
                at_least(e, S["o_mm"], t, X, x - 1)
                i = (p + x) % 2
                e.tensor_tensor(h[:, i, :, :].rearrange("p n t -> p (n t)"), sa[:, i, :, :].rearrange("p n t -> p (n t)"),
                                b_ps[i][0:HH, :], ALU.mult).then_inc(S["h_ok"], 1)

            def finish(t, p):
                at_least(e, S["o_mm"], t, X, X)
                at_least(e, S["ln_out"], t, 2, 0)
                e.tensor_tensor(xr[:, :, :], o_ps[:, :].rearrange("p (b d) -> p b d", b=BATCH), x1[:, p, :, :], ALU.add
                                ).then_inc(S["xr_ok"], 1)
                at_least(e, S["xr_ok"], t, 1, 1)

                def free():
                    if not (isinstance(t, int) and t < 2):
                        at_least(e, S["stored"][p], t - p, 8, 0)
                norm_vector(e, S, N, t, xr, x2[:, p, :, :], free)

            def step(t, p, last=False):
                at_least(e, S["x_in"][p], t - p, 16, 32)
                for x in range(X):
                    if x < E:
                        scaled(t, p, x + 1)
                    gated(t, p, x)
                    if x == 0 and not (isinstance(t, int) and t == 0):
                        finish(t - 1, 1 - p)
                    if x == 3 and not last:
                        gate_a(t + 1)
                    if x == 5 and not last:
                        gate_b(t + 1)
            gate_a(0)
            gate_b(0)
            step(0, 0)
            step(1, 1)
            with e.Fori(1, NC // 2 - 1) as j:
                step(j * 2, 0)
                step(j * 2 + 1, 1)
            step(NC - 2, 0)
            step(NC - 1, 1, True)
            finish(NC - 1, 1)


def key_value_product(nc, held, I, W):
    with ExitStack() as ctx:
        F = Phase(nc, ctx, held, "p4", "const_in prep hn_tr hT_ok q_mm q_ok q_rot q_done k_mm v_mm kb_ok vb_ok k_rot kr_ok kk_ok kn_ok "
                  "kv_ok A_mm A_ok A_out " + " ".join(norm_names()), "x_in stored")
        S, sb, ps = F.S, F.sb, F.ps
        wq = sb("wq", [P, KT, 3 * P])
        wk = sb("wk", [P, KT, 3 * P])
        wv = sb("wv", [P, KT, DM])
        bq = sb("bq", [P, 3])
        bk, bv = sb("bk", [P, 3 * P]), sb("bv", [P, DM])
        lw, lb = sb("lw", [P, KT]), sb("lb", [P, KT])
        ident = sb("ident", [P, P])
        mhalf = sb("mhalf", [P, 2])
        x2 = sb("x2", [P, 2, BATCH, DM])
        ck = sb("ck", [P, 2, 2, P])
        cq = sb("cq", [P, 2, 2, L])
        hn = sb("hn", [P, BATCH, DM])
        hT = sb("hT", [P, KT, CT])
        q = sb("q", [P, 3, CT])
        qr = sb("qr", [P, 2, CT])
        qo = sb("qo", [P, 2, KT, CT])
        kb, vb = sb("kb", [P, BATCH, 3 * P]), sb("vb", [P, BATCH, DM])
        kt = sb("kt", [P, 2, BATCH, P])
        kr = sb("kr", [P, BATCH, DM])
        kk = sb("kk", [P, DM])
        kn, kni = sb("kn", [P, BATCH]), sb("kni", [P, BATCH])
        kv = sb("kv", [P, BATCH, DM])
        A = sb("A", [P, KT * BATCH])
        N = norm_tiles(sb)
        t_ps, A_ps = ps("t"), ps("A")
        q_ps, k_ps = [ps(f"q{n}") for n in range(2)], [ps(f"k{n}") for n in range(2)]
        v_ps = ps("v")
        block = ctx.enter_context(nc.Block())

        @block.sync
        def _(e):
            for dst, src in ((wq, I["w_q"]), (wk, I["w_k"]), (wv, I["w_v"])):
                e.dma_start(dst[:, :, :], src.rearrange("(k p) n -> p k n", p=P)).then_inc(S["const_in"], 16)
            e.dma_start(bq[:, :], I["b_q"]).then_inc(S["const_in"], 16)
            e.dma_start(bk[:, :], on_all_partitions(I["b_k"])).then_inc(S["const_in"], 16)
            e.dma_start(bv[:, :], on_all_partitions(I["b_v"])).then_inc(S["const_in"], 16)
            e.dma_start(lw[:, :], I["ln_w"]).then_inc(S["const_in"], 16)
            e.dma_start(lb[:, :], I["ln_b"]).then_inc(S["const_in"], 16)
            e.dma_start(ident[:, :], I["c_ident"]).then_inc(S["const_in"], 16)

            def load(t, p):
                at_least(e, S["ln_out"], t, 2, -2)
                at_least(e, S["q_rot"], t, 2, -2)
                at_least(e, S["k_rot"], t, 4, -4)
                e.dma_start(x2[:, p, :, :], tokens_of(W["x2"], t)).then_inc(S["x_in"][p], 16)
                e.dma_start(ck[:, p, :, :], I["c_rope_k"].rearrange("a (c l) d -> c l a d", l=L)[bass.ds(t, 1), :, :, :]
                            .rearrange("c l a d -> (c l) a d")).then_inc(S["x_in"][p], 16)
                e.dma_start(cq[:, p, :, :], I["c_rope_q"].rearrange("a p (c l) -> c p a l", l=L)[bass.ds(t, 1), :, :, :]
                            .rearrange("c p a l -> (c p) a l")).then_inc(S["x_in"][p], 16)

            def store(t, p):
                at_least(e, S["q_done"], t, 2, 2)
                e.dma_start(turned_of(W["q"], t), qo[:, p, :, :]).then_inc(S["stored"][p], 16)
            stream(e, load, store)
            for p in range(2):
                e.wait_ge(S["stored"][p], 16 * NC // 2)
            e.wait_ge(S["A_ok"], NC + 1)
            e.dma_start(W["A"], A[:, :]).then_inc(S["A_out"], 16)
            e.wait_ge(S["A_out"], 16)

        @block.gpsimd
        def _(e):
            e.memset(mhalf[:, :], -0.5).then_inc(S["prep"], 1)
            e.memset(A[:, :], 0.0).then_inc(S["A_ok"], 1)
            e.wait_ge(S["prep"], 1)

            def step(t, p, last=False):
                if not last:
                    norm_pool(e, S, N, t + 1, mhalf)
                at_least(e, S["kk_ok"], t, 2, 2)
                at_least(e, S["A_mm"], t, 1, 0)
                e.tensor_tensor(kni[:, :], kn[:, :], mhalf[:, :], ALU.pow).then_inc(S["kn_ok"], 1)
            norm_pool(e, S, N, 0, mhalf)
            step(0, 0)
            step(1, 1)
            with e.Fori(1, NC // 2 - 1) as j:
                step(j * 2, 0)
                step(j * 2 + 1, 1)
            step(NC - 2, 0)
            step(NC - 1, 1, True)

        @block.tensor
        def _(e):
            e.wait_ge(S["const_in"], 16 * 9)

            def turn(t):
                at_least(e, S["ln_out"], t, 2, 2)
                at_least(e, S["hT_ok"], t, 2, 0)
                for k in range(KT):
                    for b in range(BATCH):
                        m = e.transpose(t_ps[:, (k * 2 + b) * P:(k * 2 + b + 1) * P], hn[:, b, k * P:(k + 1) * P], ident[:, :])
                m.then_inc(S["hn_tr"], 1)

            def sum_up(t):
                at_least(e, S["kn_ok"], t, 1, 1)
                at_least(e, S["kv_ok"], t, 2, 2)
                if isinstance(t, int) and t == 0:
                    e.wait_ge(S["A_ok"], 1)
                else:
                    at_least(e, S["A_ok"], t, 1, 1)
                for k in range(KT):
                    for b in range(BATCH):
                        m = e.matmul(A_ps[:, k * BATCH + b:k * BATCH + b + 1], kv[:, b, k * P:(k + 1) * P], kni[:, b:b + 1],
                                     start=True, stop=True)
                m.then_inc(S["A_mm"], 1)

            def step(t, p, last=False):
                at_least(e, S["hT_ok"], t, 2, 2)
                at_least(e, S["kb_ok"], t, 2, 0)
                for b in range(BATCH):
                    for k in range(KT):
                        m = e.matmul(k_ps[b][:, 0:3 * P], hT[:, k, b * L:(b + 1) * L], wk[:, k, :], start=(k == 0), stop=(k == KT - 1))
                    m.then_inc(S["k_mm"], 1)
                at_least(e, S["vb_ok"], t, 2, 0)
                for b in range(BATCH):
                    for k in range(KT):
                        m = e.matmul(v_ps[:, b * DM:(b + 1) * DM], hT[:, k, b * L:(b + 1) * L], wv[:, k, :], start=(k == 0), stop=(k == KT - 1))
                m.then_inc(S["v_mm"], 1)
                if not (isinstance(t, int) and t == 0):
                    sum_up(t - 1)
                at_least(e, S["q_ok"], t, 3, 0)
                for n in range(3):
                    for k in range(KT):
                        m = e.matmul(q_ps[n // 2][:, n % 2 * CT:(n % 2 + 1) * CT], wq[:, k, n * P:(n + 1) * P], hT[:, k, :],
                                     start=(k == 0), stop=(k == KT - 1))
                m.then_inc(S["q_mm"], 1)
                if not last:
                    turn(t + 1)
            turn(0)
            step(0, 0)
            step(1, 1)
            with e.Fori(1, NC // 2 - 1) as j:
                step(j * 2, 0)
                step(j * 2 + 1, 1)
            step(NC - 2, 0)
            step(NC - 1, 1, True)
            sum_up(NC - 1)

        @block.scalar
        def _(e):
            e.wait_ge(S["const_in"], 16 * 9)

            def turned(t):
                at_least(e, S["hn_tr"], t, 1, 1)
                at_least(e, S["q_mm"], t, 1, 0)
                for k in range(KT):
                    e.activation(hT[:, k, :], t_ps[:, k * CT:(k + 1) * CT], ACT.Identity, bias=lb[:, k:k + 1], scale=lw[:, k:k + 1]
                                 ).then_inc(S["hT_ok"], 1)

            def step(t, p, last=False):
                at_least(e, S["q_mm"], t, 1, 1)
                at_least(e, S["q_rot"], t, 2, 0)
                if not (isinstance(t, int) and t < 2):
                    at_least(e, S["stored"][p], t - p, 8, 0)
                for n in range(3):
                    e.activation(q[:, n, :] if n < 2 else qo[:, p, 1, :], q_ps[n // 2][:, n % 2 * CT:(n % 2 + 1) * CT],
                                 ACT.Identity, bias=bq[:, n:n + 1]).then_inc(S["q_ok"], 1)
                at_least(e, S["kr_ok"], t, 4, 4)
                at_least(e, S["kn_ok"], t, 1, 0)
                for b in range(BATCH):
                    at_least(e, S["kk_ok"], t, 2, b)
                    e.activation(kk[:, :], kr[:, b, :], ACT.Square, accum_out=kn[:, b:b + 1]).then_inc(S["kk_ok"], 1)
                if not last:
                    turned(t + 1)
            turned(0)
            step(0, 0)
            step(1, 1)
            with e.Fori(1, NC // 2 - 1) as j:
                step(j * 2, 0)
                step(j * 2 + 1, 1)
            step(NC - 2, 0)
            step(NC - 1, 1, True)

        @block.vector
        def _(e):
            e.wait_ge(S["const_in"], 16 * 9)

            def norm(t, p):
                at_least(e, S["x_in"][p], t - p, 24, 48)

                def free():
                    at_least(e, S["hn_tr"], t, 1, 0)
                norm_vector(e, S, N, t, x2[:, p, :, :], hn, free)

            def add_up(t):
                at_least(e, S["A_mm"], t, 1, 1)
                at_least(e, S["A_ok"], t, 1, 1)
                e.tensor_tensor(A[:, :], A[:, :], A_ps[:, 0:KT * BATCH], ALU.add).then_inc(S["A_ok"], 1)

            def step(t, p, last=False):
                if not last:
                    norm(t + 1, 1 - p)
                for b in range(BATCH):
                    at_least(e, S["k_mm"], t, 2, b + 1)
                    at_least(e, S["k_rot"], t, 4, 0)
                    at_least(e, S["kr_ok"], t, 4, 0)
                    e.tensor_tensor(kb[:, b, :], k_ps[b][:, 0:3 * P], bk[:, :], ALU.add).then_inc(S["kb_ok"], 1)
                at_least(e, S["v_mm"], t, 1, 1)
                at_least(e, S["kv_ok"], t, 2, 0)
                for b in range(BATCH):
                    e.tensor_tensor(vb[:, b, :], v_ps[:, b * DM:(b + 1) * DM], bv[:, :], ALU.add).then_inc(S["vb_ok"], 1)
                at_least(e, S["kb_ok"], t, 2, 2)
                for b in range(BATCH):
                    e.tensor_tensor(kt[:, 0, b, :], kb[:, b, 0:P], ck[:, p, 0, :], ALU.mult).then_inc(S["k_rot"], 1)
                    e.tensor_tensor(kt[:, 1, b, :], kb[:, b, P:2 * P], ck[:, p, 1, :], ALU.mult).then_inc(S["k_rot"], 1)
                at_least(e, S["k_rot"], t, 4, 4)
                at_least(e, S["kk_ok"], t, 2, 0)
                for b in range(BATCH):
                    e.tensor_tensor(kr[:, b, 0:P], kt[:, 0, b, :], kt[:, 1, b, :], ALU.add).then_inc(S["kr_ok"], 1)
                    e.tensor_copy(kr[:, b, P:DM], kb[:, b, 2 * P:3 * P]).then_inc(S["kr_ok"], 1)
                at_least(e, S["kr_ok"], t, 4, 4)
                at_least(e, S["vb_ok"], t, 2, 2)
                at_least(e, S["A_mm"], t, 1, 0)
                for b in range(BATCH):
                    e.tensor_tensor(kv[:, b, :], kr[:, b, :], vb[:, b, :], ALU.mult).then_inc(S["kv_ok"], 1)
                if not (isinstance(t, int) and t == 0):
                    add_up(t - 1)
                at_least(e, S["q_ok"], t, 3, 3)
                at_least(e, S["q_done"], t, 2, 0)
                for n in range(2):
                    e.tensor_tensor(qr[:, n, :].rearrange("p (b l) -> p b l", b=BATCH), q[:, n, :].rearrange("p (b l) -> p b l", b=BATCH),
                                    repeat(cq[:, p, n, :], BATCH), ALU.mult).then_inc(S["q_rot"], 1)
                at_least(e, S["q_rot"], t, 2, 2)
                if not (isinstance(t, int) and t < 2):
                    at_least(e, S["stored"][p], t - p, 8, 0)
                e.tensor_tensor(qo[:, p, 0, :], qr[:, 0, :], qr[:, 1, :], ALU.add).then_inc(S["q_done"], 2)
            norm(0, 0)
            step(0, 0)
            step(1, 1)
            with e.Fori(1, NC // 2 - 1) as j:
                step(j * 2, 0)
                step(j * 2 + 1, 1)
            step(NC - 2, 0)
            step(NC - 1, 1, True)
            add_up(NC - 1)


def output_and_ffn(nc, held, I, W):
    HI = 1024
    NI = HI // P
    NU = NI // 2
    with ExitStack() as ctx:
        F = Phase(nc, ctx, held, "p5", "const_in prep deq WA_ok Y_mm s1_ok xr_ok tr_mm xt_ok xh_ok xl_ok g_mm u_mm silu_ok h_ok hh_ok hl_ok "
                  "o_mm xm_ok xs_ok kept "
                  + " ".join(norm_names()) + " " + " ".join("b" + n for n in norm_names()), "x_in stored")
        S, sb, ps = F.S, F.sb, F.ps
        S2 = {n: S["b" + n] for n in norm_names()}
        raw = sb("raw", [P, KT, HI], mybir.dt.int32)
        rawd = sb("rawd", [P, NI, DM], mybir.dt.int32)
        rawu = sb("rawu", [P, KT, HI], mybir.dt.int32)
        wg, wu, wd = sb("wg", [P, KT, HI]), sb("wu", [P, KT, HI]), sb("wd", [P, NI, DM])
        gs, us = sb("gs", [P, NI]), sb("us", [P, NI])
        ds = sb("ds", [P, DM])
        wo = sb("wo", [P, KT, DM])
        bo = sb("bo", [P, DM])
        A = sb("A", [P, KT * BATCH])
        WA = sb("WA", [P, BATCH, KT, DM])
        ident = sb("ident", [P, P])
        mhalf = sb("mhalf", [P, 2])
        q = sb("q", [P, 2, KT, CT])
        x2 = sb("x2", [P, 2, BATCH, DM])
        s1 = sb("s1", [P, BATCH, DM])
        xr = sb("xr", [P, BATCH, DM])
        x3 = sb("x3", [P, 2, BATCH, DM])
        x3T = sb("x3T", [P, KT * CT])
        xh, xl = sb("xh", [P, 2, KT, CT]), sb("xl", [P, 2, KT, CT])
        sg = sb("sg", [P, 2, 2, CT])
        h, hh, hl = (sb(n, [P, NU, 2, CT]) for n in ("h", "hh", "hl"))
        xm = sb("xm", [P, BATCH, DM])
        xk = sb("xk", [P, 2, BATCH, DM])
        xs = sb("xs", [P, BATCH, DM])
        x4 = sb("x4", [P, 2, BATCH, DM])
        N = norm_tiles(sb)
        N2 = norm_tiles(sb, 2)
        Yt_ps = ps("Y")
        t_ps = ps("t")
        g_ps, u_ps = [ps(f"g{n}") for n in range(2)], [ps(f"u{n}") for n in range(2)]
        o_ps = [ps(f"o{b}") for b in range(BATCH)]
        block = ctx.enter_context(nc.Block())

        @block.sync
        def _(e):
            e.dma_start(raw[:, :, :], I["gate_w"].rearrange("(k p) n -> p k n", p=P)).then_inc(S["const_in"], 16)
            e.dma_start(rawu[:, :, :], I["up_w"].rearrange("(k p) n -> p k n", p=P)).then_inc(S["const_in"], 16)
            e.dma_start(rawd[:, :, :], I["down_w"].rearrange("(k p) n -> p k n", p=P)).then_inc(S["const_in"], 16)
            e.dma_start(gs[:, :], I["gate_scale"]).then_inc(S["const_in"], 16)
            e.dma_start(us[:, :], I["up_scale"]).then_inc(S["const_in"], 16)
            e.dma_start(ds[:, :], on_all_partitions(I["down_scale"])).then_inc(S["const_in"], 16)
            e.dma_start(wo[:, :, :], I["w_o"].rearrange("(k p) n -> p k n", p=P)).then_inc(S["const_in"], 16)
            e.dma_start(bo[:, :], on_all_partitions(I["b_out"])).then_inc(S["const_in"], 16)
            e.dma_start(A[:, :], W["A"]).then_inc(S["const_in"], 16)
            e.dma_start(ident[:, :], I["c_ident"]).then_inc(S["const_in"], 16)

            def load(t, p):
                at_least(e, S["Y_mm"], t, 1, -1)
                at_least(e, S["s1_ok"], t, 1, -1)
                e.dma_start(q[:, p, :, :], turned_of(W["q"], t)).then_inc(S["x_in"][p], 16)
                e.dma_start(x2[:, p, :, :], tokens_of(W["x2"], t)).then_inc(S["x_in"][p], 16)

            def store(t, p):
                at_least(e, S["bln_out"], t, 2, 2)
                e.dma_start(W["out"].rearrange("b (c l) d -> c b l d", l=L)[bass.ds(t, 1), :, :, :].rearrange("c b l d -> (c l) b d"),
                            x4[:, p, :, :]).then_inc(S["stored"][p], 16)
            for t in range(3):
                load(t, t % 2)
            with e.Fori(0, NC // 2 - 2) as j:
                for p in range(2):
                    load(j * 2 + 3 + p, 1 - p)
                    store(j * 2 + p, p)
            load(NC - 1, 1)
            for t in range(NC - 4, NC):
                store(t, t % 2)
            for p in range(2):
                e.wait_ge(S["stored"][p], 16 * NC // 2)

        @block.gpsimd
        def _(e):
            e.memset(mhalf[:, :], -0.5).then_inc(S["prep"], 1)
            e.wait_ge(S["prep"], 1)

            def low_x(t, p):
                at_least(e, S["xt_ok"], t, 1, 1)
                at_least(e, S["xh_ok"], t, 1, 1)
                at_least(e, S["u_mm"], t, NU, -NU)
                e.tensor_tensor(xl[:, p, :, :].rearrange("p k t -> p (k t)").bitcast(F32R), x3T[:, :],
                                xh[:, p, :, :].rearrange("p k t -> p (k t)"), ALU.subtract).then_inc(S["xl_ok"], 1)

            def low_h(t, n):
                at_least(e, S["o_mm"], t, NU, n + 1 - NU)
                at_least(e, S["hh_ok"], t, NU, n + 1)
                e.tensor_tensor(hl[:, n, :, :].bitcast(F32R), h[:, n, :, :], hh[:, n, :, :], ALU.subtract).then_inc(S["hl_ok"], 1)

            def step(t, p, last=False):
                low_h(t, 0)
                if not last:
                    norm_pool(e, S, N, t + 1, mhalf)
                low_h(t, 1)
                low_h(t, 2)
                if not last:
                    low_x(t + 1, 1 - p)
                low_h(t, 3)
                if not (isinstance(t, int) and t == 0):
                    norm_pool(e, S2, N2, t - 1, mhalf)
            norm_pool(e, S, N, 0, mhalf)
            low_x(0, 0)
            step(0, 0)
            step(1, 1)
            with e.Fori(1, NC // 2 - 1) as j:
                step(j * 2, 0)
                step(j * 2 + 1, 1)
            step(NC - 2, 0)
            step(NC - 1, 1, True)
            norm_pool(e, S2, N2, NC - 1, mhalf)

        @block.tensor
        def _(e):
            e.wait_ge(S["const_in"], 16 * 10)
            e.wait_ge(S["WA_ok"], BATCH)
            e.wait_ge(S["deq"], 3)

            def project(t, p):
                at_least(e, S["x_in"][p], t - p, 16, 32)
                at_least(e, S["xr_ok"], t, 2, 0)
                for b in range(BATCH):
                    for k in range(KT):
                        m = e.matmul(Yt_ps[:, b * DM:(b + 1) * DM], q[:, p, k, b * L:(b + 1) * L], WA[:, b, k, :],
                                     start=(k == 0), stop=(k == KT - 1))
                m.then_inc(S["Y_mm"], 1)

            def turn(t, p):
                at_least(e, S["ln_out"], t, 2, 2)
                at_least(e, S["xt_ok"], t, 1, 0)
                for k in range(KT):
                    for b in range(BATCH):
                        m = e.transpose(t_ps[:, (k * 2 + b) * P:(k * 2 + b + 1) * P], x3[:, p, b, k * P:(k + 1) * P], ident[:, :])
                m.then_inc(S["tr_mm"], 1)

            def up(t, p, n):
                if n == 0:
                    at_least(e, S["xh_ok"], t, 1, 1)
                    at_least(e, S["xl_ok"], t, 1, 1)
                at_least(e, S["h_ok"], t, 2 * NU, 2 * n - 2)
                for w, o, done in ((wg, g_ps, "g_mm"), (wu, u_ps, "u_mm")):
                    for i in range(2):
                        for k in range(KT):
                            for part in (xh, xl):
                                m = e.matmul(o[n % 2][:, i * CT:(i + 1) * CT],
                                             w[:, k, (2 * n + i) * P:(2 * n + i + 1) * P].bitcast(F32R), part[:, p, k, :].bitcast(F32R),
                                             start=(k == 0 and part is xh), stop=(k == KT - 1 and part is xl))
                    m.then_inc(S[done], 1)

            def down(t, n):
                at_least(e, S["hh_ok"], t, NU, n + 1)
                at_least(e, S["hl_ok"], t, NU, n + 1)
                if n == 0:
                    at_least(e, S["xm_ok"], t, 2, 0)
                for b in range(BATCH):
                    for i in range(2):
                        for part in (hh, hl):
                            m = e.matmul(o_ps[b][:, 0:DM], part[:, n, i, b * L:(b + 1) * L].bitcast(F32R),
                                         wd[:, 2 * n + i, :].bitcast(F32R), start=(n == 0 and i == 0 and part is hh),
                                         stop=(n == NU - 1 and i == 1 and part is hl))
                m.then_inc(S["o_mm"], 1)

            def step(t, p, last=False):
                later = not (isinstance(t, int) and t == 0)
                up(t, p, 0)
                if later:
                    down(t - 1, 2)
                if not last:
                    project(t + 1, 1 - p)
                up(t, p, 1)
                if later:
                    down(t - 1, 3)
                up(t, p, 2)
                if not last:
                    turn(t + 1, 1 - p)
                up(t, p, 3)
                down(t, 0)
                down(t, 1)
            project(0, 0)
            turn(0, 0)
            step(0, 0)
            step(1, 1)
            with e.Fori(1, NC // 2 - 1) as j:
                step(j * 2, 0)
                step(j * 2 + 1, 1)
            step(NC - 2, 0)
            step(NC - 1, 1, True)
            down(NC - 1, 2)
            down(NC - 1, 3)

        @block.scalar
        def _(e):
            e.wait_ge(S["const_in"], 16 * 10)

            def copy_turned(t):
                at_least(e, S["tr_mm"], t, 1, 1)
                at_least(e, S["xh_ok"], t, 1, 0)
                at_least(e, S["xl_ok"], t, 1, 0)
                e.activation(x3T[:, :], t_ps[:, :], ACT.Copy).then_inc(S["xt_ok"], 1)

            def step(t, p, last=False):
                for n in range(NU):
                    at_least(e, S["g_mm"], t, NU, n + 1)
                    at_least(e, S["h_ok"], t, 2 * NU, 2 * n - 2)
                    for i in range(2):
                        e.activation(sg[:, n % 2, i, :], g_ps[n % 2][:, i * CT:(i + 1) * CT], ACT.Silu,
                                     scale=gs[:, 2 * n + i:2 * n + i + 1]).then_inc(S["silu_ok"], 1)
                    if n == 2 and not last:
                        copy_turned(t + 1)
                if not last:
                    keep(t + 1, 1 - p)

            def keep(t, p):
                at_least(e, S["ln_out"], t, 2, 2)
                at_least(e, S["xs_ok"], t, 1, -1)
                e.activation(xk[:, p, :, :], x3[:, p, :, :], ACT.Copy).then_inc(S["kept"], 1)
            copy_turned(0)
            keep(0, 0)
            step(0, 0)
            step(1, 1)
            with e.Fori(1, NC // 2 - 1) as j:
                step(j * 2, 0)
                step(j * 2 + 1, 1)
            step(NC - 2, 0)
            step(NC - 1, 1, True)

        @block.vector
        def _(e):
            e.wait_ge(S["const_in"], 16 * 10)
            e.tensor_scalar(wg[:, :, :].bitcast(F32R), raw[:, :, :], -128.0, None, ALU.add).then_inc(S["deq"], 1)
            e.tensor_scalar(wu[:, :, :].bitcast(F32R), rawu[:, :, :], -128.0, None, ALU.add).then_inc(S["deq"], 1)
            e.tensor_scalar(wd[:, :, :].bitcast(F32R), rawd[:, :, :], -128.0, None, ALU.add).then_inc(S["deq"], 1)
            for b in range(BATCH):
                e.tensor_tensor(WA[:, b, :, :], wo[:, :, :],
                                spread(A[:, :].rearrange("p (k b) -> p k b", b=BATCH)[:, :, b], DM), ALU.mult).then_inc(S["WA_ok"], 1)

            def attention(t, p):
                at_least(e, S["x_in"][p], t - p, 16, 32)
                at_least(e, S["xr_ok"], t, 2, 0)
                e.scalar_tensor_tensor(out=s1[:, :, :], in0=x2[:, p, :, :], scalar=2.0, in1=repeat(bo[:, :], BATCH),
                                       op0=ALU.mult, op1=ALU.add).then_inc(S["s1_ok"], 1)
                at_least(e, S["Y_mm"], t, 1, 1)
                at_least(e, S["s1_ok"], t, 1, 1)
                at_least(e, S["ln_out"], t, 2, 0)
                for b in range(BATCH):
                    e.tensor_tensor(xr[:, b, :], s1[:, b, :], Yt_ps[:, b * DM:(b + 1) * DM], ALU.add).then_inc(S["xr_ok"], 1)
                at_least(e, S["xr_ok"], t, 2, 2)

                def free():
                    at_least(e, S["tr_mm"], t, 1, -1)
                    at_least(e, S["kept"], t, 1, -1)
                norm_vector(e, S, N, t, xr, x3[:, p, :, :], free)

            def high_x(t, p):
                at_least(e, S["xt_ok"], t, 1, 1)
                at_least(e, S["u_mm"], t, NU, -NU)
                e.tensor_copy(xh[:, p, :, :].rearrange("p k t -> p (k t)").bitcast(F32R), x3T[:, :]).then_inc(S["xh_ok"], 1)

            def gated(t, n):
                at_least(e, S["u_mm"], t, NU, n + 1)
                at_least(e, S["hl_ok"], t, NU, n + 1 - NU)
                for i in range(2):
                    at_least(e, S["silu_ok"], t, 2 * NU, 2 * n + i + 1)
                    e.scalar_tensor_tensor(out=h[:, n, i, :], in0=u_ps[n % 2][:, i * CT:(i + 1) * CT],
                                           scalar=us[:, 2 * n + i:2 * n + i + 1], in1=sg[:, n % 2, i, :],
                                           op0=ALU.mult, op1=ALU.mult).then_inc(S["h_ok"], 1)
                at_least(e, S["o_mm"], t, NU, n + 1 - NU)
                at_least(e, S["h_ok"], t, 2 * NU, 2 * n + 2)
                e.tensor_copy(hh[:, n, :, :].bitcast(F32R), h[:, n, :, :]).then_inc(S["hh_ok"], 1)

            def sums(t, p):
                at_least(e, S["o_mm"], t, NU, NU)
                at_least(e, S["xs_ok"], t, 1, 0)
                for b in range(BATCH):
                    e.tensor_tensor(xm[:, b, :], o_ps[b][:, 0:DM], ds[:, :], ALU.mult).then_inc(S["xm_ok"], 1)
                at_least(e, S["xm_ok"], t, 2, 2)
                at_least(e, S["bln_out"], t, 2, 0)
                at_least(e, S["kept"], t, 1, 1)
                e.tensor_tensor(xs[:, :, :], xm[:, :, :], xk[:, p, :, :], ALU.add).then_inc(S["xs_ok"], 1)

            def last_norm(t, p):
                at_least(e, S["xs_ok"], t, 1, 1)

                def free():
                    if not (isinstance(t, int) and t < 2):
                        at_least(e, S["stored"][p], t - p, 8, 0)
                norm_vector(e, S2, N2, t, xs, x4[:, p, :, :], free)

            def step(t, p, last=False):
                later = not (isinstance(t, int) and t == 0)
                gated(t, 0)
                if not last:
                    attention(t + 1, 1 - p)
                gated(t, 1)
                if later:
                    sums(t - 1, 1 - p)
                gated(t, 2)
                if not last:
                    high_x(t + 1, 1 - p)
                gated(t, 3)
                if later:
                    last_norm(t - 1, 1 - p)
            attention(0, 0)
            high_x(0, 0)
            step(0, 0)
            step(1, 1)
            with e.Fori(1, NC // 2 - 1) as j:
                step(j * 2, 0)
                step(j * 2 + 1, 1)
            step(NC - 2, 0)
            step(NC - 1, 1, True)
            sums(NC - 1, 1)
            last_norm(NC - 1, 1)


def build(nc, I, out):
    def scratch(name, shape, dt=F32):
        return nc.dram_tensor("scratch_" + name, shape, dt, kind="Internal").ap()
    W = {"bc": scratch("bc", (NC, 192, CT)), "phi": scratch("phi", (NC, 3, NH, CT), BF16),
         "pieces": scratch("pieces", (NC, 3, NH, CT), BF16), "negs": scratch("negs", (NC, 3, NH, CT), BF16),
         "dec": scratch("dec", (NB * NC, P, NG * BATCH)), "et": scratch("et", (NB * NC, P, CT)),
         "u": scratch("u", (NC, BATCH, L, DI)), "wu": scratch("wu", (NC, BATCH, L, DI)),
         "freq": scratch("freq", (NB, P, NG * P), BF16), "y": scratch("y", (NB * NC, P, CT)),
         "x1": scratch("x1", (NC, BATCH, L, DM)), "x1T": scratch("x1T", (NC, P, KT, CT)),
         "x2": scratch("x2", (NC, BATCH, L, DM)), "q": scratch("q", (NC, P, KT, CT)), "A": scratch("A", (P, KT * BATCH)),
         "out": out}
    for phases in ((project_and_decay, state_space_scan), (finish_mixer, mixture_of_experts), (key_value_product, output_and_ffn)):
        held = []
        for phase in phases:
            phase(nc, held, I, W)
        nc.clear_and_free_semaphores(held)
        nc.all_engine_barrier()


def laid_out(x):
    import numpy as np
    f = np.float32
    A = {}
    A["xT"] = np.ascontiguousarray(x["L0_attn_x"].reshape(TOK, DM).T)
    w = x["L0_attn_W_in"]
    o = 2 * DI
    A["w_bc"] = np.concatenate([w[:, o:o + NS:2], w[:, o + 1:o + NS:2], w[:, o + NS:o + 2 * NS:2], w[:, o + NS + 1:o + 2 * NS:2]], axis=1)
    A["w_dt"] = w[:, o + 2 * NS:]
    A["w_xs"] = w[:, DI:2 * DI]
    A["w_z"] = w[:, :DI]
    A["dt_bias"] = x["L0_attn_dt_bias"]
    A["A_log"] = x["L0_attn_A_log"]
    A["A_hm"] = x["L0_attn_A_log"].reshape(QA, 4).T.reshape(NH, 1)
    r = np.arange(P)
    A["c_ident"] = np.eye(P, dtype=f)
    A["c_triu"] = (r[:, None] <= r[None, :]).astype(f)
    A["c_tril"] = (r[:, None] > r[None, :]).astype(f)
    A["c_mask"] = np.where(r[:, None] > r[None, :], f(-1e30), f(0)).astype(f)
    A["c_blk"] = (r[:, None] // NS == r[None, :] // NS).astype(f)
    row_head = np.array([4 * q + h for h in range(4) for q in range(QA)])
    sel = np.zeros((NH, NB, P), f)
    for k in range(NB):
        sel[:, k, :] = row_head[:, None] == (HB * k + r // HD)[None, :]
    A["c_sel"] = sel
    ind = np.zeros((15, 4), f)
    for a in range(3):
        ind[a, :] = 1
        for h in range(4):
            ind[3 + 4 * a + h, h] = 1
    A["c_ind"] = ind
    A["c_turn"] = np.where(r % NS < NS // 2, f(TWO_PI), f(-TWO_PI)).astype(f).reshape(P, 1)
    fr = x["L0_attn_rope_freqs"]
    pairs = [(i, j) for i in range(3) for j in range(3) if (i, j) != (2, 2)]
    freq = np.zeros((NB, P, NG, P), f)
    less = np.zeros((P, 2), f)
    for n, (i, j) in enumerate(pairs):
        less[n * HB:(n + 1) * HB, 0] = -1.0 if j >= 1 else 0.0
        less[n * HB:(n + 1) * HB, 1] = -1.0 if j >= 2 else 0.0
        for h in range(NH):
            k, g, half = h // HB, h % HB // 2, h % 2
            for m in range(2):
                freq[k, n * HB + h % HB, g, half * NS + m * 32:half * NS + m * 32 + 32] = fr[h]
    A["c_less"] = less
    freq = freq.reshape(NB, P, NG * P)
    A["freq"] = freq
    beta = np.zeros((NB, P, 4, NG), f)
    for n, b in enumerate((x["L0_attn_B_bias"], x["L0_attn_C_bias"])):
        for h in range(NH):
            k, g, half = h // HB, h % HB // 2, h % 2
            for m in range(2):
                beta[k, half * NS + m * 32:half * NS + m * 32 + 32, 2 * n, g] = b[h, m::2]
                beta[k, half * NS + m * 32:half * NS + m * 32 + 32, 2 * n + 1, g] = b[h, 1 - m::2]
    A["beta"] = beta
    A["x"] = x["L0_attn_x"]
    A["w_out"] = x["L0_attn_W_out"]
    A["d_rep"] = np.repeat(x["L0_attn_D_param"], HD)
    A["norm_w"] = x["L0_attn_norm_w"].reshape(NB, P).T
    for n, (w, s) in {"w1": ("w1", "sw1"), "w3": ("w3", "sw3")}.items():
        A[n] = np.concatenate([x["L0_ffn_" + s][:, None, :], x["L0_ffn_" + w].transpose(1, 0, 2)], axis=1)
    A["w2"] = np.concatenate([x["L0_ffn_sw2"][:, None, :], x["L0_ffn_w2"].transpose(1, 0, 2)], axis=1)
    A["gate"] = x["L0_ffn_gate_w"]
    A["expert_bias"] = x["L0_ffn_expert_bias"]
    A["c_iota"] = np.arange(8, dtype=f)
    A["c_row"] = np.repeat(np.eye(8, dtype=f)[:, :, None], P, axis=2)
    e, o, rest = np.arange(0, P, 2), np.arange(1, P, 2), np.arange(P, DM)
    cols = np.concatenate([e, o, o, e, rest])
    perm = np.concatenate([e, o, rest])
    w, b = x["L1_attn_W_in"], x["L1_attn_b_in"]
    A["w_q"], A["w_k"], A["w_v"] = w[:, cols], w[:, DM + cols], w[:, 2 * DM + perm]
    A["b_q"], A["b_k"], A["b_v"] = b[cols].reshape(3, P).T, b[DM + cols], b[2 * DM + perm]
    A["ln_w"], A["ln_b"] = x["L1_attn_ln_w"].reshape(KT, P).T, x["L1_attn_ln_b"].reshape(KT, P).T
    A["w_o"], A["b_out"] = x["L1_attn_W_out"][perm, :], x["L1_attn_b_out"]
    rot = DM // 2
    inv = (f(1.0) / np.power(f(10000.0), np.arange(0, rot, 2, dtype=f) / f(rot))).astype(f)
    ang = (np.arange(SEQ, dtype=f)[:, None] * inv[None, :]).astype(f)
    cos, sin = np.cos(ang), np.sin(ang)
    A["c_rope_k"] = np.stack([np.concatenate([cos, cos], 1), np.concatenate([-sin, sin], 1)]).astype(f)
    A["c_rope_q"] = A["c_rope_k"].transpose(0, 2, 1)
    A["gate_w"], A["up_w"], A["down_w"] = x["L1_ffn_gate_w"].T, x["L1_ffn_up_w"].T, x["L1_ffn_down_w"].T
    A["gate_scale"], A["up_scale"] = x["L1_ffn_gate_scale"].reshape(-1, P).T, x["L1_ffn_up_scale"].reshape(-1, P).T
    A["down_scale"] = x["L1_ffn_down_scale"]
    return {k: np.ascontiguousarray(a) for k, a in A.items()}


def kernel(**inputs):
    import numpy as _np
    import concourse.bacc as _bacc
    from concourse import mybir as _mybir
    from concourse.bass_utils import run_bass_kernel_spmd as _run

    nc = _bacc.Bacc("TRN2", target_bir_lowering=False, num_devices=1)
    arrays, I = {}, {}
    for name, a in laid_out({k: _np.asarray(v) for k, v in inputs.items()}).items():
        arrays[f"in_{name}"] = a
        I[name] = nc.dram_tensor(f"in_{name}", a.shape, _mybir.dt.from_np(a.dtype), kind="ExternalInput").ap()
    out = nc.dram_tensor("out_0", (BATCH, SEQ, DM), F32, kind="ExternalOutput").ap()
    build(nc, I, out)
    r = _run(nc, [arrays], core_ids=[0])
    return r.results[0]["out_0"]
```
